# Optimizing a Trainium2 kernel written in Bass

```python
import numpy as np
import jax
import jax.numpy as jnp

def _softmax(x, axis=-1):
    return jax.nn.softmax(x, axis=axis)

def _gelu(x):
    return jax.nn.gelu(x, approximate=True)

def _silu(x):
    return jax.nn.silu(x)

def _sigmoid(x):
    return jax.nn.sigmoid(x)

def _layernorm(x, axis=-1, eps=1e-05):
    m = jnp.mean(x, axis=axis, keepdims=True)
    v = jnp.var(x, axis=axis, keepdims=True)
    return (x - m) / jnp.sqrt(v + eps)

def _scatter_add(tgt, idx, src, axis=0):
    return tgt.at[idx].add(src)

def _segment_sum(src, seg, n):
    return jax.ops.segment_sum(src, seg, n)
kernel_name = 'mk_decoder_preln_d1_seqx_r8_c079cc'

def setup_inputs(seed: int=0):
    np.random.seed(seed)
    _w = jnp.asarray

    def _rec_inputs():
        import jax
        import jax.numpy as jnp
        _rk = jax.random.key(seed)
        x = 7.22e-05 + 1 * jax.random.normal(jax.random.fold_in(_rk, 1), (64, 64, 256), jnp.float32)
        _lenS = 64 - jax.random.randint(jax.random.fold_in(_rk, 7), (64,), 0, max(1, 64 // 4) + 1, jnp.int32)
        _lenS2 = 64 - jax.random.randint(jax.random.fold_in(_rk, 8), (64,), 0, max(1, 64 // 4) + 1, jnp.int32)
        _ctx_2048P = jax.random.normal(jax.random.fold_in(_rk, 11), (64, 16, 256), jnp.float32)
        _ctx_2048c = jax.random.dirichlet(jax.random.fold_in(_rk, 511), 0.3 * jnp.ones((16,), jnp.float32), (64, 64))
        _ctx_2048t = jnp.einsum('bsk,bkd->bsd', _ctx_2048c, _ctx_2048P)
        _ctx_2048t = _ctx_2048t * jax.lax.rsqrt(jnp.mean(jnp.square(_ctx_2048t)) + 1e-12) * 0.953939
        ctx_2048 = 4.13588e-05 + 0.999923 * (_ctx_2048t + 0.3 * jax.random.normal(jax.random.fold_in(_rk, 611), (64, 64, 256), jnp.float32))
        return (x, ctx_2048)
    x, ctx_2048 = _rec_inputs()

    def _L0_attn_setup():
        import jax, jax.numpy as jnp
        import numpy as np
        H, DK, DV = (6, 32, 64)
        HID = 256
        CONV = 4
        NORM_EPS = 1e-05

        def causal_dwconv_silu(x, w):
            K = w.shape[1]
            xp = jnp.pad(x, ((0, 0), (K - 1, 0), (0, 0)))
            y = jax.lax.conv_general_dilated(jnp.transpose(xp, (0, 2, 1)), w[:, None, :], (1,), 'VALID', feature_group_count=w.shape[0])
            return jax.nn.silu(jnp.transpose(y, (0, 2, 1)))

        def l2norm(x, eps=1e-06):
            return x * jax.lax.rsqrt(jnp.sum(x * x, axis=-1, keepdims=True) + eps)
        key = jax.random.key(seed)
        ks = jax.random.split(key, 16)
        B, T = (2, 512)
        s = HID ** (-0.5)
        return dict(hidden_states=jax.random.normal(ks[0], (B, T, HID), jnp.float32), Wq=jax.random.normal(ks[1], (H * DK, HID), jnp.float32) * s, Wk=jax.random.normal(ks[2], (H * DK, HID), jnp.float32) * s, Wv=jax.random.normal(ks[3], (H * DV, HID), jnp.float32) * s, Wb=jax.random.normal(ks[4], (H, HID), jnp.float32) * s, Wa=jax.random.normal(ks[5], (H, HID), jnp.float32) * s, A_log=jnp.log(jax.random.uniform(ks[6], (H,), jnp.float32, 0.5, 16.0)), dt_bias=jax.random.normal(ks[7], (H,), jnp.float32) * 0.1, conv_wq=jax.random.normal(ks[8], (H * DK, CONV), jnp.float32) * 0.5, conv_wk=jax.random.normal(ks[9], (H * DK, CONV), jnp.float32) * 0.5, conv_wv=jax.random.normal(ks[10], (H * DV, CONV), jnp.float32) * 0.5, Wg=jax.random.normal(ks[11], (H * DV, HID), jnp.float32) * s, norm_w=jnp.ones((DV,), jnp.float32), Wo=jax.random.normal(ks[12], (HID, H * DV), jnp.float32) * (H * DV) ** (-0.5))
    _L0_attn_all = _L0_attn_setup()
    _L0_attn_in = {k: v for k, v in _L0_attn_all.items() if k in ('Wq', 'Wk', 'Wv', 'Wb', 'Wa', 'A_log', 'dt_bias', 'conv_wq', 'conv_wk', 'conv_wv', 'Wg', 'norm_w', 'Wo')}
    del _L0_attn_all

    def _L0_xattn_setup():
        import jax, jax.numpy as jnp
        import numpy as np
        N, E, T, H = (8, 64, 256, 8)
        key = jax.random.key(seed)
        ks = jax.random.split(key, 6)
        s = 1.0 / np.sqrt(E)
        return {'mask': jax.random.normal(ks[0], (N, E, T), jnp.float32), 'encodings': jax.random.normal(ks[1], (N, E, T), jnp.float32), 'w_in': jax.random.normal(ks[2], (3 * E, E), jnp.float32) * s, 'b_in': jnp.zeros((3 * E,), jnp.float32), 'w_out': jax.random.normal(ks[3], (E, E), jnp.float32) * s, 'b_out': jnp.zeros((E,), jnp.float32), 'w_ct': jax.random.normal(ks[4], (E, E), jnp.float32) * s, 'b_ct': jnp.zeros((E,), jnp.float32), 'local_size': 64}
    _L0_xattn_all = _L0_xattn_setup()
    _L0_xattn_in = {k: v for k, v in _L0_xattn_all.items() if k in ('w_in', 'b_in', 'w_out', 'b_out', 'w_ct', 'b_ct')}
    del _L0_xattn_all

    def _L0_ffn_setup():
        import jax, jax.numpy as jnp
        import numpy as np
        NUM_EXPERTS = 128
        NUM_KEPT = 48
        TOP_K = 8
        HIDDEN = 256
        INTER = 96
        CAP = 96
        BATCH, SEQ = (2, 128)
        key = jax.random.key(seed)
        k1, k2, k3, k4 = jax.random.split(key, 4)
        hidden_states = jax.random.normal(k1, (BATCH, SEQ, HIDDEN), jnp.float32)
        gate_weight = jax.random.normal(k2, (NUM_EXPERTS, HIDDEN), jnp.float32) * 0.02
        gate_up_proj = jax.random.normal(k3, (NUM_KEPT, 2 * INTER, HIDDEN), jnp.float32) * 0.02
        down_proj = jax.random.normal(k4, (NUM_KEPT, HIDDEN, INTER), jnp.float32) * 0.02
        o2n = -np.ones(NUM_EXPERTS, np.int32)
        o2n[np.arange(NUM_KEPT) * 2] = np.arange(NUM_KEPT, dtype=np.int32)
        old_to_new = jnp.asarray(o2n)
        return {'hidden_states': hidden_states, 'gate_weight': gate_weight, 'gate_up_proj': gate_up_proj, 'down_proj': down_proj, 'old_to_new': old_to_new}
    _L0_ffn_all = _L0_ffn_setup()
    _L0_ffn_in = {k: v for k, v in _L0_ffn_all.items() if k in ('gate_weight', 'gate_up_proj', 'down_proj', 'old_to_new')}
    del _L0_ffn_all
    return {'x': x, 'ctx_2048': ctx_2048, 'L0_attn_Wq': _L0_attn_in['Wq'], 'L0_attn_Wk': _L0_attn_in['Wk'], 'L0_attn_Wv': _L0_attn_in['Wv'], 'L0_attn_Wb': _L0_attn_in['Wb'], 'L0_attn_Wa': _L0_attn_in['Wa'], 'L0_attn_A_log': _L0_attn_in['A_log'], 'L0_attn_dt_bias': _L0_attn_in['dt_bias'], 'L0_attn_conv_wq': _L0_attn_in['conv_wq'], 'L0_attn_conv_wk': _L0_attn_in['conv_wk'], 'L0_attn_conv_wv': _L0_attn_in['conv_wv'], 'L0_attn_Wg': _L0_attn_in['Wg'], 'L0_attn_norm_w': _L0_attn_in['norm_w'], 'L0_attn_Wo': _L0_attn_in['Wo'], 'L0_xattn_w_in': _L0_xattn_in['w_in'], 'L0_xattn_b_in': _L0_xattn_in['b_in'], 'L0_xattn_w_out': _L0_xattn_in['w_out'], 'L0_xattn_b_out': _L0_xattn_in['b_out'], 'L0_xattn_w_ct': _L0_xattn_in['w_ct'], 'L0_xattn_b_ct': _L0_xattn_in['b_ct'], 'L0_ffn_gate_weight': _L0_ffn_in['gate_weight'], 'L0_ffn_gate_up_proj': _L0_ffn_in['gate_up_proj'], 'L0_ffn_down_proj': _L0_ffn_in['down_proj'], 'L0_ffn_old_to_new': _L0_ffn_in['old_to_new']}

def reference(x, ctx_2048, L0_attn_Wq, L0_attn_Wk, L0_attn_Wv, L0_attn_Wb, L0_attn_Wa, L0_attn_A_log, L0_attn_dt_bias, L0_attn_conv_wq, L0_attn_conv_wk, L0_attn_conv_wv, L0_attn_Wg, L0_attn_norm_w, L0_attn_Wo, L0_xattn_w_in, L0_xattn_b_in, L0_xattn_w_out, L0_xattn_b_out, L0_xattn_w_ct, L0_xattn_b_ct, L0_ffn_gate_weight, L0_ffn_gate_up_proj, L0_ffn_down_proj, L0_ffn_old_to_new):
    import jax
    import jax.numpy as jnp

    def _L0_attn_ref(hidden_states, Wq, Wk, Wv, Wb, Wa, A_log, dt_bias, conv_wq, conv_wk, conv_wv, Wg, norm_w, Wo):
        import jax, jax.numpy as jnp
        import numpy as np
        H, DK, DV = (6, 32, 64)
        HID = 256
        CONV = 4
        NORM_EPS = 1e-05

        def causal_dwconv_silu(x, w):
            K = w.shape[1]
            xp = jnp.pad(x, ((0, 0), (K - 1, 0), (0, 0)))
            y = jax.lax.conv_general_dilated(jnp.transpose(xp, (0, 2, 1)), w[:, None, :], (1,), 'VALID', feature_group_count=w.shape[0])
            return jax.nn.silu(jnp.transpose(y, (0, 2, 1)))

        def l2norm(x, eps=1e-06):
            return x * jax.lax.rsqrt(jnp.sum(x * x, axis=-1, keepdims=True) + eps)
        x = hidden_states
        B, T, _ = x.shape
        q = causal_dwconv_silu(x @ Wq.T, conv_wq).reshape(B, T, H, DK)
        k = causal_dwconv_silu(x @ Wk.T, conv_wk).reshape(B, T, H, DK)
        v = causal_dwconv_silu(x @ Wv.T, conv_wv).reshape(B, T, H, DV)
        beta = jax.nn.sigmoid(x @ Wb.T)
        g = -jnp.exp(A_log) * jax.nn.softplus(x @ Wa.T + dt_bias)
        q = l2norm(q) * DK ** (-0.5)
        k = l2norm(k)

        def step(S, inp):
            qt, kt, vt, gt, bt = inp
            S = S * jnp.exp(gt)[..., None, None]
            v_new = vt - jnp.einsum('bhk,bhkv->bhv', kt, S)
            S = S + bt[..., None, None] * (kt[..., :, None] * v_new[..., None, :])
            o = jnp.einsum('bhk,bhkv->bhv', qt, S)
            return (S, o)
        S0 = jnp.zeros((B, H, DK, DV), x.dtype)
        tm = lambda a: jnp.moveaxis(a, 1, 0)
        _, o = jax.lax.scan(step, S0, (tm(q), tm(k), tm(v), tm(g), tm(beta)))
        o = jnp.moveaxis(o, 0, 1)
        var = jnp.mean(jnp.square(o.astype(jnp.float32)), axis=-1, keepdims=True)
        o = o * jax.lax.rsqrt(var + NORM_EPS).astype(o.dtype) * norm_w
        gate = (x @ Wg.T).reshape(B, T, H, DV)
        o = o * jax.nn.silu(gate)
        return o.reshape(B, T, H * DV) @ Wo.T

    def _L0_xattn_ref(mask, encodings, w_in, b_in, w_out, b_out, w_ct, b_ct, local_size):
        import jax, jax.numpy as jnp
        import numpy as np
        N, E, T, H = (8, 64, 256, 8)
        n, e, t = mask.shape
        d = e // H
        x = jnp.transpose(mask, (0, 2, 1))
        qkv = x @ w_in.T + b_in
        q, k, v = jnp.split(qkv, 3, axis=-1)
        q = q.reshape(n, t, H, d)
        k = k.reshape(n, t, H, d)
        v = v.reshape(n, t, H, d)
        scores = jnp.einsum('bqhd,bkhd->bhqk', q, k) / jnp.sqrt(jnp.asarray(d, q.dtype))
        idx = jnp.arange(t)
        band = jnp.abs(idx[:, None] - idx[None, :]) <= local_size
        neg = jnp.asarray(jnp.finfo(scores.dtype).min, scores.dtype)
        scores = jnp.where(band[None, None], scores, neg)
        attn = jax.nn.softmax(scores, axis=-1)
        o = jnp.einsum('bhqk,bkhd->bqhd', attn, v).reshape(n, t, e)
        o = o @ w_out.T + b_out
        o = jnp.transpose(o, (0, 2, 1))
        y = jax.nn.relu(o) * encodings
        out = jnp.einsum('nit,io->not', y, w_ct) + b_ct[None, :, None]
        return out

    def _L0_ffn_ref(hidden_states, gate_weight, gate_up_proj, down_proj, old_to_new):
        import jax, jax.numpy as jnp
        import numpy as np
        NUM_EXPERTS = 128
        NUM_KEPT = 48
        TOP_K = 8
        HIDDEN = 256
        INTER = 96
        CAP = 96
        BATCH, SEQ = (2, 128)
        B, S, H = hidden_states.shape
        x = hidden_states.reshape(-1, H)
        T = x.shape[0]
        logits = x @ gate_weight.T
        logits = jnp.where(old_to_new[None, :] == -1, -jnp.inf, logits)
        probs = jax.nn.softmax(logits.astype(jnp.float32), axis=-1).astype(logits.dtype)
        top_v, top_i = jax.lax.top_k(probs, TOP_K)
        top_v = top_v / jnp.sum(top_v, axis=-1, keepdims=True)
        sel_new = old_to_new[top_i]
        E = gate_up_proj.shape[0]
        flat_e = sel_new.reshape(-1)
        flat_w = top_v.reshape(-1)
        tok = jnp.repeat(jnp.arange(T), TOP_K)
        oh = (flat_e[:, None] == jnp.arange(E)[None, :]).astype(jnp.int32)
        pos = jnp.sum(jnp.cumsum(oh, axis=0) * oh, axis=-1) - 1
        valid = pos < CAP
        pos_c = jnp.where(valid, pos, CAP)
        xb = jnp.zeros((E, CAP + 1, H), x.dtype).at[flat_e, pos_c].set(x[tok])
        xb = xb[:, :CAP]
        gu = jnp.einsum('ech,eoh->eco', xb, gate_up_proj)
        g, u = jnp.split(gu, 2, axis=-1)
        h = jax.nn.silu(g) * u
        out = jnp.einsum('eci,ehi->ech', h, down_proj)
        y = out[flat_e, jnp.minimum(pos_c, CAP - 1)]
        w = flat_w * valid.astype(flat_w.dtype)
        final = jnp.zeros_like(x).at[tok].add(y * w[:, None])
        return final.reshape(B, S, H)
    x = x + _L0_attn_ref(_layernorm(x, axis=-1), L0_attn_Wq, L0_attn_Wk, L0_attn_Wv, L0_attn_Wb, L0_attn_Wa, L0_attn_A_log, L0_attn_dt_bias, L0_attn_conv_wq, L0_attn_conv_wk, L0_attn_conv_wv, L0_attn_Wg, L0_attn_norm_w, L0_attn_Wo)
    x = x + _L0_xattn_ref(_layernorm(x, axis=-1), ctx_2048, L0_xattn_w_in, L0_xattn_b_in, L0_xattn_w_out, L0_xattn_b_out, L0_xattn_w_ct, L0_xattn_b_ct, 64)
    x = x + _L0_ffn_ref(_layernorm(x, axis=-1), L0_ffn_gate_weight, L0_ffn_gate_up_proj, L0_ffn_down_proj, L0_ffn_old_to_new)
    return x

_drawn_inputs = setup_inputs


def setup_inputs(seed=0):
    import zlib

    import numpy as np

    out = dict(_drawn_inputs(seed))
    spreads = {'L0_attn_norm_w': (1.0, 0.2),
     'L0_xattn_b_in': (0.0, 0.1),
     'L0_xattn_b_out': (0.0, 0.1),
     'L0_xattn_b_ct': (0.0, 0.1)}
    factors = {'L0_attn_dt_bias': 6.014,
     'L0_ffn_gate_weight': 8.0,
     'L0_ffn_gate_up_proj': 8.0,
     'L0_ffn_down_proj': 8.0}
    for name, (base, spread) in spreads.items():
        noise = np.random.default_rng([zlib.crc32(name.encode()), seed]).standard_normal(out[name].shape)
        drawn = base * np.exp(spread * noise) if base else spread * noise
        out[name] = jnp.asarray(drawn.astype(out[name].dtype))
    for name, factor in factors.items():
        out[name] = (out[name] * factor).astype(out[name].dtype)
    return out
```

```python
from contextlib import ExitStack

import numpy as np

import concourse.bass as bass
from concourse import mybir

F32 = mybir.dt.float32
BF16 = mybir.dt.bfloat16
I32 = mybir.dt.int32
ALU = mybir.AluOpType
ACT = mybir.ActivationFunctionType
AX = mybir.AxisListType

P = 128
TOKENS, HID = 4096, 256
TILES = TOKENS // P
T = 64
HEADS, DK, DV = 6, 32, 64
NCH = 7
QKC = 4
VD = HEADS * DV
LEVELS = 6
LN_EPS = 1e-5
L2_EPS = 4e-6
RMS_EPS = 4 * DK * 1e-5


def after(eng, sem, n):
    if not isinstance(n, int) or n > 0:
        eng.wait_ge(sem, n)


def delta_rule(nc, X, dram, sems):
    with ExitStack() as ctx:
        def sb(name, shape, dt=F32):
            return ctx.enter_context(nc.sbuf_tensor(name, shape, dt))

        def bank(name):
            return ctx.enter_context(nc.psum_tensor(name, [P, 512], F32))

        def sem(name):
            sems.append(nc.alloc_semaphore(name))
            return sems[-1]

        ident = sb("a_ident", [P, P])
        upto = sb("a_upto", [P, P])
        past = sb("a_past", [P, P])
        level = sb("a_level", [P, LEVELS, P])
        heads32 = sb("a_heads32", [P, P])
        hmask = sb("a_hmask", [P, 3])
        wqkv = sb("a_wqkv", [P, 2, NCH * P])
        wgab = sb("a_wgab", [P, 2, VD + 2 * HEADS])
        wo = sb("a_wo", [P, 3, HID])
        cw = sb("a_cw", [P, NCH, 4])
        nwh = sb("a_nwh", [P, VD])
        alog = sb("a_alog", [P, HEADS])
        dtb = sb("a_dtb", [P, HEADS])
        nega = sb("a_nega", [P, HEADS])
        ea = sb("a_ea", [P, HEADS])

        st = sb("a_st", [P, 6])
        mv = sb("a_mv", [P, 2])
        lv = sb("a_lv", [P, 1])
        rstd = sb("a_rstd", [P, 1])
        xn = sb("a_xn", [P, HID])
        xT = sb("a_xT", [P, 2, P])
        zp = sb("a_zp", [P, NCH, 2, T + 3])
        y = sb("a_y", [P, NCH, 2, T])
        th = sb("a_th", [P, NCH * P])
        sy = sb("a_sy", [P, NCH * P])
        sq = sb("a_sq", [P, QKC * P])
        rs = sb("a_rs", [P, QKC * P])
        rl = sb("a_rl", [P, QKC * P])
        tg = sb("a_tg", [P, VD + HEADS])
        gs = sb("a_gs", [P, VD])
        zz = sb("a_zz", [P, HEADS])
        az = sb("a_az", [P, HEADS])
        ez = sb("a_ez", [P, HEADS])
        lz = sb("a_lz", [P, HEADS])
        sp_ = sb("a_sp", [P, HEADS])
        qk = [sb(f"a_qk{p}", [P, QKC, P]) for p in range(2)]
        V = [sb(f"a_V{p}", [P, VD]) for p in range(2)]
        g = [sb(f"a_g{p}", [P, HEADS]) for p in range(2)]
        beta = [sb(f"a_beta{p}", [P, HEADS]) for p in range(2)]
        gw = [sb(f"a_gw{p}", [P, VD]) for p in range(2)]

        H3 = 3 * P
        rD = sb("a_rD", [P, 2, 3, P])
        E = sb("a_E", [P, 2, 3, P])
        Eb = sb("a_Eb", [P, 2, 3, P])
        EA = sb("a_EA", [P, 2, 3, P])
        kM = sb("a_kM", [P, HEADS, P])
        AT = sb("a_AT", [P, 2, 3, P])
        LT = sb("a_LT", [P, 2, 3, P])
        LM = sb("a_LM", [P, LEVELS, 2, 3, P])
        Xi = sb("a_Xi", [P, 2, 3, P])
        Ti = sb("a_Ti", [P, 2, 3, P])
        Pi = sb("a_Pi", [P, 2, 3, P])
        W = sb("a_W", [P, 2, 4, DV])
        Pv = sb("a_Pv", [P, 2, 4, DV])
        U = sb("a_U", [P, 2, 4, DV])
        oq = sb("a_oq", [P, 2, 3, DV])
        oss = sb("a_oss", [P, 2, 3])
        orl = sb("a_orl", [P, 2, 3])
        orr = sb("a_orr", [P, 2, 3])
        o1 = sb("a_o1", [P, 2, 3, DV])
        o2 = sb("a_o2", [P, VD])
        oT = sb("a_oT", [P, VD])

        a0, a1 = bank("a_b0"), bank("a_b1")
        bP = [bank(f"a_bP{f}") for f in range(2)]
        bA = [bank(f"a_bA{f}") for f in range(2)]
        bB = [bank(f"a_bB{f}") for f in range(2)]

        eps_ln, eps_l2, eps_rms = (sb(n, [P, 1]) for n in ("a_eps_ln", "a_eps_l2", "a_eps_rms"))
        ident3 = ident[:, :].unsqueeze(1).to_broadcast([P, 3, P])
        loaded = sem("a_loaded")
        zeroed = sem("a_zeroed")
        held = sem("a_held")
        decay_e = sem("a_decay_e")
        decay_c = sem("a_decay_c")
        stats = sem("a_stats")
        rstd_s = sem("a_rstd")
        xn_s = sem("a_xn")
        xt_mm = sem("a_xt_mm")
        xt_s = sem("a_xt")
        z_mm = [sem(f"a_z_mm{k}") for k in range(2)]
        z_s = [sem(f"a_z{k}") for k in range(2)]
        conv = sem("a_conv")
        tanh_s = sem("a_tanh")
        silu_s = sem("a_silu")
        sq_s = sem("a_sq")
        ss_mm = sem("a_ss_mm")
        rs_s = sem("a_rs")
        qk_s = sem("a_qk")
        v_mm = sem("a_v_mm")
        v_s = sem("a_v")
        gate_mm = sem("a_gate_mm")
        gate_th = sem("a_gate_th")
        gate_v = sem("a_gate_v")
        spl = sem("a_spl")
        gw_s = sem("a_gw")
        g_s = sem("a_g")

        ez_s = sem("a_ez")
        gs_s = sem("a_gs")
        L0_s = [sem(f"a_L0{f}") for f in range(2)]
        rD_s = [sem(f"a_rD{f}") for f in range(2)]
        d_mm = [sem(f"a_d_mm{f}") for f in range(2)]
        E_s = [sem(f"a_E{f}") for f in range(2)]
        Eb_s = [sem(f"a_Eb{f}") for f in range(2)]
        EA_s = [sem(f"a_EA{f}") for f in range(2)]
        kM_s = sem("a_kM")
        kk_mm = [sem(f"a_kk_mm{f}") for f in range(2)]
        qk_mm = [sem(f"a_qk_mm{f}") for f in range(2)]
        AT_s = [sem(f"a_AT{f}") for f in range(2)]
        LT_s = [sem(f"a_LT{f}") for f in range(2)]
        LM_s = [sem(f"a_LM{f}") for f in range(2)]
        X1_s = [sem(f"a_X1{f}") for f in range(2)]
        t1_mm = [sem(f"a_t1_mm{f}") for f in range(2)]
        T1_s = [sem(f"a_T1{f}") for f in range(2)]
        P_mm = [sem(f"a_P_mm{f}") for f in range(2)]
        P_s = [sem(f"a_P{f}") for f in range(2)]
        TU_mm = [sem(f"a_TU_mm{f}") for f in range(2)]
        XU_mm = [sem(f"a_XU_mm{f}") for f in range(2)]
        T_s = [sem(f"a_T{f}") for f in range(2)]
        X_s = [sem(f"a_X{f}") for f in range(2)]
        W_mm = [sem(f"a_W_mm{f}") for f in range(2)]
        W_s = [sem(f"a_W{f}") for f in range(2)]
        Pv_mm = [sem(f"a_Pv_mm{f}") for f in range(2)]
        Pv_s = [sem(f"a_Pv{f}") for f in range(2)]
        U_mm = [sem(f"a_U_mm{f}") for f in range(2)]
        U_s = [sem(f"a_U{f}") for f in range(2)]
        O_mm = [sem(f"a_O_mm{f}") for f in range(2)]
        oq_s = [sem(f"a_oq{f}") for f in range(2)]
        oss_s = sem("a_oss")
        orr_s = sem("a_orr")
        o1_s = [sem(f"a_o1{f}") for f in range(2)]
        o2_s = sem("a_o2")
        oT_mm = sem("a_oT_mm")
        oT_s = sem("a_oT")
        out_mm = sem("a_out_mm")
        x_s = sem("a_x")

        block = ctx.enter_context(nc.Block())
        NL = LEVELS - 2

        @block.sync
        def _(sp):
            for dst, src in ((ident, "c_ident"), (upto, "c_upto"), (past, "c_past"), (heads32, "c_heads32"),
                             (hmask, "c_hmask"), (nwh, "norm_w"), (alog, "A_log"), (dtb, "dt_bias")):
                sp.dma_start(dst[:, :], dram[src]).then_inc(loaded, 16)
            sp.dma_start(level[:, :, :], dram["c_level"].rearrange("l p t -> p l t")).then_inc(loaded, 16)
            sp.dma_start(wqkv[:, :, :], dram["w_qkv"].rearrange("(c p) n -> p c n", p=P)).then_inc(loaded, 16)
            sp.dma_start(wgab[:, :, :], dram["w_gab"].rearrange("(c p) n -> p c n", p=P)).then_inc(loaded, 16)
            sp.dma_start(wo[:, :, :], dram["w_o"].rearrange("(c p) n -> p c n", p=P)).then_inc(loaded, 16)
            sp.dma_start(cw[:, :, :], dram["w_conv"].rearrange("c p j -> p c j")).then_inc(loaded, 16)
            for part in range(2):
                n = TILES // 2
                sp.dma_start(X[:, part * n:part * n + n, :],
                             dram["x"][part * n * P:(part + 1) * n * P, :].rearrange("(n p) d -> p n d", p=P)
                             ).then_inc(loaded, 16)

        N_LOADS = 15

        def schedule(eng, A, B):
            for part in A(0):
                part()

            def both(i, a, b):
                parts_b = B(i, b)
                parts_a = A(i + 1, a) if a is not None else []
                n = max(len(parts_a), len(parts_b))
                for k in range(n):
                    if k < len(parts_b):
                        parts_b[k]()
                    if k < len(parts_a):
                        parts_a[k]()
            with eng.Fori(0, TILES // 2 - 1) as t:
                both(2 * t, 1, 0)
                both(2 * t + 1, 0, 1)
            both(TILES - 2, 1, 0)
            both(TILES - 1, None, 1)

        @block.tensor
        def _(pe):
            pe.wait_ge(loaded, 16 * N_LOADS)

            def A(i, p=0):
                def x_turn():
                    pe.wait_ge(xn_s, i + 1)
                    after(pe, gate_v, i)
                    for c in range(2):
                        m = nc.tensor.transpose(a0[:, c * P:(c + 1) * P], xn[:, c * P:(c + 1) * P], ident[:, :])
                    m.then_inc(xt_mm, 1)

                def project():
                    pe.wait_ge(xt_s, i + 1)
                    after(pe, v_s, i)
                    for ch in range(NCH):
                        o = (a0 if ch < 4 else a1)[:, (ch % 4) * P:(ch % 4 + 1) * P]
                        for c in range(2):
                            m = nc.tensor.matmul(o, wqkv[:, c, ch * P:(ch + 1) * P], xT[:, c, :],
                                                 start=(c == 0), stop=(c == 1))
                        if ch in (3, 6):
                            m.then_inc(z_mm[ch // 4], 1)

                def gates():
                    pe.wait_ge(z_s[0], i + 1)
                    for c in range(2):
                        m = nc.tensor.matmul(a0[:, 0:VD + 2 * HEADS], xT[:, c, :], wgab[:, c, :],
                                             start=(c == 0), stop=(c == 1))
                    m.then_inc(gate_mm, 1)

                def squares():
                    pe.wait_ge(sq_s, i + 1)
                    pe.wait_ge(z_s[1], i + 1)
                    nc.tensor.matmul(a1[:, :], heads32[:, :], sq[:, :], start=True, stop=True).then_inc(ss_mm, 1)

                def v_turn():
                    pe.wait_ge(silu_s, i + 1)
                    pe.wait_ge(rs_s, 2 * i + 1)
                    for c in range(3):
                        m = nc.tensor.transpose(a1[:, c * P:(c + 1) * P], sy[:, (QKC + c) * P:(QKC + c + 1) * P],
                                                ident[:, :])
                    m.then_inc(v_mm, 1)
                return [x_turn, project, gates, squares, v_turn]

            def B(i, p):
                def decay():
                    for f in range(2):
                        pe.wait_ge(rD_s[f], i + 1)
                        after(pe, o1_s[f], i)
                        nc.tensor.matmul(bP[f][:, 0:H3], past[:, :],
                                         rD[:, f, :, :].rearrange("p h t -> p (h t)"),
                                         start=True, stop=True).then_inc(d_mm[f], 1)

                def scores():
                    pe.wait_ge(kM_s, HEADS * (i + 1))
                    after(pe, x_s, i)
                    for f in range(2):
                        for h in range(3):
                            mk = nc.tensor.matmul(bA[f][:, h * P:(h + 1) * P], kM[:, 3 * f + h, :],
                                                  qk[p][:, 2 + f, :], start=True, stop=True)
                            mq = nc.tensor.matmul(bB[f][:, h * P:(h + 1) * P], kM[:, 3 * f + h, :],
                                                  qk[p][:, f, :], start=True, stop=True)
                        mk.then_inc(kk_mm[f], 1)
                        mq.then_inc(qk_mm[f], 1)

                def first():
                    for f in range(2):
                        pe.wait_ge(X1_s[f], i + 1)
                        pe.wait_ge(E_s[f], i + 1)
                        for h in range(3):
                            m = nc.tensor.transpose(bP[f][:, h * P:(h + 1) * P], Xi[:, f, h, :], ident[:, :])
                        m.then_inc(t1_mm[f], 1)

                def level_p(l):
                    def go():
                        for f in range(2):
                            if l == 1:
                                pe.wait_ge(T1_s[f], i + 1)
                            else:
                                pe.wait_ge(T_s[f], NL * i + l - 1)
                                pe.wait_ge(P_s[f], NL * i + l - 1)
                            pe.wait_ge(LM_s[f], (LEVELS - 1) * i + l)
                            for h in range(3):
                                m = nc.tensor.matmul(bP[f][:, h * P:(h + 1) * P], LM[:, l, f, h, :],
                                                     Ti[:, f, h, :], start=True, stop=True)
                            m.then_inc(P_mm[f], 1)
                    return go

                def level_u(l):
                    def go():
                        for f in range(2):
                            pe.wait_ge(P_s[f], NL * i + l)
                            if l == 1:
                                pe.wait_ge(AT_s[f], i + 1)
                                pe.wait_ge(LT_s[f], i + 1)
                            else:
                                pe.wait_ge(X_s[f], NL * i + l - 1)
                                pe.wait_ge(T_s[f], NL * i + l - 1)
                            for h in range(3):
                                m = nc.tensor.matmul(bA[f][:, h * P:(h + 1) * P], Xi[:, f, h, :],
                                                     Pi[:, f, h, :], start=True, stop=True)
                            m.then_inc(TU_mm[f], 1)
                            for h in range(3):
                                m = nc.tensor.matmul(bB[f][:, h * P:(h + 1) * P], Pi[:, f, h, :],
                                                     Xi[:, f, h, :], start=True, stop=True)
                            m.then_inc(XU_mm[f], 1)
                    return go

                def vcols(buf, f, h):
                    return buf[:, f, h:h + 2, :].rearrange("p h d -> p (h d)")

                def solve_w():
                    for f in range(2):
                        pe.wait_ge(X_s[f], NL * (i + 1))
                        pe.wait_ge(P_s[f], NL * (i + 1))
                        pe.wait_ge(v_s, i + 1)
                        for h in range(3):
                            c = min((3 * f + h) * DV, VD - P)
                            m = nc.tensor.matmul(bP[f][:, h * P:(h + 1) * P], Xi[:, f, h, :],
                                                 V[p][:, c:c + P], start=True, stop=True)
                        m.then_inc(W_mm[f], 1)

                def solve_p():
                    for f in range(2):
                        pe.wait_ge(W_s[f], i + 1)
                        pe.wait_ge(LM_s[f], (LEVELS - 1) * (i + 1))
                        pe.wait_ge(T_s[f], NL * (i + 1))
                        for h in range(3):
                            m = nc.tensor.matmul(bA[f][:, h * P:(h + 1) * P], LM[:, LEVELS - 1, f, h, :],
                                                 vcols(W, f, h), start=True, stop=True)
                        m.then_inc(Pv_mm[f], 1)

                def solve_u():
                    for f in range(2):
                        pe.wait_ge(Pv_s[f], i + 1)
                        for h in range(3):
                            m = nc.tensor.matmul(bB[f][:, h * P:(h + 1) * P], Xi[:, f, h, :],
                                                 vcols(Pv, f, h), start=True, stop=True)
                        m.then_inc(U_mm[f], 1)

                def outputs():
                    for f in range(2):
                        pe.wait_ge(U_s[f], i + 1)
                        for h in range(3):
                            m = nc.tensor.matmul(bP[f][:, h * P:(h + 1) * P], AT[:, f, h, :],
                                                 vcols(U, f, h), start=True, stop=True)
                        m.then_inc(O_mm[f], 1)

                def o_turn():
                    pe.wait_ge(o2_s, i + 1)
                    for c in range(3):
                        m = nc.tensor.transpose(bA[0][:, c * P:(c + 1) * P], o2[:, c * P:(c + 1) * P], ident[:, :])
                    m.then_inc(oT_mm, 1)

                def o_project():
                    pe.wait_ge(oT_s, i + 1)
                    for c in range(3):
                        m = nc.tensor.matmul(bB[0][:, 0:HID], oT[:, c * P:(c + 1) * P], wo[:, c, :],
                                             start=(c == 0), stop=(c == 2))
                    m.then_inc(out_mm, 1)
                parts = [decay, scores, first]
                for l in range(1, LEVELS - 1):
                    parts += [level_p(l), level_u(l)]
                return parts + [solve_w, solve_p, solve_u, outputs, o_turn, o_project]

            def A_spread(i, p=0):
                x_turn, project, gates, squares, v_turn = A(i, p)
                at = {0: x_turn, 2: project, 4: gates, 10: squares, 12: v_turn}
                return [at.get(k, lambda: None) for k in range(13)]
            schedule(pe, A_spread, B)

        @block.scalar
        def _(act):
            act.wait_ge(loaded, 16 * N_LOADS)
            nc.scalar.activation(ea[:, :], alog[:, :], ACT.Exp).then_inc(decay_e, 1)

            def A(i, p=0):
                def norm_rstd():
                    act.wait_ge(stats, 2 * (i + 1))
                    after(act, xn_s, i)
                    nc.scalar.activation(lv[:, :], mv[:, 1:2], ACT.Ln, bias=eps_ln[:, :]).then_inc(rstd_s, 1)
                    act.wait_ge(rstd_s, 2 * i + 1)
                    nc.scalar.activation(rstd[:, :], lv[:, :], ACT.Exp, scale=-0.5).then_inc(rstd_s, 1)

                def x_copy():
                    act.wait_ge(xt_mm, i + 1)
                    after(act, gate_mm, i)
                    nc.scalar.copy(xT[:, :, :].rearrange("p c t -> p (c t)"), a0[:, 0:HID]).then_inc(xt_s, 1)

                def z_copy():
                    for k, (c0, c1) in enumerate(((0, 4), (4, 7))):
                        act.wait_ge(z_mm[k], i + 1)
                        after(act, conv, 4 * NCH * i)
                        nc.scalar.copy(zp[:, c0:c1, :, 3:3 + T].rearrange("p c b t -> p (c b) t"),
                                       (a0 if k == 0 else a1)[:, 0:(c1 - c0) * P].rearrange("p (c t) -> p c t", t=T)
                                       ).then_inc(z_s[k], 1)

                def tanhs():
                    act.wait_ge(gate_mm, i + 1)
                    after(act, spl, 3 * i)
                    nc.scalar.activation(tg[:, :], a0[:, 0:VD + HEADS], ACT.Tanh, scale=0.5).then_inc(gate_th, 1)
                    act.wait_ge(conv, 4 * NCH * (i + 1))
                    after(act, silu_s, i)
                    nc.scalar.activation(th[:, :], y[:, :, :, :].rearrange("p c b t -> p (c b t)"), ACT.Tanh,
                                         scale=0.5).then_inc(tanh_s, 1)
                    nc.scalar.preload_act_table_set("natural_log_exp_and_others")

                def squares():
                    act.wait_ge(silu_s, i + 1)
                    after(act, ss_mm, i)
                    nc.scalar.activation(sq[:, :], sy[:, 0:QKC * P], ACT.Square).then_inc(sq_s, 1)

                def softplus():
                    act.wait_ge(spl, 3 * i + 2)
                    nc.scalar.activation(ez[:, :], az[:, :], ACT.Exp, scale=-1.0).then_inc(ez_s, 1)
                    act.wait_ge(ez_s, 2 * i + 1)
                    nc.scalar.activation(lz[:, :], ez[:, :], ACT.Ln, bias=1.0).then_inc(ez_s, 1)

                def inv_norms():
                    act.wait_ge(ss_mm, i + 1)
                    after(act, qk_s, i)
                    nc.scalar.activation(rl[:, :], a1[:, :], ACT.Ln, bias=eps_l2[:, :]).then_inc(rs_s, 1)
                    act.wait_ge(rs_s, 2 * i + 1)
                    nc.scalar.activation(rs[:, :], rl[:, :], ACT.Exp, scale=-0.5).then_inc(rs_s, 1)

                def v_copy():
                    act.wait_ge(v_mm, i + 1)
                    for f in range(2):
                        after(act, W_mm[f], i - 1)
                    nc.scalar.copy(V[p][:, :], a1[:, 0:VD]).then_inc(v_s, 1)
                return norm_rstd, x_copy, z_copy, tanhs, softplus, squares, inv_norms, v_copy

            def B(i, p):
                def decay():
                    for f in range(2):
                        act.wait_ge(d_mm[f], i + 1)
                        after(act, Eb_s[f], i)
                        nc.scalar.activation(E[:, f, :, :].rearrange("p h t -> p (h t)"), bP[f][:, 0:H3],
                                             ACT.Exp).then_inc(E_s[f], 1)

                def t_copy():
                    for f in range(2):
                        act.wait_ge(t1_mm[f], i + 1)
                        nc.scalar.copy(Ti[:, f, :, :].rearrange("p h t -> p (h t)"), bP[f][:, 0:H3]
                                       ).then_inc(T1_s[f], 1)

                def p_copy(l):
                    def go():
                        for f in range(2):
                            act.wait_ge(P_mm[f], NL * i + l)
                            after(act, XU_mm[f], NL * i + l - 1)
                            nc.scalar.copy(Pi[:, f, :, :].rearrange("p h t -> p (h t)"), bP[f][:, 0:H3]
                                           ).then_inc(P_s[f], 1)
                    return go

                def diag(b, f):
                    return b[f][:, 0:H3].rearrange("p (h d) -> p h d", d=P)

                def w_copy():
                    for f in range(2):
                        act.wait_ge(W_mm[f], i + 1)
                        for h in range(3):
                            c = 3 * f + h
                            o = c * DV - min(c * DV, VD - P)
                            m = nc.scalar.copy(W[:, f, h, :], bP[f][:, h * P + o:h * P + o + DV])
                        m.then_inc(W_s[f], 1)

                def pv_copy():
                    for f in range(2):
                        act.wait_ge(Pv_mm[f], i + 1)
                        nc.scalar.copy(Pv[:, f, 0:3, :], diag(bA, f)[:, :, 0:DV]).then_inc(Pv_s[f], 1)

                def o_squares():
                    for f in range(2):
                        act.wait_ge(O_mm[f], i + 1)
                        after(act, oss_s, i)
                        nc.scalar.activation(oq[:, f, :, :], diag(bP, f)[:, :, 0:DV], ACT.Square).then_inc(oq_s[f], 1)

                def o_rms():
                    act.wait_ge(oss_s, i + 1)
                    nc.scalar.activation(orl[:, :, :], oss[:, :, :], ACT.Ln, scale=1.0 / DV,
                                         bias=eps_rms[:, :]).then_inc(orr_s, 1)
                    act.wait_ge(orr_s, 2 * i + 1)
                    after(act, o1_s[1], i)
                    nc.scalar.activation(orr[:, :, :], orl[:, :, :], ACT.Exp, scale=-0.5).then_inc(orr_s, 1)

                def o_copy():
                    act.wait_ge(oT_mm, i + 1)
                    nc.scalar.copy(oT[:, :], bA[0][:, 0:VD]).then_inc(oT_s, 1)
                return decay, t_copy, p_copy, w_copy, pv_copy, o_squares, o_rms, o_copy

            act.wait_ge(zeroed, 8)
            for part in A(0):
                part()

            def both(i, a, b):
                decay, t_copy, p_copy, w_copy, pv_copy, o_squares, o_rms, o_copy = B(i, b)
                decay()
                if a is not None:
                    norm_rstd, x_copy, z_copy, tanhs, softplus, squares, inv_norms, v_copy = A(i + 1, a)
                    norm_rstd()
                    x_copy()
                t_copy()
                if a is not None:
                    z_copy()
                p_copy(1)()
                p_copy(2)()
                if a is not None:
                    tanhs()
                    softplus()
                p_copy(3)()
                if a is not None:
                    squares()
                p_copy(4)()
                if a is not None:
                    inv_norms()
                w_copy()
                if a is not None:
                    v_copy()
                pv_copy()
                o_squares()
                o_rms()
                o_copy()
            with act.Fori(0, TILES // 2 - 1) as t:
                both(2 * t, 1, 0)
                both(2 * t + 1, 0, 1)
            both(TILES - 2, 1, 0)
            both(TILES - 1, None, 1)

        @block.vector
        def _(dve):
            nc.vector.memset(zp[:, :, :, :], 0.0).then_inc(zeroed, 1)
            nc.vector.memset(W[:, :, :, :], 0.0).then_inc(zeroed, 1)
            nc.vector.memset(Pv[:, :, :, :], 0.0).then_inc(zeroed, 1)
            nc.vector.memset(U[:, :, :, :], 0.0).then_inc(zeroed, 1)
            nc.vector.memset(eps_ln[:, :], LN_EPS).then_inc(zeroed, 1)
            nc.vector.memset(eps_l2[:, :], L2_EPS).then_inc(zeroed, 1)
            nc.vector.memset(eps_rms[:, :], RMS_EPS).then_inc(zeroed, 1)
            dve.wait_ge(loaded, 16 * N_LOADS)
            dve.wait_ge(decay_e, 1)
            nc.vector.tensor_scalar(nega[:, :], ea[:, :], -1.0, None, ALU.mult).then_inc(decay_c, 1)
            nc.vector.tensor_scalar(nwh[:, :], nwh[:, :], 0.5, None, ALU.mult).then_inc(zeroed, 1)
            dve.wait_ge(zeroed, 8)
            dve.wait_ge(decay_c, 1)

            def A(i, p=0):
                xi = X[:, i, :] if isinstance(i, int) else X[:, bass.ds(i, 1), :].rearrange("p n d -> p (n d)")

                def norm():
                    after(dve, rstd_s, 2 * i)
                    nc.vector.bn_stats(st[:, :], xi).then_inc(stats, 1)
                    dve.wait_ge(stats, 2 * i + 1)
                    dve.sem_inc(held, 1)
                    nc.vector.bn_aggr(mv[:, :], st[:, :]).then_inc(stats, 1)
                    dve.wait_ge(rstd_s, 2 * (i + 1))
                    after(dve, xt_mm, i)
                    nc.vector.tensor_scalar(xn[:, :], xi, mv[:, 0:1], rstd[:, 0:1], ALU.subtract, ALU.mult
                                            ).then_inc(xn_s, 1)

                def convolve():
                    for k in range(2):
                        dve.wait_ge(z_s[k], i + 1)
                    after(dve, silu_s, i)
                    after(dve, tanh_s, i)
                    for j in range(4):
                        for c in range(NCH):
                            if j == 0:
                                nc.vector.tensor_scalar(y[:, c, :, :], zp[:, c, :, 3:3 + T], cw[:, c, 3:4], None,
                                                        ALU.mult).then_inc(conv, 1)
                            else:
                                dve.wait_ge(conv, 4 * NCH * i + (j - 1) * NCH + c + 1)
                                nc.vector.scalar_tensor_tensor(out=y[:, c, :, :], in0=zp[:, c, :, 3 - j:3 - j + T],
                                                               scalar=cw[:, c, 3 - j:4 - j], in1=y[:, c, :, :],
                                                               op0=ALU.mult, op1=ALU.add).then_inc(conv, 1)

                def gates():
                    dve.wait_ge(gate_th, i + 1)
                    after(dve, gw_s, i)
                    nc.vector.scalar_tensor_tensor(out=gs[:, :], in0=tg[:, 0:VD], scalar=1.0, in1=a0[:, 0:VD],
                                                   op0=ALU.add, op1=ALU.mult).then_inc(gs_s, 1)
                    nc.vector.tensor_tensor(zz[:, :], a0[:, VD + HEADS:VD + 2 * HEADS], dtb[:, :], ALU.add
                                            ).then_inc(gate_v, 1)
                    for f in range(2):
                        after(dve, Eb_s[f], i - 1)
                    nc.vector.tensor_scalar(beta[p][:, :], tg[:, VD:VD + HEADS], 0.5, 0.5, ALU.mult, ALU.add
                                            ).then_inc(spl, 1)
                    dve.wait_ge(gate_v, i + 1)
                    nc.vector.scalar_tensor_tensor(out=az[:, :], in0=zz[:, :], scalar=-1.0, in1=zz[:, :],
                                                   op0=ALU.mult, op1=ALU.max).then_inc(spl, 1)

                def softplus():
                    dve.wait_ge(ez_s, 2 * (i + 1))
                    nc.vector.scalar_tensor_tensor(out=sp_[:, :], in0=zz[:, :], scalar=0.0, in1=lz[:, :],
                                                   op0=ALU.max, op1=ALU.add).then_inc(spl, 1)
                    dve.wait_ge(spl, 3 * (i + 1))
                    nc.vector.tensor_tensor(g[p][:, :], sp_[:, :], nega[:, :], ALU.mult).then_inc(g_s, 1)

                def silus():
                    dve.wait_ge(tanh_s, i + 1)
                    after(dve, v_mm, i)
                    after(dve, qk_s, i)
                    nc.vector.scalar_tensor_tensor(out=sy[:, :], in0=th[:, :], scalar=1.0,
                                                   in1=y[:, :, :, :].rearrange("p c b t -> p (c b t)"),
                                                   op0=ALU.add, op1=ALU.mult).then_inc(silu_s, 1)

                def norm_qk():
                    dve.wait_ge(rs_s, 2 * (i + 1))
                    for f in range(2):
                        after(dve, kk_mm[f], i - 1)
                        after(dve, qk_mm[f], i - 1)
                    nc.vector.tensor_tensor(qk[p][:, :, :].rearrange("p c t -> p (c t)"), sy[:, 0:QKC * P], rs[:, :],
                                            ALU.mult).then_inc(qk_s, 1)
                return norm, convolve, gates, softplus, silus, norm_qk

            def B(i, p):
                xi = X[:, i, :] if isinstance(i, int) else X[:, bass.ds(i, 1), :].rearrange("p n d -> p (n d)")

                def k_heads():
                    dve.wait_ge(qk_s, i + 1)
                    for f in range(2):
                        after(dve, kk_mm[f], i)
                        after(dve, qk_mm[f], i)
                    for h in range(HEADS):
                        nc.vector.tensor_scalar(kM[:, h, :], qk[p][:, 2 + h // 3, :], hmask[:, h % 3:h % 3 + 1], None,
                                                ALU.mult).then_inc(kM_s, 1)

                def weigh():
                    for f in range(2):
                        dve.wait_ge(kk_mm[f], i + 1)
                        dve.wait_ge(EA_s[f], i + 1)
                        after(dve, LM_s[f], (LEVELS - 1) * i)
                        nc.vector.tensor_tensor(LT[:, f, :, :].rearrange("p h t -> p (h t)"), bA[f][:, 0:H3],
                                                EA[:, f, :, :].rearrange("p h t -> p (h t)"), ALU.mult
                                                ).then_inc(LT_s[f], 1)
                        dve.wait_ge(LT_s[f], i + 1)
                        after(dve, XU_mm[f], NL * i)
                        after(dve, U_mm[f], i)
                        nc.vector.tensor_tensor(LM[:, 0, f, :, :], LT[:, f, :, :],
                                                level[:, 0:1, :].to_broadcast([P, 3, P]), ALU.mult
                                                ).then_inc(L0_s[f], 1)
                        dve.wait_ge(L0_s[f], i + 1)
                        nc.vector.tensor_tensor(Xi[:, f, :, :], ident3, LM[:, 0, f, :, :], ALU.subtract
                                                ).then_inc(X1_s[f], 1)
                    for f in range(2):
                        dve.wait_ge(qk_mm[f], i + 1)
                        after(dve, O_mm[f], i)
                        nc.vector.tensor_tensor(AT[:, f, :, :].rearrange("p h t -> p (h t)"), bB[f][:, 0:H3],
                                                EA[:, f, :, :].rearrange("p h t -> p (h t)"), ALU.mult
                                                ).then_inc(AT_s[f], 1)

                def level_u(l):
                    def go():
                        for f in range(2):
                            dve.wait_ge(TU_mm[f], NL * i + l)
                            if l == 1:
                                dve.wait_ge(T1_s[f], i + 1)
                            else:
                                dve.wait_ge(T_s[f], NL * i + l - 1)
                            nc.vector.tensor_tensor(Ti[:, f, :, :].rearrange("p h t -> p (h t)"),
                                                    Ti[:, f, :, :].rearrange("p h t -> p (h t)"), bA[f][:, 0:H3],
                                                    ALU.subtract).then_inc(T_s[f], 1)
                            dve.wait_ge(XU_mm[f], NL * i + l)
                            if l == 1:
                                dve.wait_ge(X1_s[f], i + 1)
                            else:
                                dve.wait_ge(X_s[f], NL * i + l - 1)
                            nc.vector.tensor_tensor(Xi[:, f, :, :].rearrange("p h t -> p (h t)"),
                                                    Xi[:, f, :, :].rearrange("p h t -> p (h t)"), bB[f][:, 0:H3],
                                                    ALU.subtract).then_inc(X_s[f], 1)
                    return go

                def u_sub():
                    for f in range(2):
                        dve.wait_ge(U_mm[f], i + 1)
                        dve.wait_ge(W_s[f], i + 1)
                        after(dve, O_mm[f], i)
                        nc.vector.tensor_tensor(U[:, f, 0:3, :], W[:, f, 0:3, :],
                                                bB[f][:, 0:H3].rearrange("p (h d) -> p h d", d=P)[:, :, 0:DV],
                                                ALU.subtract).then_inc(U_s[f], 1)

                def o_norm():
                    for f in range(2):
                        dve.wait_ge(oq_s[f], i + 1)
                    after(dve, orr_s, 2 * i)
                    nc.vector.tensor_reduce(oss[:, :, :].rearrange("p f h -> p (f h)"),
                                            oq[:, :, :, :].rearrange("p f h d -> p (f h) d"), AX.X, ALU.add
                                            ).then_inc(oss_s, 1)
                    for f in range(2):
                        after(dve, o2_s, i)
                        if f == 0:
                            dve.wait_ge(orr_s, 2 * (i + 1))
                        m = nc.vector.tensor_tensor(o1[:, f, :, :],
                                                    bP[f][:, 0:H3].rearrange("p (h d) -> p h d", d=P)[:, :, 0:DV],
                                                    orr[:, f, :].unsqueeze(2).to_broadcast([P, 3, DV]), ALU.mult)
                        m.then_inc(o1_s[f], 1)
                    for f in range(2):
                        dve.wait_ge(o1_s[f], i + 1)
                    after(dve, oT_mm, i)
                    dve.wait_ge(gw_s, i + 1)
                    nc.vector.tensor_tensor(o2[:, :], o1[:, :, :, :].rearrange("p f h d -> p (f h d)"), gw[p][:, :],
                                            ALU.mult).then_inc(o2_s, 1)

                def add():
                    dve.wait_ge(out_mm, i + 1)
                    nc.vector.tensor_tensor(xi, xi, bB[0][:, 0:HID], ALU.add).then_inc(x_s, 1)
                return k_heads, weigh, level_u, u_sub, o_norm, add

            for part in A(0):
                part()

            def both(i, a, b):
                k_heads, weigh, level_u, u_sub, o_norm, add = B(i, b)
                nop = lambda: None
                norm, convolve, gates, softplus, silus, norm_qk = A(i + 1, a) if a is not None else (nop,) * 6
                k_heads()
                norm()
                weigh()
                level_u(1)()
                convolve()
                level_u(2)()
                gates()
                level_u(3)()
                softplus()
                silus()
                level_u(4)()
                norm_qk()
                u_sub()
                o_norm()
                add()
            with dve.Fori(0, TILES // 2 - 1) as t:
                both(2 * t, 1, 0)
                both(2 * t + 1, 0, 1)
            both(TILES - 2, 1, 0)
            both(TILES - 1, None, 1)

        @block.gpsimd
        def _(pool):
            pool.wait_ge(loaded, 16 * N_LOADS)
            pool.wait_ge(zeroed, 8)

            def gate_weight(i, p):
                pool.wait_ge(gs_s, i + 1)
                after(pool, o2_s, i - 1)
                nc.gpsimd.tensor_tensor(gw[p][:, :], gs[:, :], nwh[:, :], ALU.mult).then_inc(gw_s, 1)

            def decays(i, p):
                pool.wait_ge(g_s, i + 1)
                for f in range(2):
                    after(pool, d_mm[f], i)
                    nc.gpsimd.tensor_tensor(rD[:, f, :, :], upto[:, :].unsqueeze(1).to_broadcast([P, 3, P]),
                                            g[p][:, 3 * f:3 * f + 3].unsqueeze(2).to_broadcast([P, 3, P]), ALU.mult
                                            ).then_inc(rD_s[f], 1)

            def weights(i, p):
                for f in range(2):
                    pool.wait_ge(E_s[f], i + 1)
                    after(pool, EA_s[f], i)
                    nc.gpsimd.tensor_tensor(Eb[:, f, :, :], E[:, f, :, :],
                                            beta[p][:, 3 * f:3 * f + 3].unsqueeze(2).to_broadcast([P, 3, P]),
                                            ALU.mult).then_inc(Eb_s[f], 1)
                    pool.wait_ge(Eb_s[f], i + 1)
                    after(pool, LT_s[f], i)
                    after(pool, AT_s[f], i)
                    nc.gpsimd.tensor_tensor(EA[:, f, :, :], Eb[:, f, :, :],
                                            upto[:, :].unsqueeze(1).to_broadcast([P, 3, P]), ALU.mult
                                            ).then_inc(EA_s[f], 1)

            def levels(i, p):
                for l in range(1, LEVELS):
                    for f in range(2):
                        pool.wait_ge(LT_s[f], i + 1)
                        after(pool, Pv_mm[f], i)
                        nc.gpsimd.tensor_tensor(LM[:, l, f, :, :], LT[:, f, :, :],
                                                level[:, l:l + 1, :].to_broadcast([P, 3, P]), ALU.mult
                                                ).then_inc(LM_s[f], 1)

            gate_weight(0, 0)
            decays(0, 0)

            def both(i, a, b):
                weights(i, b)
                levels(i, b)
                if a is not None:
                    gate_weight(i + 1, a)
                    decays(i + 1, a)
            with pool.Fori(0, TILES // 2 - 1) as t:
                both(2 * t, 1, 0)
                both(2 * t + 1, 0, 1)
            both(TILES - 2, 1, 0)
            both(TILES - 1, None, 1)


def constants():
    r, c = np.arange(P)[:, None], np.arange(P)[None, :]
    same = r // T == c // T
    level = [same & (r // (2 * m) == c // (2 * m)) & (r // m % 2 == 0) & (c // m % 2 == 1)
             for m in (1 << l for l in range(LEVELS))]
    f = np.float32
    return {
        "c_ident": np.eye(P, dtype=f),
        "c_upto": (same & (r <= c)).astype(f),
        "c_past": (same & (r > c)).astype(f),
        "c_level": np.stack(level).astype(f),
        "c_heads32": (r // DK == c // DK).astype(f),
        "c_hmask": np.stack([(np.arange(P) // DK == h) for h in range(3)], 1).astype(f),
    }


def banded_attention(nc, X, dram, sems):
    with ExitStack() as ctx:
        def sb(name, shape, dt=F32):
            return ctx.enter_context(nc.sbuf_tensor(name, shape, dt))

        def bank(name, dt=F32):
            return ctx.enter_context(nc.psum_tensor(name, [P, 2048 // (4 if dt == F32 else 2)], dt))

        def sem(name):
            sems.append(nc.alloc_semaphore(name))
            return sems[-1]

        UNITS = 2 * TILES
        NH, D8 = 8, 8
        KEYS = 256
        SPAN = 192
        ROWS = 9 * D8
        SUB = 8

        ident32 = sb("b_ident32", [P, P])
        band32 = sb("b_band32", [P, 2, SPAN])
        identb = sb("b_identb", [P, P], BF16)
        band = sb("b_band", [P, 2, SPAN], BF16)
        seld = sb("b_seld", [P, P])
        wq = sb("b_wq", [P, P])
        wk = sb("b_wk", [P, P])
        wv = sb("b_wv", [P, P])
        wout = sb("b_wout", [P, 2, T])
        wct = sb("b_wct", [P, P])
        bq = sb("b_bq", [P, 1])
        bk = sb("b_bk", [P, 1])
        bv = sb("b_bv", [P, 2 * P])
        bo = sb("b_bo", [P, 1])
        bct = sb("b_bct", [P, 1])
        ctxs = [sb(f"b_ctx{p}", [P, HID]) for p in range(2)]
        eps = sb("b_eps", [P, 1])

        st = sb("b_st", [P, 6])
        mv = sb("b_mv", [P, 2])
        lv = sb("b_lv", [P, 1])
        rstd = sb("b_rstd", [P, 1])
        xn = sb("b_xn", [P, HID])
        r0 = sb("b_r0", [P, 2 * KEYS])
        r1 = sb("b_r1", [P, 2 * KEYS])
        r2 = sb("b_r2", [P, 2 * KEYS])
        parts = sb("b_parts", [P, 3, 2, KEYS], BF16)
        QS = [sb(f"b_QS{p}", [P, 2 * NH, KEYS], BF16) for p in range(2)]
        KS = [sb(f"b_KS{p}", [P, 2 * NH, KEYS], BF16) for p in range(2)]
        VA = [sb(f"b_VA{p}", [P, 2, 2 * NH, 32]) for p in range(2)]
        nm = sb("b_nm", [P, 2, NH])
        n1 = sb("b_n1", [P, 2, NH])
        n2 = sb("b_n2", [P, 2, NH])
        NPt = sb("b_NP", [P, 2, 3, NH], BF16)
        MT = sb("b_MT", [3 * NH, KEYS], BF16)
        PT = [sb(f"b_PT{k}", [P, 2, SPAN]) for k in range(4)]
        Os = sb("b_Os", [P, 2 * KEYS])
        lD = sb("b_lD", [P, 2 * KEYS])
        rDn = sb("b_rDn", [P, 2 * KEYS])
        On = sb("b_On", [P, 2 * KEYS])
        yr = sb("b_yr", [P, HID])
        yy = sb("b_yy", [P, HID])

        bM = [bank(f"b_bM{k}") for k in range(2)]
        bS = [bank(f"b_bS{k}") for k in range(2)]
        bO = bank("b_bO")
        m0 = bank("b_m0")
        m1 = bank("b_m1")
        m2 = bank("b_m2")
        m2h = m2[:, :].bitcast(BF16)

        scratch = [nc.dram_tensor(f"b_scratch{p}", [3, 2, P, KEYS], BF16, kind="Internal").ap() for p in range(2)]

        mscratch = [nc.dram_tensor(f"b_mscratch{b}", [3 * NH, KEYS], BF16, kind="Internal").ap() for b in range(2)]

        loaded = sem("b_loaded")
        ctx_ld = [sem(f"b_ctx_ld{p}") for p in range(2)]
        zeroed = sem("b_zeroed")
        zeroed_k = sem("b_zeroed_k")
        held = sem("b_held")
        stats = sem("b_stats")
        rstd_s = sem("b_rstd")
        xn_s = sem("b_xn")
        qk_mm = sem("b_qk_mm")
        v_mm = sem("b_v_mm")
        r0_s = sem("b_r0")
        part_s = [sem(f"b_part{j}") for j in range(3)]
        r1_s = sem("b_r1")
        r2_s = sem("b_r2")
        v_s = sem("b_v")
        put = [sem(f"b_put{p}") for p in range(2)]
        got = [sem(f"b_got{p}") for p in range(2)]
        max_mm = sem("b_max_mm")
        max_s = sem("b_max")
        np_s = sem("b_np")
        mt_mm = sem("b_mt_mm")
        mt_s = sem("b_mt")
        mput = sem("b_mput")
        mrow = [sem(f"b_mrow{b}") for b in range(2)]
        s_mm = sem("b_s_mm")
        exp_s = sem("b_exp")
        pv_mm = sem("b_pv_mm")
        o_s = sem("b_o")
        den_mm = sem("b_den_mm")
        ln_s = sem("b_ln")
        on_s = sem("b_on")
        out_mm = sem("b_out_mm")
        relu_s = sem("b_relu")
        y_s = sem("b_y")
        ct_mm = sem("b_ct_mm")
        x_s = sem("b_x")


        ZEROED = 9
        block = ctx.enter_context(nc.Block())

        def run_slots(slot):
            for k in range(4):
                slot(0, k)
            with slot.engine.Fori(1, UNITS // 4 - 1) as t:
                for k in range(4):
                    slot(t, k)
            for k in range(4):
                slot(UNITS // 4 - 1, k)

        def is_first(t, k):
            return isinstance(t, int) and t == 0 and k == 0

        def has_next_unit(t, k):
            return not (isinstance(t, int) and 4 * t + k == UNITS - 1)

        def has_tile(t, k, ahead):
            return not isinstance(t, int) or 2 * t + k // 2 + ahead < TILES

        @block.sync
        def _(sp):
            for dst, src in ((ident32, "c_ident"), (seld, "c_seld"), (wct, "w_ct"),
                             (bq, "b_q"), (bk, "b_k"), (bv, "b_v"), (bo, "b_out"), (bct, "b_ct")):
                sp.dma_start(dst[:, :], dram[src]).then_inc(loaded, 16)
            for dst, src in ((band32, "c_band"), (wout, "w_out")):
                sp.dma_start(dst[:, :, :], dram[src]).then_inc(loaded, 16)
            for n, dst in enumerate((wq, wk, wv)):
                sp.dma_start(dst[:, :], dram["w_in"][n]).then_inc(loaded, 16)

            def stack(i, p, half):
                after(sp, s_mm, 2 * SUB * (i - 1))
                sp.sem_inc(held, 1)
                sp.wait_ge(part_s[2], i + 1)
                sp.sem_inc(held, 1)
                sp.dma_start(scratch[p].rearrange("j w c t -> c (j w) t"),
                             parts[:, :, :, :].rearrange("c j w t -> c (j w) t")).then_inc(put[p], 16)
                sp.wait_ge(put[p], 16 * (half + 1))
                for a in range(3):
                    for b in range(3):
                        r = (3 * a + b) * D8
                        for side, dst, part in ((0, QS, a), (1, KS, b)):
                            sp.dma_start(dst[p][r:r + D8, :, :],
                                         scratch[p][part, side].rearrange("(g d) t -> d g t", d=D8)
                                         ).then_inc(got[p], 16)

            def load_ctx(i, p):
                rows = dram["ctx"][i] if isinstance(i, int) else \
                    dram["ctx"][bass.ds(i, 1)].rearrange("n p d -> (n p) d")
                after(sp, y_s, i - 1)
                sp.sem_inc(held, 1)
                sp.dma_start(ctxs[p][:, :], rows).then_inc(ctx_ld[p], 16)

            def max_rows(u, b, p):
                sp.wait_ge(mt_s, u + 1)
                sp.dma_start(mscratch[b], MT[:, :]).then_inc(mput, 16)
                sp.wait_ge(mput, 16 * (u + 1))
                sp.dma_start(QS[p][ROWS:ROWS + 3, b * NH:(b + 1) * NH, :],
                             mscratch[b].rearrange("(a h) t -> a h t", h=NH)).then_inc(mrow[b], 16)

            sp.wait_ge(zeroed, ZEROED)
            sp.wait_ge(zeroed_k, 2)
            load_ctx(0, 0)
            stack(0, 0, 0)
            max_rows(0, 0, 0)

            def slot(t, k):
                u, i, b, p = 4 * t + k, 2 * t + k // 2, k % 2, k // 2
                if b == 0 and has_tile(t, k, 1):
                    stack(i + 1, 1 - p, t + k // 2)
                if has_next_unit(t, k):
                    max_rows(u + 1, 1 - b, p if b == 0 else 1 - p)
                if b == 1 and has_tile(t, k, 1):
                    load_ctx(i + 1, 1 - p)
            slot.engine = sp
            run_slots(slot)

        @block.tensor
        def _(pe):
            pe.wait_ge(loaded, 16 * 13)
            pe.wait_ge(zeroed, ZEROED)
            pe.wait_ge(zeroed_k, 2)

            def project(i):
                pe.wait_ge(xn_s, i + 1)
                after(pe, ln_s, 2 * (2 * i - 4) + 1)
                after(pe, relu_s, 2 * i - 3)
                for n, w in enumerate((wq, wk)):
                    m = nc.tensor.matmul(m0[:, n * KEYS:(n + 1) * KEYS], w[:, :], xn[:, :], start=True, stop=True)
                m.then_inc(qk_mm, 1)
                for c in range(2):
                    m = nc.tensor.matmul(m1[:, c * P:(c + 1) * P], xn[:, c * P:(c + 1) * P], wv[:, :],
                                         start=True, stop=True)
                m.then_inc(v_mm, 1)

            def maximum(u, b, p, n):
                hp, qt = n // 2, n % 2
                after(pe, max_s, SUB * u + n - 1)
                o = bM[n % 2]
                nc.tensor.matmul(o[:, 0:2 * SPAN].rearrange("p (h k) -> p h k", h=2), identb[:, :],
                                 band[:, qt:qt + 1, :].to_broadcast([P, 2, SPAN]),
                                 start=True, stop=False, skip_group_check=True)
                for h in range(2):
                    g = b * NH + 2 * hp + h
                    m = nc.tensor.matmul(o[:, h * SPAN:(h + 1) * SPAN], QS[p][0:ROWS, g, qt * P:(qt + 1) * P],
                                         KS[p][0:ROWS, g, qt * T:qt * T + SPAN],
                                         start=False, stop=True, skip_group_check=True)
                m.then_inc(max_mm, 1)

            def turn_max(u):
                pe.wait_ge(np_s, 5 * (u + 1))
                after(pe, mt_s, u)
                for c in range(2):
                    m = nc.tensor.transpose(m2h[0:3 * NH, c * P:(c + 1) * P],
                                            NPt[:, c, :, :].rearrange("p j h -> p (j h)"), identb[:, :])
                m.then_inc(mt_mm, 1)

            def score(u, b, p, n):
                hp, kt = n // 2, n % 2
                after(pe, exp_s, SUB * u + n - 1)
                o = bS[n % 2]
                nc.tensor.matmul(o[:, 0:2 * SPAN].rearrange("p (h k) -> p h k", h=2), identb[:, :],
                                 band[:, kt:kt + 1, :].to_broadcast([P, 2, SPAN]),
                                 start=True, stop=False, skip_group_check=True)
                for h in range(2):
                    g = b * NH + 2 * hp + h
                    m = nc.tensor.matmul(o[:, h * SPAN:(h + 1) * SPAN], KS[p][:, g, kt * P:(kt + 1) * P],
                                         QS[p][:, g, kt * T:kt * T + SPAN],
                                         start=False, stop=True, skip_group_check=True)
                m.then_inc(s_mm, 1)

            def weigh(u, b, p, n):
                hp, kt = n // 2, n % 2
                pe.wait_ge(exp_s, SUB * u + n + 1)
                if n == 0:
                    after(pe, o_s, u)
                for h in range(2):
                    g = 2 * hp + h
                    r, c = 32 * (g % 4), (g // 4) * KEYS + kt * T
                    m = nc.tensor.matmul(bO[r:r + 32, c:c + SPAN], VA[p][:, kt, b * NH + g, :],
                                         PT[n % 4][:, h, :], start=(kt == 0), stop=(kt == 1),
                                         skip_group_check=True, tile_position=(0, r))
                m.then_inc(pv_mm, 1)

            def sums(u):
                pe.wait_ge(o_s, u + 1)
                nc.tensor.matmul(m0[:, :], seld[:, :], Os[:, :], start=True, stop=True).then_inc(den_mm, 1)

            def out_project(u, b):
                pe.wait_ge(on_s, u + 1)
                for g in range(2):
                    m = nc.tensor.matmul(m1[b * T:(b + 1) * T, 0:KEYS], wout[:, g, :], On[:, g * KEYS:(g + 1) * KEYS],
                                         start=(g == 0), stop=(g == 1))
                m.then_inc(out_mm, 1)

            def combine(i):
                pe.wait_ge(y_s, i + 1)
                nc.tensor.matmul(m2[:, 0:KEYS], wct[:, :], yy[:, :], start=True, stop=True).then_inc(ct_mm, 1)

            def slot(t, k):
                u, i, b, p = 4 * t + k, 2 * t + k // 2, k % 2, k // 2
                first = is_first(t, k)
                for n in range(SUB + 2):
                    if n == 0 and b == 0 and has_tile(t, k, 1):
                        project(i + 1)
                    if n == 1 and b == 1 and (not isinstance(t, int) or i >= 1):
                        pe.wait_ge(mt_s, u + 1)
                        combine(i - 1)
                    if n == 3 and not first:
                        if b == 0:
                            pe.wait_ge(r0_s, 2 * (i + 2) if has_tile(t, k, 1) else 2 * TILES)
                        else:
                            after(pe, ln_s, 2 * (u - 1))
                        sums(u - 1)
                    if n == 6 and not first:
                        if b == 0:
                            pe.wait_ge(v_s, i + 2 if has_tile(t, k, 1) else TILES)
                        else:
                            after(pe, relu_s, u - 1)
                        out_project(u - 1, 1 - b)
                    if n == 8 and has_next_unit(t, k):
                        if b == 1 and (not isinstance(t, int) or i >= 1):
                            pe.wait_ge(x_s, i)
                        turn_max(u + 1)
                    if n < SUB:
                        if n == 0:
                            pe.wait_ge(mrow[b], 16 * (i + 1))
                            pe.wait_ge(v_s, i + 1)
                        score(u, b, p, n)
                    if 1 <= n <= 4 and has_next_unit(t, k):
                        if n == 1 and b == 1:
                            pe.wait_ge(got[1 - p], 16 * 18 * (t + p + 1))
                        for m in range(2 * n - 2, 2 * n):
                            maximum(u + 1, 1 - b, p if b == 0 else 1 - p, m)
                    if n >= 2:
                        weigh(u, b, p, n - 2)

            project(0)
            pe.wait_ge(got[0], 16 * 18)
            for m in range(SUB):
                maximum(0, 0, 0, m)
            turn_max(0)
            slot.engine = pe
            run_slots(slot)
            last = UNITS - 1
            pe.wait_ge(ln_s, 2 * last)
            sums(last)
            pe.wait_ge(relu_s, last)
            out_project(last, 1)
            combine(TILES - 1)

        @block.scalar
        def _(act):
            nc.scalar.preload_act_table_set("natural_log_exp_and_others")
            act.wait_ge(loaded, 16 * 13)
            act.wait_ge(zeroed, ZEROED)

            def norm(i):
                act.wait_ge(stats, 2 * (i + 1))
                nc.scalar.activation(lv[:, :], mv[:, 1:2], ACT.Ln, bias=eps[:, :]).then_inc(rstd_s, 1)
                act.wait_ge(rstd_s, 2 * i + 1)
                nc.scalar.activation(rstd[:, :], lv[:, :], ACT.Exp, scale=-0.5).then_inc(rstd_s, 1)

            def part(i, j):
                src, ready = ((r0, r0_s), (r1, r1_s), (r2, r2_s))[j]
                act.wait_ge(ready, (2 if j == 0 else 1) * (i + 1))
                nc.scalar.copy(parts[:, j, :, :].rearrange("p w t -> p (w t)"), src[:, :]).then_inc(part_s[j], 1)

            def exps(u, n):
                act.wait_ge(s_mm, SUB * u + n + 1)
                after(act, pv_mm, SUB * u + n - 3)
                nc.scalar.activation(PT[n % 4][:, :, :].rearrange("p h t -> p (h t)"), bS[n % 2][:, 0:2 * SPAN],
                                     ACT.Exp).then_inc(exp_s, 1)

            def inverse_sums(u):
                act.wait_ge(den_mm, u + 1)
                after(act, on_s, u)
                nc.scalar.activation(lD[:, :], m0[:, :], ACT.Ln).then_inc(ln_s, 1)
                act.wait_ge(ln_s, 2 * u + 1)
                nc.scalar.activation(rDn[:, :], lD[:, :], ACT.Exp, scale=-1.0).then_inc(ln_s, 1)

            def relu(u, b, i):
                act.wait_ge(out_mm, u + 1)
                after(act, y_s, i)
                nc.scalar.activation(yr[b * T:(b + 1) * T, :], m1[b * T:(b + 1) * T, 0:KEYS], ACT.Relu,
                                     bias=bo[b * T:(b + 1) * T, :]).then_inc(relu_s, 1)

            def turned(u):
                act.wait_ge(mt_mm, u + 1)
                nc.scalar.copy(MT[:, :], m2h[0:3 * NH, 0:KEYS]).then_inc(mt_s, 1)

            def slot(t, k):
                u, i, b, p = 4 * t + k, 2 * t + k // 2, k % 2, k // 2
                first = is_first(t, k)
                nxt = b == 0 and has_tile(t, k, 1)
                for n in range(SUB):
                    exps(u, n)
                    if n == 0 and nxt:
                        act.wait_ge(put[p], 16 * (t + 1))
                    if n < 3 and nxt:
                        part(i + 1, n)
                    if n == 4 and not first:
                        inverse_sums(u - 1)
                    if n == 7 and not first:
                        relu(u - 1, 1 - b, i - 1 if b == 0 else i)
                if has_next_unit(t, k):
                    act.wait_ge(mput, 16 * (u + 1))
                    turned(u + 1)
                if b == 1 and has_tile(t, k, 2):
                    norm(i + 2)

            norm(0)
            for j in range(3):
                part(0, j)
            norm(1)
            turned(0)
            slot.engine = act
            run_slots(slot)
            inverse_sums(UNITS - 1)
            relu(UNITS - 1, 1, TILES - 1)

        @block.vector
        def _(dve):
            for p in range(2):
                nc.vector.memset(QS[p][64:P, :, :], 0.0).then_inc(zeroed, 1)
                nc.vector.memset(VA[p][:, :, :, :], 0.0).then_inc(zeroed, 1)
                dve.wait_ge(zeroed, 3 * p + 2)
                nc.vector.memset(VA[p][:, :, :, D8:D8 + 1], 1.0).then_inc(zeroed, 1)
            nc.vector.memset(eps[:, :], LN_EPS).then_inc(zeroed, 1)
            dve.wait_ge(loaded, 16 * 13)
            nc.vector.tensor_copy(identb[:, :], ident32[:, :]).then_inc(zeroed, 1)
            nc.vector.tensor_copy(band[:, :, :], band32[:, :, :]).then_inc(zeroed, 1)
            dve.wait_ge(zeroed, ZEROED)

            def tile_of(i):
                return X[:, i, :] if isinstance(i, int) else X[:, bass.ds(i, 1), :].rearrange("p n d -> p (n d)")

            def norm(i):
                nc.vector.bn_stats(st[:, :], tile_of(i)).then_inc(stats, 1)
                dve.wait_ge(stats, 2 * i + 1)
                dve.sem_inc(held, 1)
                nc.vector.bn_aggr(mv[:, :], st[:, :]).then_inc(stats, 1)

            def normalise(i):
                dve.wait_ge(rstd_s, 2 * (i + 1))
                after(dve, v_mm, i)
                nc.vector.tensor_scalar(xn[:, :], tile_of(i), mv[:, 0:1], rstd[:, 0:1], ALU.subtract, ALU.mult
                                        ).then_inc(xn_s, 1)

            def take_qkv(i, p):
                dve.wait_ge(qk_mm, i + 1)
                after(dve, r1_s, i)
                after(dve, part_s[0], i)
                nc.vector.tensor_scalar(r0[:, 0:KEYS], m0[:, 0:KEYS], bq[:, 0:1], float(D8) ** -0.5,
                                        ALU.add, ALU.mult).then_inc(r0_s, 1)
                nc.vector.tensor_scalar(r0[:, KEYS:2 * KEYS], m0[:, KEYS:2 * KEYS], bk[:, 0:1], None,
                                        ALU.add).then_inc(r0_s, 1)
                dve.wait_ge(v_mm, i + 1)
                after(dve, pv_mm, 2 * SUB * (i - 1))
                nc.vector.tensor_tensor(VA[p][:, :, :, 0:D8].rearrange("p c g d -> p (c g) d"),
                                        m1[:, 0:2 * P].rearrange("p (c d) -> p c d", d=D8),
                                        bv[:, :].rearrange("p (c d) -> p c d", d=D8), ALU.add).then_inc(v_s, 1)

            def maximum(u, n):
                dve.wait_ge(max_mm, SUB * u + n + 1)
                if n == 0:
                    after(dve, np_s, 5 * u)
                hp, qt = n // 2, n % 2
                nc.vector.tensor_reduce(nm[:, qt, 2 * hp:2 * hp + 2],
                                        bM[n % 2][:, 0:2 * SPAN].rearrange("p (h k) -> p h k", h=2),
                                        AX.X, ALU.max, negate=True).then_inc(max_s, 1)

            def take_o(u):
                dve.wait_ge(pv_mm, SUB * (u + 1))
                after(dve, den_mm, u)
                after(dve, on_s, u)
                nc.vector.tensor_copy(Os[:, :], bO[:, :]).then_inc(o_s, 1)

            def divide(u):
                dve.wait_ge(ln_s, 2 * (u + 1))
                after(dve, out_mm, u)
                nc.vector.tensor_tensor(On[:, :], Os[:, :], rDn[:, :], ALU.mult).then_inc(on_s, 1)

            def add(i):
                dve.wait_ge(ct_mm, i + 1)
                nc.vector.scalar_tensor_tensor(out=tile_of(i), in0=m2[:, 0:KEYS], scalar=bct[:, 0:1], in1=tile_of(i),
                                               op0=ALU.add, op1=ALU.add).then_inc(x_s, 1)

            def slot(t, k):
                u, i, b, p = 4 * t + k, 2 * t + k // 2, k % 2, k // 2
                first = is_first(t, k)
                if b == 0 and has_tile(t, k, 1):
                    take_qkv(i + 1, 1 - p)
                if has_next_unit(t, k):
                    for n in range(4):
                        maximum(u + 1, n)
                if b == 1 and (not isinstance(t, int) or i >= 1):
                    add(i - 1)
                if has_next_unit(t, k):
                    for n in range(4, SUB):
                        maximum(u + 1, n)
                if not first:
                    divide(u - 1)
                if b == 1 and has_tile(t, k, 2):
                    norm(i + 2)
                take_o(u)
                if b == 1 and has_tile(t, k, 2):
                    normalise(i + 2)

            norm(0)
            normalise(0)
            take_qkv(0, 0)
            norm(1)
            normalise(1)
            for n in range(SUB):
                maximum(0, n)
            slot.engine = dve
            run_slots(slot)
            divide(UNITS - 1)
            add(TILES - 1)

        @block.gpsimd
        def _(pool):
            for p in range(2):
                nc.gpsimd.memset(KS[p][64:P, :, :], 1.0).then_inc(zeroed_k, 1)
            pool.wait_ge(zeroed, ZEROED)

            def rest(i, j):
                src, dst, done = ((r0, r1, r1_s), (r1, r2, r2_s))[j]
                pool.wait_ge(part_s[j], i + 1)
                after(pool, part_s[j + 1], i)
                nc.gpsimd.tensor_tensor(dst[:, :], src[:, :], parts[:, j, :, :].rearrange("p w t -> p (w t)"),
                                        ALU.subtract).then_inc(done, 1)

            def split_max(u):
                pool.wait_ge(max_s, SUB * (u + 1))
                after(pool, mt_mm, u)
                pool.sem_inc(held, 1)
                s = 5 * u
                nc.gpsimd.tensor_copy(NPt[:, :, 0, :], nm[:, :, :]).then_inc(np_s, 1)
                pool.wait_ge(np_s, s + 1)
                nc.gpsimd.tensor_tensor(n1[:, :, :], nm[:, :, :], NPt[:, :, 0, :], ALU.subtract).then_inc(np_s, 1)
                pool.wait_ge(np_s, s + 2)
                pool.sem_inc(held, 1)
                nc.gpsimd.tensor_copy(NPt[:, :, 1, :], n1[:, :, :]).then_inc(np_s, 1)
                pool.wait_ge(np_s, s + 3)
                nc.gpsimd.tensor_tensor(n2[:, :, :], n1[:, :, :], NPt[:, :, 1, :], ALU.subtract).then_inc(np_s, 1)
                pool.wait_ge(np_s, s + 4)
                pool.sem_inc(held, 1)
                nc.gpsimd.tensor_copy(NPt[:, :, 2, :], n2[:, :, :]).then_inc(np_s, 1)

            def times_ctx(i, p, half):
                pool.wait_ge(relu_s, 2 * (i + 1))
                pool.wait_ge(ctx_ld[p], 16 * (half + 1))
                after(pool, ct_mm, i)
                nc.gpsimd.tensor_tensor(yy[:, :], yr[:, :], ctxs[p][:, :], ALU.mult).then_inc(y_s, 1)

            def slot(t, k):
                u, i, b, p = 4 * t + k, 2 * t + k // 2, k % 2, k // 2
                if b == 0 and has_tile(t, k, 1):
                    rest(i + 1, 0)
                    rest(i + 1, 1)
                if has_next_unit(t, k):
                    split_max(u + 1)
                if b == 0 and (not isinstance(t, int) or i >= 1):
                    times_ctx(i - 1, 1 - p, t - 1 + p)

            rest(0, 0)
            rest(0, 1)
            split_max(0)
            slot.engine = pool
            run_slots(slot)
            times_ctx(TILES - 1, 1, TILES // 2 - 1)


def attention_constants():
    r = np.arange(P)[:, None]
    c = np.arange(192)[None, :]
    masks = []
    for half in range(2):
        query, key = half * P + r, half * 64 + c
        masks.append(np.where(np.abs(query - key) <= 64, 0.0, -1e30))
    band = np.ascontiguousarray(np.stack(masks, 1)).astype(np.float32)
    rr, cc = np.arange(P)[:, None], np.arange(P)[None, :]
    return {
        "c_band": band,
        "c_seld": ((rr // 32 == cc // 32) & (rr % 32 == 8)).astype(np.float32),
    }


def experts(nc, X, dram, sems, out):
    with ExitStack() as ctx:
        def sb(name, shape, dt=F32):
            return ctx.enter_context(nc.sbuf_tensor(name, shape, dt))

        def bank(name, dt=F32):
            return ctx.enter_context(nc.psum_tensor(name, [P, 512], dt))

        def sem(name):
            sems.append(nc.alloc_semaphore(name))
            return sems[-1]

        OLD, NEW, TOPK, CAP, INTER = 128, 48, 8, 96, 96
        ROW = HID + NEW
        HALF = TOKENS // 2
        HT = TILES // 2
        ROUNDS = CAP // TOPK
        RING = 4

        ident = sb("e_ident", [P, P])
        identb = sb("e_identb", [P, P], BF16)
        names = sb("e_names", [P, NEW])
        ramp = sb("e_ramp", [P, HALF])
        slotno = sb("e_slotno", [NEW, CAP])
        o2n = sb("e_o2n", [P, 1], I32)
        o2nf = sb("e_o2nf", [P, 1])
        perm = sb("e_perm", [P, NEW])
        gate = sb("e_gate", [P, HID])
        gT = sb("e_gT", [P, 2, NEW])
        eps = sb("e_eps", [P, 1])
        zrow = sb("e_zrow", [CAP, ROW])

        st = [sb(f"e_st{p}", [P, 6]) for p in range(2)]
        mv = [sb(f"e_mv{p}", [P, 2]) for p in range(2)]
        lv = [sb(f"e_lv{p}", [P, 1]) for p in range(2)]
        rstd = [sb(f"e_rstd{p}", [P, 1]) for p in range(2)]
        hw = [sb(f"e_hw{p}", [P, ROW]) for p in range(2)]
        hT = [sb(f"e_hT{p}", [P, 2, P]) for p in range(2)]
        lg = [sb(f"e_lg{p}", [P, NEW]) for p in range(2)]
        top = [sb(f"e_top{p}", [P, TOPK]) for p in range(2)]
        rest = [sb(f"e_rest{p}", [P, NEW]) for p in range(2)]
        chosen = [sb(f"e_chosen{p}", [P, NEW], BF16) for p in range(2)]
        ntop = [sb(f"e_ntop{p}", [P, 1]) for p in range(2)]
        ex = [sb(f"e_ex{p}", [P, NEW]) for p in range(2)]
        em = [sb(f"e_em{p}", [P, NEW]) for p in range(2)]
        es = [sb(f"e_es{p}", [P, 1]) for p in range(2)]
        ei = [sb(f"e_ei{p}", [P, 1]) for p in range(2)]
        queue = sb("e_queue", [P, HALF])
        first1 = sb("e_first1", [P, CAP])
        both2 = sb("e_both2", [NEW, 2 * CAP])
        first2 = sb("e_first2", [NEW, CAP])
        none = sb("e_none", [NEW, CAP])
        idf = sb("e_idf", [NEW, CAP])
        index = sb("e_index", [CAP, NEW], I32)
        gi = [sb(f"e_gi{k}", [CAP, 1], I32) for k in range(RING)]
        si = [sb(f"e_si{k}", [CAP, 1], I32) for k in range(2)]
        G = [sb(f"e_G{k}", [CAP, ROW]) for k in range(RING)]
        wgu = [sb(f"e_wgu{k}", [P, 2, 2 * INTER]) for k in range(RING)]
        wdn = [sb(f"e_wdn{k}", [INTER, HID]) for k in range(RING)]
        GT = [sb(f"e_GT{p}", [P, 2, CAP]) for p in range(2)]
        sg = [sb(f"e_sg{p}", [INTER, CAP]) for p in range(2)]
        act_ = [sb(f"e_act{p}", [INTER, CAP]) for p in range(2)]
        Y = [sb(f"e_Y{p}", [CAP, HID]) for p in range(2)]

        bT = [bank(f"e_bT{p}") for p in range(2)]
        bL = [bank(f"e_bL{p}") for p in range(2)]
        bC = [bank(f"e_bC{p}") for p in range(2)]
        bD = [bank(f"e_bD{p}") for p in range(2)]

        rows = nc.dram_tensor("e_rows", [TOKENS + CAP, ROW], F32, kind="Internal").ap()
        acc = nc.dram_tensor("e_acc", [TOKENS + CAP, HID], F32, kind="Internal").ap()

        loaded = sem("e_loaded")
        consts = sem("e_consts")
        held = sem("e_held")
        gT_mm = sem("e_gT_mm")
        gT_s = sem("e_gT")
        stats = sem("e_stats")
        rstd_s = sem("e_rstd")
        h_s = sem("e_h")
        hT_mm = sem("e_hT_mm")
        hT_s = sem("e_hT")
        l_mm = sem("e_l_mm")
        lg_s = sem("e_lg")
        top_s = sem("e_top")
        rest_s = sem("e_rest")
        chosen_s = sem("e_chosen")
        ntop_s = sem("e_ntop")
        ex_s = sem("e_ex")
        em_s = sem("e_em")
        ei_s = sem("e_ei")
        w_s = sem("e_w")
        c_mm = sem("e_c_mm")
        queue_s = sem("e_queue")
        rows_out = [sem(f"e_rows_out{p}") for p in range(2)]
        acc_out = sem("e_acc_out")
        pad_out = sem("e_pad_out")
        pick = sem("e_pick")
        pick2 = sem("e_pick2")
        idf_s = sem("e_idf")
        id_mm = sem("e_id_mm")
        id_s = sem("e_id")
        gi_s = sem("e_gi")
        si_s = sem("e_si")
        fetched = [sem(f"e_fetched{k}") for k in range(RING)]
        w_ld = [sem(f"e_w_ld{k}") for k in range(RING)]
        gt_mm = sem("e_gt_mm")
        gt_s = sem("e_gt")
        gu_mm = sem("e_gu_mm")
        sg_s = sem("e_sg")
        act_s = sem("e_act")
        dn_mm = sem("e_dn_mm")
        y_s = sem("e_y")
        added = sem("e_added")
        final = sem("e_final")

        block = ctx.enter_context(nc.Block())

        def tile_of(i):
            return X[:, i, :] if isinstance(i, int) else X[:, bass.ds(i, 1), :].rearrange("p n d -> p (n d)")

        @block.sync
        def _(sp):
            for dst, src in ((ident, "c_ident"), (names, "c_names"), (ramp, "c_ramp"), (slotno, "c_slotno"),
                             (gate, "w_gate"), (o2n, "old_to_new")):
                sp.dma_start(dst[:, :], dram[src]).then_inc(loaded, 16)
            for part in range(2):
                n = TILES // 2
                sp.dma_start(acc[part * n * P:(part + 1) * n * P, :].rearrange("(n p) d -> p n d", p=P),
                             X[:, part * n:(part + 1) * n, :]).then_inc(acc_out, 16)
            sp.wait_ge(consts, 3)
            sp.dma_start(rows[TOKENS:TOKENS + CAP, :], zrow[:, :]).then_inc(pad_out, 16)
            sp.dma_start(acc[TOKENS:TOKENS + CAP, :], zrow[:, 0:HID]).then_inc(pad_out, 16)

            def load_weights(e, k):
                src_gu = dram["w_gu"][e] if isinstance(e, int) else \
                    dram["w_gu"][bass.ds(e, 1)].rearrange("n p c m -> (n p) c m")
                src_dn = dram["w_dn"][e] if isinstance(e, int) else \
                    dram["w_dn"][bass.ds(e, 1)].rearrange("n p m -> (n p) m")
                after(sp, dn_mm, e - RING + 1)
                sp.sem_inc(held, 1)
                sp.dma_start(wgu[k][:, :, :], src_gu).then_inc(w_ld[k], 16)
                sp.dma_start(wdn[k][:, :], src_dn).then_inc(w_ld[k], 16)

            for e in range(RING):
                load_weights(e, e)
            rows_t = rows[0:TOKENS, :].rearrange("(n p) d -> n p d", p=P)
            with sp.Fori(0, TILES // 2) as t:
                for p in range(2):
                    sp.wait_ge(w_s, 2 * t + p + 1)
                    sp.sem_inc(held, 1)
                    sp.dma_start(rows_t[bass.ds(2 * t + p, 1)].rearrange("n p d -> (n p) d"), hw[p][:, :]
                                 ).then_inc(rows_out[p], 16)
            with sp.Fori(1, NEW // RING) as t:
                for k in range(RING):
                    load_weights(RING * t + k, k)
            sp.wait_ge(added, 16 * NEW)
            sp.dma_start(out, acc[0:TOKENS, :]).then_inc(final, 16)
            sp.wait_ge(final, 16)
            sp.wait_ge(pad_out, 32)
            sp.wait_ge(acc_out, 32)
            for p in range(2):
                sp.wait_ge(rows_out[p], 16 * HT)

        def run_tiles(eng, stage_a, stage_b):
            stage_a(0, 0)
            for i in range(2):
                stage_a(i + 1, (i + 1) % 2)
                stage_b(i, i % 2)
            with eng.Fori(1, TILES // 2 - 1) as t:
                for p in range(2):
                    stage_a(2 * t + p + 1, 1 - p)
                    stage_b(2 * t + p, p)
            stage_a(TILES - 1, 1)
            stage_b(TILES - 2, 0)
            stage_b(TILES - 1, 1)

        @block.tensor
        def _(pe):
            pe.wait_ge(loaded, 16 * 6)
            pe.wait_ge(consts, 5)
            for c in range(2):
                m = nc.tensor.matmul(bT[0][:, c * NEW:(c + 1) * NEW], gate[:, c * P:(c + 1) * P], perm[:, :],
                                     start=True, stop=True)
            m.then_inc(gT_mm, 1)
            pe.wait_ge(gT_s, 1)

            def turn(i, p):
                pe.wait_ge(h_s, i + 1)
                after(pe, hT_s, i - 1)
                for c in range(2):
                    m = nc.tensor.transpose(bT[p][:, c * P:(c + 1) * P], hw[p][:, c * P:(c + 1) * P], ident[:, :])
                m.then_inc(hT_mm, 1)

            def route(i, p):
                pe.wait_ge(hT_s, i + 1)
                after(pe, lg_s, i - 1)
                for c in range(2):
                    m = nc.tensor.matmul(bL[p][:, 0:NEW], hT[p][:, c, :], gT[:, c, :], start=(c == 0), stop=(c == 1))
                m.then_inc(l_mm, 1)

            def turn_chosen(i, p, half):
                pe.wait_ge(chosen_s, i + 1)
                after(pe, queue_s, i - 1)
                nc.tensor.matmul(bC[p][64 * half:64 * half + NEW, 0:P], chosen[p][:, :], identb[:, :],
                                 start=True, stop=True).then_inc(c_mm, 1)

            def step(t, p, half, more=True):
                i = 2 * t + p + half * HT
                if more:
                    turn(i + 1, 1 - p)
                route(i, p)
                turn_chosen(i, p, half)

            turn(0, 0)
            step(0, 0, 0)
            step(0, 1, 0)
            for half in range(2):
                with pe.Fori(1 - half, HT // 2 - half) as t:
                    for p in range(2):
                        step(t, p, half)
            step(HT // 2 - 1, 0, 1)
            step(HT // 2 - 1, 1, 1, more=False)
            pe.wait_ge(idf_s, 3)
            nc.tensor.transpose(bT[0][0:CAP, 0:NEW], idf[:, :], ident[0:NEW, 0:NEW]).then_inc(id_mm, 1)
            pe.wait_ge(id_s, 1)

            def expert(e, k, t):
                p = k % 2
                pe.wait_ge(fetched[k], 16 * (t + 1))
                after(pe, gt_s, e - 1)
                for c in range(2):
                    m = nc.tensor.transpose(bT[p][:, c * CAP:(c + 1) * CAP], G[k][:, c * P:(c + 1) * P],
                                            ident[0:CAP, 0:CAP])
                m.then_inc(gt_mm, 1)

            def expert_up(e, k, t):
                p = k % 2
                pe.wait_ge(w_ld[k], 32 * (t + 1))
                pe.wait_ge(gt_s, e + 1)
                after(pe, act_s, e - 1)
                for s in range(2):
                    for c in range(2):
                        m = nc.tensor.matmul(bL[p][0:INTER, s * CAP:(s + 1) * CAP],
                                             wgu[k][:, c, s * INTER:(s + 1) * INTER], GT[p][:, c, :],
                                             start=(c == 0), stop=(c == 1))
                m.then_inc(gu_mm, 1)

            def expert_down(e, k):
                p = k % 2
                pe.wait_ge(act_s, e + 1)
                after(pe, y_s, e - 1)
                nc.tensor.matmul(bD[p][0:CAP, 0:HID], act_[p][:, :], wdn[k][:, :], start=True, stop=True
                                 ).then_inc(dn_mm, 1)
            def experts_of(t):
                for k in range(RING):
                    e = RING * t + k
                    expert(e, k, t)
                    expert_up(e, k, t)
                    expert_down(e, k)
            experts_of(0)
            with pe.Fori(1, NEW // RING) as t:
                experts_of(t)

        @block.scalar
        def _(act):
            nc.scalar.preload_act_table_set("natural_log_exp_and_others")
            act.wait_ge(loaded, 16 * 6)
            act.wait_ge(consts, 5)
            act.wait_ge(gT_mm, 1)
            nc.scalar.copy(gT[:, :, :].rearrange("p c n -> p (c n)"), bT[0][:, 0:2 * NEW]).then_inc(gT_s, 1)

            def norm(i, p):
                act.wait_ge(stats, 2 * (i + 1))
                nc.scalar.activation(lv[p][:, :], mv[p][:, 1:2], ACT.Ln, bias=eps[:, :]).then_inc(rstd_s, 1)
                act.wait_ge(rstd_s, 2 * i + 1)
                nc.scalar.activation(rstd[p][:, :], lv[p][:, :], ACT.Exp, scale=-0.5).then_inc(rstd_s, 1)

            def route(i, p):
                act.wait_ge(hT_mm, i + 1)
                after(act, l_mm, i - 1)
                nc.scalar.copy(hT[p][:, :, :].rearrange("p c t -> p (c t)"), bT[p][:, 0:2 * P]).then_inc(hT_s, 1)
                act.wait_ge(ntop_s, i + 1)
                after(act, em_s, i - 1)
                nc.scalar.activation(ex[p][:, :], lg[p][:, :], ACT.Exp, bias=ntop[p][:, :]).then_inc(ex_s, 1)

            run_tiles(act, norm, route)

            def gather_turned(e, k):
                p = k % 2
                act.wait_ge(gt_mm, e + 1)
                after(act, gu_mm, e - 1)
                nc.scalar.copy(GT[p][:, :, :].rearrange("p c t -> p (c t)"), bT[p][:, 0:2 * CAP]).then_inc(gt_s, 1)

            def silu(e, k):
                p = k % 2
                act.wait_ge(gu_mm, e + 1)
                after(act, act_s, e - 1)
                nc.scalar.activation(sg[p][:, :], bL[p][0:INTER, 0:CAP], ACT.Silu).then_inc(sg_s, 1)
            def experts_of(t):
                for k in range(RING):
                    gather_turned(RING * t + k, k)
                    silu(RING * t + k, k)
            experts_of(0)
            with act.Fori(1, NEW // RING) as t:
                experts_of(t)

        @block.vector
        def _(dve):
            nc.vector.memset(eps[:, :], LN_EPS).then_inc(consts, 1)
            nc.vector.memset(queue[:, :], 0.0).then_inc(consts, 1)
            nc.vector.memset(zrow[:, :], 0.0).then_inc(consts, 1)
            dve.wait_ge(loaded, 16 * 6)
            nc.vector.tensor_copy(identb[:, :], ident[:, :]).then_inc(consts, 1)
            nc.vector.tensor_copy(o2nf[:, :], o2n[:, :]).then_inc(pick, 1)
            dve.wait_ge(pick, 1)
            nc.vector.tensor_scalar(perm[:, :], names[:, :], o2nf[:, 0:1], None, ALU.is_equal).then_inc(consts, 1)
            dve.wait_ge(consts, 5)

            def norm(i, p):
                after(dve, rstd_s, 2 * (i - 1))
                nc.vector.bn_stats(st[p][:, :], tile_of(i)).then_inc(stats, 1)
                dve.wait_ge(stats, 2 * i + 1)
                dve.sem_inc(held, 1)
                nc.vector.bn_aggr(mv[p][:, :], st[p][:, :]).then_inc(stats, 1)

            def normalise(i, p, before):
                dve.wait_ge(rstd_s, 2 * (i + 1))
                after(dve, hT_mm, i - 1)
                after(dve, rows_out[p], 16 * before)
                nc.vector.tensor_scalar(hw[p][:, 0:HID], tile_of(i), mv[p][:, 0:1], rstd[p][:, 0:1],
                                        ALU.subtract, ALU.mult).then_inc(h_s, 1)

            def choose(i, p):
                dve.wait_ge(l_mm, i + 1)
                after(dve, ex_s, i - 1)
                nc.vector.tensor_copy(lg[p][:, :], bL[p][:, 0:NEW]).then_inc(lg_s, 1)
                dve.wait_ge(lg_s, i + 1)
                dve.sem_inc(held, 1)
                nc.vector.max(top[p][:, :], lg[p][:, :]).then_inc(top_s, 1)
                dve.wait_ge(top_s, i + 1)
                nc.vector.tensor_scalar(ntop[p][:, :], top[p][:, 0:1], -1.0, None, ALU.mult).then_inc(ntop_s, 1)
                nc.vector.match_replace(out=rest[p][:, :], in_to_replace=top[p][:, :], in_values=lg[p][:, :],
                                        imm_value=-3e38).then_inc(rest_s, 1)
                dve.wait_ge(rest_s, i + 1)
                after(dve, c_mm, i - 1)
                nc.vector.tensor_tensor(chosen[p][:, :], rest[p][:, :], lg[p][:, :], ALU.not_equal
                                        ).then_inc(chosen_s, 1)
                dve.wait_ge(ex_s, i + 1)
                dve.wait_ge(chosen_s, i + 1)
                nc.vector.scalar_tensor_tensor(out=em[p][:, :], in0=ex[p][:, :], scalar=1.0, in1=chosen[p][:, :],
                                               op0=ALU.mult, op1=ALU.mult, accum_out=es[p][:, :]).then_inc(em_s, 1)
                dve.wait_ge(em_s, i + 1)
                nc.vector.reciprocal(ei[p][:, :], es[p][:, :]).then_inc(ei_s, 1)
                dve.wait_ge(ei_s, i + 1)
                nc.vector.tensor_scalar(hw[p][:, HID:ROW], em[p][:, :], ei[p][:, 0:1], None, ALU.mult
                                        ).then_inc(w_s, 1)

            def enqueue(i, p, half, col):
                dve.wait_ge(c_mm, i + 1)
                r = 64 * half
                where = bass.ds(col, P)
                nc.vector.tensor_tensor(queue[r:r + NEW, where], bC[p][r:r + NEW, 0:P], ramp[r:r + NEW, where],
                                        ALU.mult).then_inc(queue_s, 1)

            def step(t, p, half, more=True):
                i = 2 * t + p + half * HT
                if more:
                    norm(i + 1, 1 - p)
                    normalise(i + 1, 1 - p, t + p + half * HT // 2)
                choose(i, p)
                enqueue(i, p, half, (2 * t + p) * P)

            norm(0, 0)
            normalise(0, 0, 0)
            step(0, 0, 0)
            step(0, 1, 0)
            for half in range(2):
                with dve.Fori(1 - half, HT // 2 - half) as t:
                    for p in range(2):
                        step(t, p, half)
            step(HT // 2 - 1, 0, 1)
            step(HT // 2 - 1, 1, 1, more=False)
            for r in range(ROUNDS):
                dve.wait_ge(pick, 1 + 2 * r)
                if r == 0:
                    dve.wait_ge(queue_s, TILES)
                nc.vector.max(first1[0:112, r * TOPK:(r + 1) * TOPK], queue[0:112, :]).then_inc(pick, 1)
                dve.wait_ge(pick, 2 + 2 * r)
                nc.vector.match_replace(out=queue[0:112, :], in_to_replace=first1[0:112, r * TOPK:(r + 1) * TOPK],
                                        in_values=queue[0:112, :], imm_value=-1.0).then_inc(pick, 1)
            dve.wait_ge(pick, 1 + 2 * ROUNDS)
            nc.vector.tensor_scalar(none[:, :], first1[0:NEW, :], 0.0, float(HALF), ALU.is_gt, ALU.mult
                                    ).then_inc(pick2, 1)
            nc.vector.tensor_copy(both2[:, CAP:2 * CAP], first1[64:64 + NEW, :]).then_inc(pick2, 1)
            dve.wait_ge(pick2, 2)
            nc.vector.tensor_tensor(both2[:, 0:CAP], first1[0:NEW, :], none[:, :], ALU.add).then_inc(pick2, 1)
            for r in range(ROUNDS):
                dve.wait_ge(pick2, 3 + 2 * r)
                nc.vector.max(first2[:, r * TOPK:(r + 1) * TOPK], both2[:, :]).then_inc(pick2, 1)
                dve.wait_ge(pick2, 4 + 2 * r)
                nc.vector.match_replace(out=both2[:, :], in_to_replace=first2[:, r * TOPK:(r + 1) * TOPK],
                                        in_values=both2[:, :], imm_value=-1.0).then_inc(pick2, 1)
            dve.wait_ge(pick2, 3 + 2 * ROUNDS)
            nc.vector.tensor_scalar(none[:, :], first2[:, :], 0.0, None, ALU.is_le).then_inc(idf_s, 1)
            dve.wait_ge(idf_s, 1)
            nc.vector.tensor_tensor(none[:, :], none[:, :], slotno[:, :], ALU.mult).then_inc(idf_s, 1)
            dve.wait_ge(idf_s, 2)
            nc.vector.scalar_tensor_tensor(out=idf[:, :], in0=none[:, :], scalar=float(TOKENS), in1=first2[:, :],
                                           op0=ALU.add, op1=ALU.subtract).then_inc(idf_s, 1)
            dve.wait_ge(id_mm, 1)
            nc.vector.tensor_copy(index[:, :], bT[0][0:CAP, 0:NEW]).then_inc(id_s, 1)

            def gated(e, k):
                p = k % 2
                dve.wait_ge(sg_s, e + 1)
                after(dve, dn_mm, e - 1)
                nc.vector.tensor_tensor(act_[p][:, :], sg[p][:, :], bL[p][0:INTER, CAP:2 * CAP], ALU.mult
                                        ).then_inc(act_s, 1)

            def weighted(e, k):
                p = k % 2
                dve.wait_ge(dn_mm, e + 1)
                after(dve, added, 16 * (e - 1))
                nc.vector.tensor_scalar(Y[p][:, :], bD[p][0:CAP, 0:HID], G[k][:, bass.ds(e + HID, 1)], None,
                                        ALU.mult).then_inc(y_s, 1)
            def experts_of(t):
                for k in range(RING):
                    gated(RING * t + k, k)
                    weighted(RING * t + k, k)
            experts_of(0)
            with dve.Fori(1, NEW // RING) as t:
                experts_of(t)

        @block.gpsimd
        def _(pool):
            pool.wait_ge(id_s, 1)
            for p in range(2):
                pool.wait_ge(rows_out[p], 16 * HT)
            pool.wait_ge(acc_out, 32)
            pool.wait_ge(pad_out, 32)

            def fetch(e, k):
                after(pool, y_s, e - RING + 1)
                pool.sem_inc(held, 1)
                nc.gpsimd.tensor_copy(gi[k][:, :], index[:, bass.ds(e, 1)]).then_inc(gi_s, 1)
                pool.wait_ge(gi_s, e + 1)
                pool.sem_inc(held, 1)
                nc.gpsimd.indirect_dma_start(G[k][:, :], None, rows, bass.IndirectOffsetOnAxis(ap=gi[k][:, :], axis=0)
                                             ).then_inc(fetched[k], 16)

            def scatter(e, p):
                after(pool, added, 16 * e)
                pool.sem_inc(held, 1)
                nc.gpsimd.tensor_copy(si[p][:, :], index[:, bass.ds(e, 1)]).then_inc(si_s, 1)
                pool.wait_ge(si_s, e + 1)
                pool.wait_ge(y_s, e + 1)
                pool.sem_inc(held, 1)
                nc.gpsimd.indirect_dma_start(acc, bass.IndirectOffsetOnAxis(ap=si[p][:, :], axis=0), Y[p][:, :], None,
                                             compute_op=ALU.add).then_inc(added, 16)
            for e in range(RING - 1):
                fetch(e, e)
            for e in range(RING):
                fetch(e + RING - 1, (e + RING - 1) % RING)
                scatter(e, e % 2)
            with pool.Fori(1, NEW // RING - 1) as t:
                for k in range(RING):
                    fetch(RING * t + k + RING - 1, (k + RING - 1) % RING)
                    scatter(RING * t + k, k % 2)
            for k in range(RING):
                e = NEW - RING + k
                if e + RING - 1 < NEW:
                    fetch(e + RING - 1, (k + RING - 1) % RING)
                scatter(e, k % 2)


def expert_constants():
    return {
        "c_names": np.ascontiguousarray(np.broadcast_to(np.arange(48), (P, 48))).astype(np.float32),
        "c_ramp": np.ascontiguousarray(np.broadcast_to(TOKENS // 2 - np.arange(TOKENS // 2),
                                                       (P, TOKENS // 2))).astype(np.float32),
        "c_slotno": np.ascontiguousarray(np.broadcast_to(np.arange(96), (48, 96))).astype(np.float32),
    }


def build(nc, dram, out):
    with nc.sbuf_tensor("x_residual", [P, TILES, HID], F32) as X:
        for stage, args in ((delta_rule, ()), (banded_attention, ()), (experts, (out,))):
            sems = []
            stage(nc, X, dram, sems, *args)
            nc.clear_and_free_semaphores(sems)
            nc.all_engine_barrier()


def laid_out(v):
    f = np.float32

    def chunks(q, k, v_):
        o = np.zeros((NCH, P) + q.shape[1:], f)
        h = 3 * DK
        o[0, :h], o[1, :h], o[2, :h], o[3, :h] = q[:h], q[h:], k[:h], k[h:]
        o[QKC:] = v_.reshape((3, P) + v_.shape[1:])
        return o

    def rows(a, n=P):
        return np.ascontiguousarray(np.broadcast_to(a, (n, a.shape[-1])))

    def diagonal(w):
        o = np.zeros((P, P), f)
        o[:T, :T] = w
        o[T:, T:] = w
        return o

    def column(b):
        return np.ascontiguousarray(np.concatenate([b, b])[:, None])

    w_in, b_in = v["L0_xattn_w_in"], v["L0_xattn_b_in"]
    w_out = np.zeros((4, 32, 2, T), f)
    w_out[:, :8] = v["L0_xattn_w_out"].T.reshape(2, 4, 8, T).transpose(1, 2, 0, 3)
    gu, dn = v["L0_ffn_gate_up_proj"], v["L0_ffn_down_proj"]
    return {
        "x": np.ascontiguousarray(v["x"].reshape(TOKENS, HID)),
        "w_qkv": np.ascontiguousarray(chunks(v["L0_attn_Wq"], v["L0_attn_Wk"], v["L0_attn_Wv"])
                                      .reshape(NCH * P, HID).T),
        "w_conv": chunks(v["L0_attn_conv_wq"], v["L0_attn_conv_wk"], v["L0_attn_conv_wv"]),
        "w_gab": np.ascontiguousarray(np.concatenate([v["L0_attn_Wg"], v["L0_attn_Wb"], v["L0_attn_Wa"]]).T),
        "w_o": np.ascontiguousarray(v["L0_attn_Wo"].T),
        "norm_w": rows(np.tile(v["L0_attn_norm_w"], HEADS)),
        "A_log": rows(v["L0_attn_A_log"]),
        "dt_bias": rows(v["L0_attn_dt_bias"]),
        "ctx": np.ascontiguousarray(v["ctx_2048"].reshape(TILES, P, HID)),
        "w_in": np.stack([diagonal(w_in[T * n:T * n + T].T) for n in range(3)]),
        "w_out": np.ascontiguousarray(w_out.reshape(P, 2, T)),
        "w_ct": diagonal(v["L0_xattn_w_ct"]),
        "b_q": column(b_in[:T]),
        "b_k": column(b_in[T:2 * T]),
        "b_v": rows(np.tile(b_in[2 * T:], 4)),
        "b_out": column(v["L0_xattn_b_out"]),
        "b_ct": column(v["L0_xattn_b_ct"]),
        "w_gate": np.ascontiguousarray(v["L0_ffn_gate_weight"]),
        "old_to_new": np.ascontiguousarray(v["L0_ffn_old_to_new"][:, None]),
        "w_gu": np.ascontiguousarray(gu.transpose(0, 2, 1).reshape(48, 2, P, 192).transpose(0, 2, 1, 3)),
        "w_dn": np.ascontiguousarray(dn.transpose(0, 2, 1)),
    }


def kernel(**inputs):
    import concourse.bacc as bacc
    from concourse.bass_utils import run_bass_kernel_spmd

    arrays = laid_out({k: np.asarray(a) for k, a in inputs.items()})
    arrays.update(constants())
    arrays.update(attention_constants())
    arrays.update(expert_constants())
    nc = bacc.Bacc("TRN2", target_bir_lowering=False, num_devices=1)
    dram = {k: nc.dram_tensor("in_" + k, a.shape, mybir.dt.from_np(a.dtype), kind="ExternalInput").ap()
            for k, a in arrays.items()}
    out = nc.dram_tensor("out_dram", (TOKENS, HID), F32, kind="ExternalOutput").ap()
    build(nc, dram, out)
    r = run_bass_kernel_spmd(nc, [{"in_" + k: a for k, a in arrays.items()}], core_ids=[0])
    return np.asarray(r.results[0]["out_dram"]).reshape(64, 64, 256)
```

```python
from contextlib import ExitStack

import numpy as np

import concourse.bass as bass
from concourse import mybir

F32 = mybir.dt.float32
BF16 = mybir.dt.bfloat16
I32 = mybir.dt.int32
ALU = mybir.AluOpType
ACT = mybir.ActivationFunctionType
AX = mybir.AxisListType

P = 128
TOKENS, HID = 4096, 256
TILES = TOKENS // P
T = 64
HEADS, DK, DV = 6, 32, 64
NCH = 7
QKC = 4
VD = HEADS * DV
LEVELS = 6
LN_EPS = 1e-5
L2_EPS = 4e-6
RMS_EPS = 4 * DK * 1e-5


def after(eng, sem, n):
    if not isinstance(n, int) or n > 0:
        eng.wait_ge(sem, n)


def delta_rule(nc, X, dram, sems):
    with ExitStack() as ctx:
        def sb(name, shape, dt=F32):
            return ctx.enter_context(nc.sbuf_tensor(name, shape, dt))

        def bank(name):
            return ctx.enter_context(nc.psum_tensor(name, [P, 512], F32))

        def sem(name):
            sems.append(nc.alloc_semaphore(name))
            return sems[-1]

        ident = sb("a_ident", [P, P])
        upto = sb("a_upto", [P, P])
        past = sb("a_past", [P, P])
        level = sb("a_level", [P, LEVELS, P])
        heads32 = sb("a_heads32", [P, P])
        hmask = sb("a_hmask", [P, 3])
        wqkv = sb("a_wqkv", [P, 2, NCH * P])
        wgab = sb("a_wgab", [P, 2, VD + 2 * HEADS])
        wo = sb("a_wo", [P, 3, HID])
        cw = sb("a_cw", [P, NCH, 4])
        nwh = sb("a_nwh", [P, VD])
        alog = sb("a_alog", [P, HEADS])
        dtb = sb("a_dtb", [P, HEADS])
        nega = sb("a_nega", [P, HEADS])
        ea = sb("a_ea", [P, HEADS])

        st = sb("a_st", [P, 6])
        mv = sb("a_mv", [P, 2])
        lv = sb("a_lv", [P, 1])
        rstd = sb("a_rstd", [P, 1])
        xn = sb("a_xn", [P, HID])
        xT = sb("a_xT", [P, 2, P])
        zp = sb("a_zp", [P, NCH, 2, T + 3])
        y = sb("a_y", [P, NCH, 2, T])
        th = sb("a_th", [P, NCH * P])
        sy = sb("a_sy", [P, NCH * P])
        sq = sb("a_sq", [P, QKC * P])
        rs = sb("a_rs", [P, QKC * P])
        rl = sb("a_rl", [P, QKC * P])
        tg = sb("a_tg", [P, VD + HEADS])
        gs = sb("a_gs", [P, VD])
        zz = sb("a_zz", [P, HEADS])
        az = sb("a_az", [P, HEADS])
        ez = sb("a_ez", [P, HEADS])
        lz = sb("a_lz", [P, HEADS])
        sp_ = sb("a_sp", [P, HEADS])
        qk = [sb(f"a_qk{p}", [P, QKC, P]) for p in range(2)]
        V = [sb(f"a_V{p}", [P, VD]) for p in range(2)]
        g = [sb(f"a_g{p}", [P, HEADS]) for p in range(2)]
        beta = [sb(f"a_beta{p}", [P, HEADS]) for p in range(2)]
        gw = [sb(f"a_gw{p}", [P, VD]) for p in range(2)]

        H3 = 3 * P
        rD = sb("a_rD", [P, 2, 3, P])
        E = sb("a_E", [P, 2, 3, P])
        Eb = sb("a_Eb", [P, 2, 3, P])
        EA = sb("a_EA", [P, 2, 3, P])
        kM = sb("a_kM", [P, HEADS, P])
        AT = sb("a_AT", [P, 2, 3, P])
        LT = sb("a_LT", [P, 2, 3, P])
        LM = sb("a_LM", [P, LEVELS, 2, 3, P])
        Xi = sb("a_Xi", [P, 2, 3, P])
        Ti = sb("a_Ti", [P, 2, 3, P])
        Pi = sb("a_Pi", [P, 2, 3, P])
        W = sb("a_W", [P, 2, 4, DV])
        Pv = sb("a_Pv", [P, 2, 4, DV])
        U = sb("a_U", [P, 2, 4, DV])
        oq = sb("a_oq", [P, 2, 3, DV])
        oss = sb("a_oss", [P, 2, 3])
        orl = sb("a_orl", [P, 2, 3])
        orr = sb("a_orr", [P, 2, 3])
        o1 = sb("a_o1", [P, 2, 3, DV])
        o2 = sb("a_o2", [P, VD])
        oT = sb("a_oT", [P, VD])

        a0, a1 = bank("a_b0"), bank("a_b1")
        bP = [bank(f"a_bP{f}") for f in range(2)]
        bA = [bank(f"a_bA{f}") for f in range(2)]
        bB = [bank(f"a_bB{f}") for f in range(2)]

        eps_ln, eps_l2, eps_rms = (sb(n, [P, 1]) for n in ("a_eps_ln", "a_eps_l2", "a_eps_rms"))
        ident3 = ident[:, :].unsqueeze(1).to_broadcast([P, 3, P])
        loaded = sem("a_loaded")
        x_first = sem("a_x_first")
        x_rest = sem("a_x_rest")
        zeroed = sem("a_zeroed")
        held = sem("a_held")
        decay_e = sem("a_decay_e")
        decay_c = sem("a_decay_c")
        stats = sem("a_stats")
        rstd_s = sem("a_rstd")
        xn_s = sem("a_xn")
        xt_mm = sem("a_xt_mm")
        xt_s = sem("a_xt")
        z_mm = [sem(f"a_z_mm{k}") for k in range(2)]
        z_s = [sem(f"a_z{k}") for k in range(2)]
        conv = sem("a_conv")
        tanh_s = sem("a_tanh")
        silu_s = sem("a_silu")
        sq_s = sem("a_sq")
        ss_mm = sem("a_ss_mm")
        rs_s = sem("a_rs")
        qk_s = sem("a_qk")
        v_mm = sem("a_v_mm")
        v_s = sem("a_v")
        gate_mm = sem("a_gate_mm")
        gate_th = sem("a_gate_th")
        gate_v = sem("a_gate_v")
        spl = sem("a_spl")
        gw_s = sem("a_gw")
        g_s = sem("a_g")

        ez_s = sem("a_ez")
        gs_s = sem("a_gs")
        L0_s = [sem(f"a_L0{f}") for f in range(2)]
        rD_s = [sem(f"a_rD{f}") for f in range(2)]
        d_mm = [sem(f"a_d_mm{f}") for f in range(2)]
        E_s = [sem(f"a_E{f}") for f in range(2)]
        Eb_s = [sem(f"a_Eb{f}") for f in range(2)]
        EA_s = [sem(f"a_EA{f}") for f in range(2)]
        kM_s = sem("a_kM")
        kk_mm = [sem(f"a_kk_mm{f}") for f in range(2)]
        qk_mm = [sem(f"a_qk_mm{f}") for f in range(2)]
        AT_s = [sem(f"a_AT{f}") for f in range(2)]
        LT_s = [sem(f"a_LT{f}") for f in range(2)]
        LM_s = [sem(f"a_LM{f}") for f in range(2)]
        X1_s = [sem(f"a_X1{f}") for f in range(2)]
        t1_mm = [sem(f"a_t1_mm{f}") for f in range(2)]
        T1_s = [sem(f"a_T1{f}") for f in range(2)]
        P_mm = [sem(f"a_P_mm{f}") for f in range(2)]
        P_s = [sem(f"a_P{f}") for f in range(2)]
        TU_mm = [sem(f"a_TU_mm{f}") for f in range(2)]
        XU_mm = [sem(f"a_XU_mm{f}") for f in range(2)]
        T_s = [sem(f"a_T{f}") for f in range(2)]
        X_s = [sem(f"a_X{f}") for f in range(2)]
        W_mm = [sem(f"a_W_mm{f}") for f in range(2)]
        W_s = [sem(f"a_W{f}") for f in range(2)]
        Pv_mm = [sem(f"a_Pv_mm{f}") for f in range(2)]
        Pv_s = [sem(f"a_Pv{f}") for f in range(2)]
        U_mm = [sem(f"a_U_mm{f}") for f in range(2)]
        U_s = [sem(f"a_U{f}") for f in range(2)]
        O_mm = [sem(f"a_O_mm{f}") for f in range(2)]
        oq_s = [sem(f"a_oq{f}") for f in range(2)]
        oss_s = sem("a_oss")
        orr_s = sem("a_orr")
        o1_s = [sem(f"a_o1{f}") for f in range(2)]
        o2_s = sem("a_o2")
        oT_mm = sem("a_oT_mm")
        oT_s = sem("a_oT")
        out_mm = sem("a_out_mm")
        x_s = sem("a_x")

        block = ctx.enter_context(nc.Block())
        NL = LEVELS - 2

        @block.sync
        def _(sp):
            def load_x(first, end, done):
                sp.dma_start(X[:, first:end, :],
                             dram["x"][first * P:end * P, :].rearrange("(n p) d -> p n d", p=P)).then_inc(done, 16)

            load_x(0, 2, x_first)
            for dst, src in ((ident, "c_ident"), (upto, "c_upto"), (past, "c_past"), (heads32, "c_heads32"),
                             (hmask, "c_hmask"), (nwh, "norm_w"), (alog, "A_log"), (dtb, "dt_bias")):
                sp.dma_start(dst[:, :], dram[src]).then_inc(loaded, 16)
            sp.dma_start(level[:, :, :], dram["c_level"].rearrange("l p t -> p l t")).then_inc(loaded, 16)
            sp.dma_start(wqkv[:, :, :], dram["w_qkv"].rearrange("(c p) n -> p c n", p=P)).then_inc(loaded, 16)
            sp.dma_start(wgab[:, :, :], dram["w_gab"].rearrange("(c p) n -> p c n", p=P)).then_inc(loaded, 16)
            sp.dma_start(wo[:, :, :], dram["w_o"].rearrange("(c p) n -> p c n", p=P)).then_inc(loaded, 16)
            sp.dma_start(cw[:, :, :], dram["w_conv"].rearrange("c p j -> p c j")).then_inc(loaded, 16)
            load_x(2, TILES, x_rest)

        N_LOADS = 13

        def run_tiles(eng, both):
            both(0, 0, True, True)
            both(1, 1, True, True)
            with eng.Fori(1, TILES // 2 - 1) as t:
                both(2 * t, 0, True, True)
                both(2 * t + 1, 1, True, True)
            both(TILES - 2, 0, True, False)
            both(TILES - 1, 1, False, False)

        @block.tensor
        def _(pe):
            pe.wait_ge(loaded, 16 * N_LOADS)

            def A(i, p=0):
                def x_turn():
                    pe.wait_ge(xn_s, i + 1)
                    after(pe, gate_v, i)
                    for c in range(2):
                        m = nc.tensor.transpose(a0[:, c * P:(c + 1) * P], xn[:, c * P:(c + 1) * P], ident[:, :])
                    m.then_inc(xt_mm, 1)

                def project(first):
                    pe.wait_ge(xt_s, i + 1)
                    after(pe, E_s[0 if first else 1], i)
                    for ch in range(4) if first else range(4, NCH):
                        o = (a0 if ch < 4 else a1)[:, (ch % 4) * P:(ch % 4 + 1) * P]
                        for c in range(2):
                            m = nc.tensor.matmul(o, wqkv[:, c, ch * P:(ch + 1) * P], xT[:, c, :],
                                                 start=(c == 0), stop=(c == 1))
                        if ch in (3, 6):
                            m.then_inc(z_mm[ch // 4], 1)

                def gates():
                    pe.wait_ge(z_s[0], i + 1)
                    for c in range(2):
                        m = nc.tensor.matmul(a0[:, 0:VD + 2 * HEADS], xT[:, c, :], wgab[:, c, :],
                                             start=(c == 0), stop=(c == 1))
                    m.then_inc(gate_mm, 1)

                def squares():
                    pe.wait_ge(sq_s, i + 1)
                    pe.wait_ge(v_s, i + 1)
                    nc.tensor.matmul(a1[:, :], heads32[:, :], sq[:, :], start=True, stop=True).then_inc(ss_mm, 1)

                def v_turn():
                    pe.wait_ge(silu_s, i + 1)
                    pe.wait_ge(z_s[1], i + 1)
                    for c in range(3):
                        m = nc.tensor.transpose(a1[:, c * P:(c + 1) * P], sy[:, (QKC + c) * P:(QKC + c + 1) * P],
                                                ident[:, :])
                    m.then_inc(v_mm, 1)

                def decay(more):
                    if more:
                        pe.wait_ge(xt_s, i + 2)
                    for f in range(2):
                        pe.wait_ge(rD_s[f], i + 1)
                        if f == 1:
                            pe.wait_ge(rs_s, 2 * i + 1)
                        nc.tensor.matmul((a0, a1)[f][:, 0:H3], past[:, :],
                                         rD[:, f, :, :].rearrange("p h t -> p (h t)"),
                                         start=True, stop=True).then_inc(d_mm[f], 1)
                return x_turn, project, gates, squares, v_turn, decay

            def B(i, p):
                def scores():
                    pe.wait_ge(kM_s, HEADS * (i + 1))
                    after(pe, oT_s, i)
                    for side, banks, done in ((2, bA, kk_mm), (0, bB, qk_mm)):
                        if side == 0:
                            after(pe, x_s, i)
                        for f in range(2):
                            for h in range(3):
                                m = nc.tensor.matmul(banks[f][:, h * P:(h + 1) * P], kM[:, 3 * f + h, :],
                                                     qk[p][:, side + f, :], start=True, stop=True)
                            m.then_inc(done[f], 1)

                def first():
                    for f in range(2):
                        pe.wait_ge(X1_s[f], i + 1)
                        after(pe, o1_s[f], i)
                        for h in range(3):
                            m = nc.tensor.transpose(bP[f][:, h * P:(h + 1) * P], Xi[:, f, h, :], ident[:, :])
                        m.then_inc(t1_mm[f], 1)

                def level_p(l):
                    def go():
                        for f in range(2):
                            if l == 1:
                                pe.wait_ge(T1_s[f], i + 1)
                            else:
                                pe.wait_ge(T_s[f], (NL - 1) * i + l - 1)
                                pe.wait_ge(P_s[f], NL * i + l - 1)
                            pe.wait_ge(LM_s[f], (LEVELS - 1) * i + l)
                            for h in range(3):
                                m = nc.tensor.matmul(bP[f][:, h * P:(h + 1) * P], LM[:, l, f, h, :],
                                                     Ti[:, f, h, :], start=True, stop=True)
                            m.then_inc(P_mm[f], 1)
                    return go

                def level_u(l):
                    def go():
                        for f in range(2):
                            pe.wait_ge(P_s[f], NL * i + l)
                            if l == 1:
                                pe.wait_ge(AT_s[f], i + 1)
                                pe.wait_ge(LT_s[f], i + 1)
                            else:
                                pe.wait_ge(X_s[f], NL * i + l - 1)
                                pe.wait_ge(T_s[f], (NL - 1) * i + l - 1)
                            if l < NL:
                                for h in range(3):
                                    m = nc.tensor.matmul(bA[f][:, h * P:(h + 1) * P], Xi[:, f, h, :],
                                                         Pi[:, f, h, :], start=True, stop=True)
                                m.then_inc(TU_mm[f], 1)
                            for h in range(3):
                                m = nc.tensor.matmul(bB[f][:, h * P:(h + 1) * P], Pi[:, f, h, :],
                                                     Xi[:, f, h, :], start=True, stop=True)
                            m.then_inc(XU_mm[f], 1)
                    return go

                def vcols(buf, f, h):
                    return buf[:, f, h:h + 2, :].rearrange("p h d -> p (h d)")

                def solve_w():
                    for f in range(2):
                        pe.wait_ge(X_s[f], NL * (i + 1))
                        pe.wait_ge(P_s[f], NL * (i + 1))
                        pe.wait_ge(v_s, i + 1)
                        for h in range(3):
                            c = min((3 * f + h) * DV, VD - P)
                            m = nc.tensor.matmul(bP[f][:, h * P:(h + 1) * P], Xi[:, f, h, :],
                                                 V[p][:, c:c + P], start=True, stop=True)
                        m.then_inc(W_mm[f], 1)

                def solve_p():
                    for f in range(2):
                        pe.wait_ge(W_s[f], i + 1)
                        pe.wait_ge(LM_s[f], (LEVELS - 1) * (i + 1))
                        pe.wait_ge(T_s[f], (NL - 1) * (i + 1))
                        for h in range(3):
                            m = nc.tensor.matmul(bA[f][:, h * P:(h + 1) * P], LM[:, LEVELS - 1, f, h, :],
                                                 vcols(W, f, h), start=True, stop=True)
                        m.then_inc(Pv_mm[f], 1)

                def solve_u():
                    for f in range(2):
                        pe.wait_ge(Pv_s[f], i + 1)
                        for h in range(3):
                            m = nc.tensor.matmul(bB[f][:, h * P:(h + 1) * P], Xi[:, f, h, :],
                                                 vcols(Pv, f, h), start=True, stop=True)
                        m.then_inc(U_mm[f], 1)

                def outputs():
                    for f in range(2):
                        pe.wait_ge(U_s[f], i + 1)
                        for h in range(3):
                            m = nc.tensor.matmul(bP[f][:, h * P:(h + 1) * P], AT[:, f, h, :],
                                                 vcols(U, f, h), start=True, stop=True)
                        m.then_inc(O_mm[f], 1)

                def o_turn():
                    pe.wait_ge(o2_s, i + 1)
                    for c in range(3):
                        m = nc.tensor.transpose(bA[0][:, c * P:(c + 1) * P], o2[:, c * P:(c + 1) * P], ident[:, :])
                    m.then_inc(oT_mm, 1)

                def o_project():
                    pe.wait_ge(oT_s, i + 1)
                    for c in range(3):
                        m = nc.tensor.matmul(bB[0][:, 0:HID], oT[:, c * P:(c + 1) * P], wo[:, c, :],
                                             start=(c == 0), stop=(c == 2))
                    m.then_inc(out_mm, 1)
                return scores, first, level_p, level_u, solve_w, solve_p, solve_u, outputs, o_turn, o_project

            x_turn, project, gates, squares, v_turn, decay = A(0)
            x_turn()
            project(True)
            project(False)
            gates()
            A(1)[0]()
            v_turn()
            squares()
            decay(True)

            def both(i, p, ahead, further):
                scores, first, level_p, level_u, solve_w, solve_p, solve_u, outputs, o_turn, o_project = B(i, p)
                if ahead:
                    _, project, gates, squares, v_turn, decay = A(i + 1)
                scores()
                if ahead:
                    project(True)
                first()
                if ahead:
                    project(False)
                level_p(1)()
                level_u(1)()
                if ahead:
                    gates()
                for l in range(2, LEVELS - 1):
                    level_p(l)()
                    level_u(l)()
                solve_w()
                solve_p()
                if ahead:
                    v_turn()
                if further:
                    A(i + 2)[0]()
                solve_u()
                outputs()
                if ahead:
                    squares()
                    decay(further)
                o_turn()
                o_project()
            run_tiles(pe, both)

        @block.scalar
        def _(act):
            act.wait_ge(loaded, 16 * N_LOADS)
            nc.scalar.activation(ea[:, :], alog[:, :], ACT.Exp).then_inc(decay_e, 1)

            def A(i, p=0):
                def norm_rstd():
                    act.wait_ge(stats, 2 * (i + 1))
                    after(act, xn_s, i)
                    nc.scalar.activation(lv[:, :], mv[:, 1:2], ACT.Ln, bias=eps_ln[:, :]).then_inc(rstd_s, 1)
                    act.wait_ge(rstd_s, 2 * i + 1)
                    nc.scalar.activation(rstd[:, :], lv[:, :], ACT.Exp, scale=-0.5).then_inc(rstd_s, 1)

                def x_copy():
                    act.wait_ge(xt_mm, i + 1)
                    after(act, gate_mm, i)
                    nc.scalar.copy(xT[:, :, :].rearrange("p c t -> p (c t)"), a0[:, 0:HID]).then_inc(xt_s, 1)

                def z_copy():
                    for k, (c0, c1) in enumerate(((0, 4), (4, 7))):
                        act.wait_ge(z_mm[k], i + 1)
                        after(act, conv, 4 * NCH * i)
                        nc.scalar.copy(zp[:, c0:c1, :, 3:3 + T].rearrange("p c b t -> p (c b) t"),
                                       (a0 if k == 0 else a1)[:, 0:(c1 - c0) * P].rearrange("p (c t) -> p c t", t=T)
                                       ).then_inc(z_s[k], 1)

                def gate_tanh():
                    act.wait_ge(gate_mm, i + 1)
                    after(act, spl, 3 * i)
                    nc.scalar.activation(tg[:, :], a0[:, 0:VD + HEADS], ACT.Tanh, scale=0.5).then_inc(gate_th, 1)

                def conv_tanh():
                    act.wait_ge(conv, 4 * NCH * (i + 1))
                    after(act, silu_s, i)
                    nc.scalar.activation(th[:, :], y[:, :, :, :].rearrange("p c b t -> p (c b t)"), ACT.Tanh,
                                         scale=0.5).then_inc(tanh_s, 1)
                    nc.scalar.preload_act_table_set("natural_log_exp_and_others")

                def squares():
                    act.wait_ge(silu_s, i + 1)
                    after(act, ss_mm, i)
                    nc.scalar.activation(sq[:, :], sy[:, 0:QKC * P], ACT.Square).then_inc(sq_s, 1)

                def softplus():
                    act.wait_ge(spl, 3 * i + 2)
                    nc.scalar.activation(ez[:, :], az[:, :], ACT.Exp, scale=-1.0).then_inc(ez_s, 1)
                    act.wait_ge(ez_s, 2 * i + 1)
                    nc.scalar.activation(lz[:, :], ez[:, :], ACT.Ln, bias=1.0).then_inc(ez_s, 1)

                def inv_norms():
                    act.wait_ge(ss_mm, i + 1)
                    after(act, qk_s, i)
                    nc.scalar.activation(rl[:, :], a1[:, :], ACT.Ln, bias=eps_l2[:, :]).then_inc(rs_s, 1)
                    act.wait_ge(rs_s, 2 * i + 1)
                    nc.scalar.activation(rs[:, :], rl[:, :], ACT.Exp, scale=-0.5).then_inc(rs_s, 1)

                def v_copy():
                    act.wait_ge(v_mm, i + 1)
                    for f in range(2):
                        after(act, W_mm[f], i - 1)
                    nc.scalar.copy(V[p][:, :], a1[:, 0:VD]).then_inc(v_s, 1)

                def decay():
                    for f in range(2):
                        act.wait_ge(d_mm[f], i + 1)
                        after(act, Eb_s[f], i)
                        nc.scalar.activation(E[:, f, :, :].rearrange("p h t -> p (h t)"), (a0, a1)[f][:, 0:H3],
                                             ACT.Exp).then_inc(E_s[f], 1)
                return (norm_rstd, x_copy), z_copy, gate_tanh, conv_tanh, softplus, squares, inv_norms, v_copy, decay

            def B(i, p):
                def t_copy():
                    for f in range(2):
                        act.wait_ge(t1_mm[f], i + 1)
                        nc.scalar.copy(Ti[:, f, :, :].rearrange("p h t -> p (h t)"), bP[f][:, 0:H3]
                                       ).then_inc(T1_s[f], 1)

                def p_copy(l):
                    def go():
                        for f in range(2):
                            act.wait_ge(P_mm[f], NL * i + l)
                            after(act, XU_mm[f], NL * i + l - 1)
                            nc.scalar.copy(Pi[:, f, :, :].rearrange("p h t -> p (h t)"), bP[f][:, 0:H3]
                                           ).then_inc(P_s[f], 1)
                    return go

                def diag(b, f):
                    return b[f][:, 0:H3].rearrange("p (h d) -> p h d", d=P)

                def w_copy():
                    for f in range(2):
                        act.wait_ge(W_mm[f], i + 1)
                        for h in range(3):
                            c = 3 * f + h
                            o = c * DV - min(c * DV, VD - P)
                            m = nc.scalar.copy(W[:, f, h, :], bP[f][:, h * P + o:h * P + o + DV])
                        m.then_inc(W_s[f], 1)

                def pv_copy():
                    for f in range(2):
                        act.wait_ge(Pv_mm[f], i + 1)
                        nc.scalar.copy(Pv[:, f, 0:3, :], diag(bA, f)[:, :, 0:DV]).then_inc(Pv_s[f], 1)

                def o_squares():
                    for f in range(2):
                        act.wait_ge(O_mm[f], i + 1)
                        after(act, oss_s, i)
                        nc.scalar.activation(oq[:, f, :, :], diag(bP, f)[:, :, 0:DV], ACT.Square).then_inc(oq_s[f], 1)

                def o_rms():
                    act.wait_ge(oss_s, i + 1)
                    nc.scalar.activation(orl[:, :, :], oss[:, :, :], ACT.Ln, scale=1.0 / DV,
                                         bias=eps_rms[:, :]).then_inc(orr_s, 1)
                    act.wait_ge(orr_s, 2 * i + 1)
                    after(act, o1_s[1], i)
                    nc.scalar.activation(orr[:, :, :], orl[:, :, :], ACT.Exp, scale=-0.5).then_inc(orr_s, 1)

                def o_copy():
                    act.wait_ge(oT_mm, i + 1)
                    nc.scalar.copy(oT[:, :], bA[0][:, 0:VD]).then_inc(oT_s, 1)
                return t_copy, p_copy, w_copy, pv_copy, o_squares, o_rms, o_copy

            act.wait_ge(zeroed, 8)
            (norm_rstd, x_copy), z_copy, gate_tanh, conv_tanh, softplus, squares, inv_norms, v_copy, decay = A(0)
            norm_rstd()
            x_copy()
            z_copy()
            gate_tanh()
            conv_tanh()
            softplus()
            A(1)[0][0]()
            squares()
            A(1)[0][1]()
            v_copy()
            inv_norms()
            decay()

            def both(i, p, ahead, further):
                t_copy, p_copy, w_copy, pv_copy, o_squares, o_rms, o_copy = B(i, p)
                if ahead:
                    _, z_copy, gate_tanh, conv_tanh, softplus, squares, inv_norms, v_copy, decay = A(i + 1, 1 - p)
                if further:
                    norm_rstd, x_copy = A(i + 2)[0]
                t_copy()
                if ahead:
                    z_copy()
                p_copy(1)()
                p_copy(2)()
                if ahead:
                    gate_tanh()
                p_copy(3)()
                p_copy(4)()
                if ahead:
                    conv_tanh()
                    softplus()
                if further:
                    norm_rstd()
                w_copy()
                if ahead:
                    squares()
                pv_copy()
                if ahead:
                    v_copy()
                if further:
                    x_copy()
                o_squares()
                o_rms()
                if ahead:
                    inv_norms()
                    decay()
                o_copy()
            run_tiles(act, both)

        @block.vector
        def _(dve):
            nc.vector.memset(zp[:, :, :, :], 0.0).then_inc(zeroed, 1)
            nc.vector.memset(W[:, :, :, :], 0.0).then_inc(zeroed, 1)
            nc.vector.memset(Pv[:, :, :, :], 0.0).then_inc(zeroed, 1)
            nc.vector.memset(U[:, :, :, :], 0.0).then_inc(zeroed, 1)
            nc.vector.memset(eps_ln[:, :], LN_EPS).then_inc(zeroed, 1)
            nc.vector.memset(eps_l2[:, :], L2_EPS).then_inc(zeroed, 1)
            nc.vector.memset(eps_rms[:, :], RMS_EPS).then_inc(zeroed, 1)
            dve.wait_ge(loaded, 16 * N_LOADS)
            dve.wait_ge(decay_e, 1)
            nc.vector.tensor_scalar(nega[:, :], ea[:, :], -1.0, None, ALU.mult).then_inc(decay_c, 1)
            nc.vector.tensor_scalar(nwh[:, :], nwh[:, :], 0.5, None, ALU.mult).then_inc(zeroed, 1)
            dve.wait_ge(zeroed, 8)
            dve.wait_ge(decay_c, 1)

            def A(i, p=0):
                xi = X[:, i, :] if isinstance(i, int) else X[:, bass.ds(i, 1), :].rearrange("p n d -> p (n d)")

                def norm():
                    after(dve, rstd_s, 2 * i)
                    nc.vector.bn_stats(st[:, :], xi).then_inc(stats, 1)
                    dve.wait_ge(stats, 2 * i + 1)
                    dve.sem_inc(held, 1)
                    nc.vector.bn_aggr(mv[:, :], st[:, :]).then_inc(stats, 1)

                def normalise():
                    dve.wait_ge(rstd_s, 2 * (i + 1))
                    after(dve, xt_mm, i)
                    nc.vector.tensor_scalar(xn[:, :], xi, mv[:, 0:1], rstd[:, 0:1], ALU.subtract, ALU.mult
                                            ).then_inc(xn_s, 1)

                def convolve(j, part):
                    if j == 0:
                        dve.wait_ge(z_s[part], i + 1)
                        after(dve, silu_s, i)
                        after(dve, tanh_s, i)
                    for c in range(4) if part == 0 else range(4, NCH):
                        if j == 0:
                            nc.vector.tensor_scalar(y[:, c, :, :], zp[:, c, :, 3:3 + T], cw[:, c, 3:4], None,
                                                    ALU.mult).then_inc(conv, 1)
                        else:
                            dve.wait_ge(conv, 4 * NCH * i + (j - 1) * NCH + c + 1)
                            nc.vector.scalar_tensor_tensor(out=y[:, c, :, :], in0=zp[:, c, :, 3 - j:3 - j + T],
                                                           scalar=cw[:, c, 3 - j:4 - j], in1=y[:, c, :, :],
                                                           op0=ALU.mult, op1=ALU.add).then_inc(conv, 1)

                def gates():
                    dve.wait_ge(gate_th, i + 1)
                    after(dve, gw_s, i)
                    nc.vector.scalar_tensor_tensor(out=gs[:, :], in0=tg[:, 0:VD], scalar=1.0, in1=a0[:, 0:VD],
                                                   op0=ALU.add, op1=ALU.mult).then_inc(gs_s, 1)
                    nc.vector.tensor_tensor(zz[:, :], a0[:, VD + HEADS:VD + 2 * HEADS], dtb[:, :], ALU.add
                                            ).then_inc(gate_v, 1)
                    for f in range(2):
                        after(dve, Eb_s[f], i - 1)
                    nc.vector.tensor_scalar(beta[p][:, :], tg[:, VD:VD + HEADS], 0.5, 0.5, ALU.mult, ALU.add
                                            ).then_inc(spl, 1)
                    dve.wait_ge(gate_v, i + 1)
                    nc.vector.scalar_tensor_tensor(out=az[:, :], in0=zz[:, :], scalar=-1.0, in1=zz[:, :],
                                                   op0=ALU.mult, op1=ALU.max).then_inc(spl, 1)

                def softplus():
                    dve.wait_ge(ez_s, 2 * (i + 1))
                    nc.vector.scalar_tensor_tensor(out=sp_[:, :], in0=zz[:, :], scalar=0.0, in1=lz[:, :],
                                                   op0=ALU.max, op1=ALU.add).then_inc(spl, 1)
                    dve.wait_ge(spl, 3 * (i + 1))
                    nc.vector.tensor_tensor(g[p][:, :], sp_[:, :], nega[:, :], ALU.mult).then_inc(g_s, 1)

                def silus():
                    dve.wait_ge(tanh_s, i + 1)
                    after(dve, v_mm, i)
                    after(dve, qk_s, i)
                    nc.vector.scalar_tensor_tensor(out=sy[:, :], in0=th[:, :], scalar=1.0,
                                                   in1=y[:, :, :, :].rearrange("p c b t -> p (c b t)"),
                                                   op0=ALU.add, op1=ALU.mult).then_inc(silu_s, 1)

                def norm_qk():
                    dve.wait_ge(rs_s, 2 * (i + 1))
                    for f in range(2):
                        after(dve, kk_mm[f], i - 1)
                        after(dve, qk_mm[f], i - 1)
                    nc.vector.tensor_tensor(qk[p][:, :, :].rearrange("p c t -> p (c t)"), sy[:, 0:QKC * P], rs[:, :],
                                            ALU.mult).then_inc(qk_s, 1)

                def k_heads():
                    dve.wait_ge(qk_s, i + 1)
                    for f in range(2):
                        after(dve, kk_mm[f], i)
                        after(dve, qk_mm[f], i)
                    for h in range(HEADS):
                        nc.vector.tensor_scalar(kM[:, h, :], qk[p][:, 2 + h // 3, :], hmask[:, h % 3:h % 3 + 1], None,
                                                ALU.mult).then_inc(kM_s, 1)

                return (norm, normalise), convolve, gates, softplus, silus, norm_qk, k_heads

            def B(i, p):
                xi = X[:, i, :] if isinstance(i, int) else X[:, bass.ds(i, 1), :].rearrange("p n d -> p (n d)")

                def weigh():
                    for f in range(2):
                        dve.wait_ge(kk_mm[f], i + 1)
                        dve.wait_ge(EA_s[f], i + 1)
                        after(dve, LM_s[f], (LEVELS - 1) * i)
                        nc.vector.tensor_tensor(LT[:, f, :, :].rearrange("p h t -> p (h t)"), bA[f][:, 0:H3],
                                                EA[:, f, :, :].rearrange("p h t -> p (h t)"), ALU.mult
                                                ).then_inc(LT_s[f], 1)
                        dve.wait_ge(LT_s[f], i + 1)
                        after(dve, XU_mm[f], NL * i)
                        after(dve, U_mm[f], i)
                        nc.vector.tensor_tensor(LM[:, 0, f, :, :], LT[:, f, :, :],
                                                level[:, 0:1, :].to_broadcast([P, 3, P]), ALU.mult
                                                ).then_inc(L0_s[f], 1)
                        dve.wait_ge(L0_s[f], i + 1)
                        nc.vector.tensor_tensor(Xi[:, f, :, :], ident3, LM[:, 0, f, :, :], ALU.subtract
                                                ).then_inc(X1_s[f], 1)
                    for f in range(2):
                        dve.wait_ge(qk_mm[f], i + 1)
                        after(dve, O_mm[f], i)
                        nc.vector.tensor_tensor(AT[:, f, :, :].rearrange("p h t -> p (h t)"), bB[f][:, 0:H3],
                                                EA[:, f, :, :].rearrange("p h t -> p (h t)"), ALU.mult
                                                ).then_inc(AT_s[f], 1)

                def level_u(l, between):
                    def go():
                        for f in range(2):
                            if l < NL:
                                dve.wait_ge(TU_mm[f], (NL - 1) * i + l)
                                if l == 1:
                                    dve.wait_ge(T1_s[f], i + 1)
                                else:
                                    dve.wait_ge(T_s[f], (NL - 1) * i + l - 1)
                                nc.vector.tensor_tensor(Ti[:, f, :, :].rearrange("p h t -> p (h t)"),
                                                        Ti[:, f, :, :].rearrange("p h t -> p (h t)"),
                                                        bA[f][:, 0:H3], ALU.subtract).then_inc(T_s[f], 1)
                            dve.wait_ge(XU_mm[f], NL * i + l)
                            if l == 1:
                                dve.wait_ge(X1_s[f], i + 1)
                            else:
                                dve.wait_ge(X_s[f], NL * i + l - 1)
                            nc.vector.tensor_tensor(Xi[:, f, :, :].rearrange("p h t -> p (h t)"),
                                                    Xi[:, f, :, :].rearrange("p h t -> p (h t)"), bB[f][:, 0:H3],
                                                    ALU.subtract).then_inc(X_s[f], 1)
                            between(f)
                    return go

                def u_sub():
                    for f in range(2):
                        dve.wait_ge(U_mm[f], i + 1)
                        dve.wait_ge(W_s[f], i + 1)
                        after(dve, O_mm[f], i)
                        nc.vector.tensor_tensor(U[:, f, 0:3, :], W[:, f, 0:3, :],
                                                bB[f][:, 0:H3].rearrange("p (h d) -> p h d", d=P)[:, :, 0:DV],
                                                ALU.subtract).then_inc(U_s[f], 1)

                def o_sums():
                    for f in range(2):
                        dve.wait_ge(oq_s[f], i + 1)
                    after(dve, orr_s, 2 * i)
                    nc.vector.tensor_reduce(oss[:, :, :].rearrange("p f h -> p (f h)"),
                                            oq[:, :, :, :].rearrange("p f h d -> p (f h) d"), AX.X, ALU.add
                                            ).then_inc(oss_s, 1)

                def o_norm():
                    for f in range(2):
                        after(dve, o2_s, i)
                        if f == 0:
                            dve.wait_ge(orr_s, 2 * (i + 1))
                        m = nc.vector.tensor_tensor(o1[:, f, :, :],
                                                    bP[f][:, 0:H3].rearrange("p (h d) -> p h d", d=P)[:, :, 0:DV],
                                                    orr[:, f, :].unsqueeze(2).to_broadcast([P, 3, DV]), ALU.mult)
                        m.then_inc(o1_s[f], 1)
                    for f in range(2):
                        dve.wait_ge(o1_s[f], i + 1)
                    after(dve, oT_mm, i)
                    dve.wait_ge(gw_s, i + 1)
                    nc.vector.tensor_tensor(o2[:, :], o1[:, :, :, :].rearrange("p f h d -> p (f h d)"), gw[p][:, :],
                                            ALU.mult).then_inc(o2_s, 1)

                def add():
                    dve.wait_ge(out_mm, i + 1)
                    nc.vector.tensor_tensor(xi, xi, bB[0][:, 0:HID], ALU.add).then_inc(x_s, 1)
                return weigh, level_u, u_sub, o_sums, o_norm, add

            (norm, normalise), convolve, gates, softplus, silus, norm_qk, k_heads = A(0)
            dve.wait_ge(x_first, 16)
            norm()
            normalise()
            for j in range(4):
                for part in range(2):
                    convolve(j, part)
            gates()
            softplus()
            A(1)[0][0]()
            A(1)[0][1]()
            silus()
            norm_qk()
            k_heads()

            def both(i, p, ahead, further):
                weigh, level_u, u_sub, o_sums, o_norm, add = B(i, p)
                if ahead:
                    _, convolve, gates, softplus, silus, norm_qk, k_heads = A(i + 1, 1 - p)
                weigh()

                def beside(l):
                    def go(f):
                        if ahead and l < 4:
                            convolve(l, f)
                            if (l, f) == (2, 1):
                                gates()
                        if further and (l, f) == (3, 1):
                            A(i + 2)[0][0]()
                    return go
                beside(0)(0)
                beside(0)(1)
                for l in range(1, LEVELS - 1):
                    level_u(l, beside(l))()
                if ahead:
                    silus()
                    softplus()
                if further:
                    A(i + 2)[0][1]()
                u_sub()
                o_sums()
                o_norm()
                if ahead:
                    norm_qk()
                    k_heads()
                add()
            dve.wait_ge(x_rest, 16)
            run_tiles(dve, both)

        @block.gpsimd
        def _(pool):
            pool.wait_ge(loaded, 16 * N_LOADS)
            pool.wait_ge(zeroed, 8)

            def gate_weight(i, p):
                pool.wait_ge(gs_s, i + 1)
                after(pool, o2_s, i - 1)
                nc.gpsimd.tensor_tensor(gw[p][:, :], gs[:, :], nwh[:, :], ALU.mult).then_inc(gw_s, 1)

            def decays(i, p):
                pool.wait_ge(g_s, i + 1)
                for f in range(2):
                    after(pool, d_mm[f], i)
                    nc.gpsimd.tensor_tensor(rD[:, f, :, :], upto[:, :].unsqueeze(1).to_broadcast([P, 3, P]),
                                            g[p][:, 3 * f:3 * f + 3].unsqueeze(2).to_broadcast([P, 3, P]), ALU.mult
                                            ).then_inc(rD_s[f], 1)

            def weights(i, p):
                for f in range(2):
                    pool.wait_ge(E_s[f], i + 1)
                    after(pool, EA_s[f], i)
                    nc.gpsimd.tensor_tensor(Eb[:, f, :, :], E[:, f, :, :],
                                            beta[p][:, 3 * f:3 * f + 3].unsqueeze(2).to_broadcast([P, 3, P]),
                                            ALU.mult).then_inc(Eb_s[f], 1)
                    pool.wait_ge(Eb_s[f], i + 1)
                    after(pool, LT_s[f], i)
                    after(pool, AT_s[f], i)
                    nc.gpsimd.tensor_tensor(EA[:, f, :, :], Eb[:, f, :, :],
                                            upto[:, :].unsqueeze(1).to_broadcast([P, 3, P]), ALU.mult
                                            ).then_inc(EA_s[f], 1)

            def levels(i, p):
                for l in range(1, LEVELS):
                    for f in range(2):
                        pool.wait_ge(LT_s[f], i + 1)
                        after(pool, Pv_mm[f], i)
                        nc.gpsimd.tensor_tensor(LM[:, l, f, :, :], LT[:, f, :, :],
                                                level[:, l:l + 1, :].to_broadcast([P, 3, P]), ALU.mult
                                                ).then_inc(LM_s[f], 1)

            gate_weight(0, 0)
            decays(0, 0)
            weights(0, 0)

            def both(i, p, ahead, further):
                levels(i, p)
                if ahead:
                    gate_weight(i + 1, 1 - p)
                    decays(i + 1, 1 - p)
                    weights(i + 1, 1 - p)
            run_tiles(pool, both)


def constants():
    r, c = np.arange(P)[:, None], np.arange(P)[None, :]
    same = r // T == c // T
    level = [same & (r // (2 * m) == c // (2 * m)) & (r // m % 2 == 0) & (c // m % 2 == 1)
             for m in (1 << l for l in range(LEVELS))]
    f = np.float32
    return {
        "c_ident": np.eye(P, dtype=f),
        "c_upto": (same & (r <= c)).astype(f),
        "c_past": (same & (r > c)).astype(f),
        "c_level": np.stack(level).astype(f),
        "c_heads32": (r // DK == c // DK).astype(f),
        "c_hmask": np.stack([(np.arange(P) // DK == h) for h in range(3)], 1).astype(f),
    }


def banded_attention(nc, X, dram, sems):
    with ExitStack() as ctx:
        def sb(name, shape, dt=F32):
            return ctx.enter_context(nc.sbuf_tensor(name, shape, dt))

        def bank(name, dt=F32):
            return ctx.enter_context(nc.psum_tensor(name, [P, 2048 // (4 if dt == F32 else 2)], dt))

        def sem(name):
            sems.append(nc.alloc_semaphore(name))
            return sems[-1]

        UNITS = 2 * TILES
        NH, D8 = 8, 8
        KEYS = 256
        SPAN = 192
        ROWS = 9 * D8
        SUB = 8

        ident32 = sb("b_ident32", [P, P])
        band32 = sb("b_band32", [P, 2, SPAN])
        identb = sb("b_identb", [P, P], BF16)
        band = sb("b_band", [P, 2, SPAN], BF16)
        seld = sb("b_seld", [P, P])
        wq = sb("b_wq", [P, P])
        wk = sb("b_wk", [P, P])
        wv = sb("b_wv", [P, P])
        wout = sb("b_wout", [P, 2, T])
        wct = sb("b_wct", [P, P])
        bq = sb("b_bq", [P, 1])
        bk = sb("b_bk", [P, 1])
        bv = sb("b_bv", [P, 2 * P])
        bo = sb("b_bo", [P, 1])
        bct = sb("b_bct", [P, 1])
        ctxs = [sb(f"b_ctx{p}", [P, HID]) for p in range(2)]
        eps = sb("b_eps", [P, 1])

        st = sb("b_st", [P, 6])
        mv = sb("b_mv", [P, 2])
        lv = sb("b_lv", [P, 1])
        rstd = sb("b_rstd", [P, 1])
        xn = sb("b_xn", [P, HID])
        r0 = sb("b_r0", [P, 2 * KEYS])
        r1 = sb("b_r1", [P, 2 * KEYS])
        r2 = sb("b_r2", [P, 2 * KEYS])
        parts = sb("b_parts", [P, 2, 3, KEYS], BF16)
        QS = [sb(f"b_QS{p}", [P, 2 * NH, KEYS], BF16) for p in range(2)]
        KS = [sb(f"b_KS{p}", [P, 2 * NH, KEYS], BF16) for p in range(2)]
        VA = [sb(f"b_VA{p}", [P, 2, 2 * NH, 32]) for p in range(2)]
        nm = sb("b_nm", [P, 2, NH])
        n1 = sb("b_n1", [P, 2, NH])
        n2 = sb("b_n2", [P, 2, NH])
        NPt = sb("b_NP", [P, 2, 3, NH], BF16)
        MT = sb("b_MT", [3 * NH, KEYS], BF16)
        PT = [sb(f"b_PT{k}", [P, 2, SPAN]) for k in range(4)]
        Os = sb("b_Os", [P, 2 * KEYS])
        lD = sb("b_lD", [P, 2 * KEYS])
        rDn = sb("b_rDn", [P, 2 * KEYS])
        On = sb("b_On", [P, 2 * KEYS])
        yr = sb("b_yr", [P, HID])
        yy = sb("b_yy", [P, HID])

        bM = [bank(f"b_bM{k}") for k in range(2)]
        bS = [bank(f"b_bS{k}") for k in range(2)]
        bO = bank("b_bO")
        m0 = bank("b_m0")
        m1 = bank("b_m1")
        m2 = bank("b_m2")
        m2h = m2[:, :].bitcast(BF16)

        scratch = [nc.dram_tensor(f"b_scratch{p}", [2, 3, P, KEYS], BF16, kind="Internal").ap() for p in range(2)]

        loaded = sem("b_loaded")
        ctx_ld = [sem(f"b_ctx_ld{p}") for p in range(2)]
        zeroed = sem("b_zeroed")
        zeroed_k = sem("b_zeroed_k")
        held = sem("b_held")
        stats = sem("b_stats")
        rstd_s = sem("b_rstd")
        xn_s = sem("b_xn")
        qk_mm = sem("b_qk_mm")
        v_mm = sem("b_v_mm")
        r0_s = sem("b_r0")
        part_s = [sem(f"b_part{j}") for j in range(3)]
        r1_s = sem("b_r1")
        r2_s = sem("b_r2")
        v_s = sem("b_v")
        put = [sem(f"b_put{p}") for p in range(2)]
        got = [sem(f"b_got{p}") for p in range(2)]
        max_mm = sem("b_max_mm")
        max_s = sem("b_max")
        np_s = sem("b_np")
        mt_mm = sem("b_mt_mm")
        mt_s = sem("b_mt")
        mrow = [sem(f"b_mrow{b}") for b in range(2)]
        s_mm = sem("b_s_mm")
        exp_s = sem("b_exp")
        pv_mm = sem("b_pv_mm")
        o_s = sem("b_o")
        den_mm = sem("b_den_mm")
        ln_s = sem("b_ln")
        on_s = sem("b_on")
        out_mm = sem("b_out_mm")
        relu_s = sem("b_relu")
        y_s = sem("b_y")
        ct_mm = sem("b_ct_mm")
        x_s = sem("b_x")


        ZEROED = 9
        block = ctx.enter_context(nc.Block())

        def run_slots(slot):
            for k in range(4):
                slot(0, k)
            with slot.engine.Fori(1, UNITS // 4 - 1) as t:
                for k in range(4):
                    slot(t, k)
            for k in range(4):
                slot(UNITS // 4 - 1, k)

        def is_first(t, k):
            return isinstance(t, int) and t == 0 and k == 0

        def has_next_unit(t, k):
            return not (isinstance(t, int) and 4 * t + k == UNITS - 1)

        def has_tile(t, k, ahead):
            return not isinstance(t, int) or 2 * t + k // 2 + ahead < TILES

        @block.sync
        def _(sp):
            for dst, src in ((ident32, "c_ident"), (seld, "c_seld"), (wct, "w_ct"),
                             (bq, "b_q"), (bk, "b_k"), (bv, "b_v"), (bo, "b_out"), (bct, "b_ct")):
                sp.dma_start(dst[:, :], dram[src]).then_inc(loaded, 16)
            for dst, src in ((band32, "c_band"), (wout, "w_out")):
                sp.dma_start(dst[:, :, :], dram[src]).then_inc(loaded, 16)
            for n, dst in enumerate((wq, wk, wv)):
                sp.dma_start(dst[:, :], dram["w_in"][n]).then_inc(loaded, 16)

            def stack(i, p, half):
                after(sp, s_mm, 2 * SUB * (i - 1))
                sp.sem_inc(held, 1)
                sp.wait_ge(part_s[2], i + 1)
                sp.sem_inc(held, 1)
                sp.dma_start(scratch[p].rearrange("w j c t -> c w j t"), parts[:, :, :, :]).then_inc(put[p], 16)
                sp.wait_ge(put[p], 16 * (half + 1))
                q, k = (scratch[p][w].rearrange("j (d g) t -> j d (g t)", d=D8) for w in range(2))
                sp.dma_start(QS[p][0:ROWS, :, :].rearrange("r g t -> r (g t)"),
                             q.rearrange("a d n -> (a d) n").unsqueeze(0)
                             .to_broadcast([3, 3 * D8, 2 * NH * KEYS])).then_inc(got[p], 16)
                for m in range(3):
                    r = m * 3 * D8
                    sp.dma_start(KS[p][r:r + 3 * D8, :, :].rearrange("r g t -> r (g t)"),
                                 k[m:m + 1].to_broadcast([3, D8, 2 * NH * KEYS])).then_inc(got[p], 16)

            def load_ctx(i, p):
                rows = dram["ctx"][i] if isinstance(i, int) else \
                    dram["ctx"][bass.ds(i, 1)].rearrange("n p d -> (n p) d")
                after(sp, y_s, i - 1)
                sp.sem_inc(held, 1)
                sp.dma_start(ctxs[p][:, :], rows).then_inc(ctx_ld[p], 16)

            def max_rows(u, b, p):
                sp.wait_ge(mt_s, u + 1)
                for a in range(3):
                    sp.dma_start(QS[p][ROWS + a:ROWS + a + 1, b * NH:(b + 1) * NH, :],
                                 MT[a * NH:(a + 1) * NH, :]).then_inc(mrow[b], 16)

            sp.wait_ge(zeroed, ZEROED)
            sp.wait_ge(zeroed_k, 2)
            load_ctx(0, 0)
            stack(0, 0, 0)
            max_rows(0, 0, 0)

            def slot(t, k):
                u, i, b, p = 4 * t + k, 2 * t + k // 2, k % 2, k // 2
                if b == 0 and has_tile(t, k, 1):
                    stack(i + 1, 1 - p, t + p)
                if has_next_unit(t, k):
                    max_rows(u + 1, 1 - b, p if b == 0 else 1 - p)
                if b == 1 and has_tile(t, k, 1):
                    load_ctx(i + 1, 1 - p)
            slot.engine = sp
            run_slots(slot)

        @block.tensor
        def _(pe):
            pe.wait_ge(loaded, 16 * 13)
            pe.wait_ge(zeroed, ZEROED)
            pe.wait_ge(zeroed_k, 2)

            def project_qk(i):
                pe.wait_ge(xn_s, i + 1)
                after(pe, ln_s, 2 * (2 * i - 4) + 1)
                after(pe, r0_s, 2 * i)
                for n, w in enumerate((wq, wk)):
                    m = nc.tensor.matmul(m0[:, n * KEYS:(n + 1) * KEYS], w[:, :], xn[:, :], start=True, stop=True)
                m.then_inc(qk_mm, 1)

            def project_v(i):
                after(pe, relu_s, 2 * i - 3)
                after(pe, v_s, i)
                for c in range(2):
                    m = nc.tensor.matmul(m1[:, c * P:(c + 1) * P], xn[:, c * P:(c + 1) * P], wv[:, :],
                                         start=True, stop=True)
                m.then_inc(v_mm, 1)

            def maximum(u, b, p, n):
                hp, qt = n // 2, n % 2
                after(pe, max_s, SUB * u + n - 1)
                o = bM[n % 2]
                nc.tensor.matmul(o[:, 0:2 * SPAN].rearrange("p (h k) -> p h k", h=2), identb[:, :],
                                 band[:, qt:qt + 1, :].to_broadcast([P, 2, SPAN]),
                                 start=True, stop=False, skip_group_check=True)
                for h in range(2):
                    g = b * NH + 2 * hp + h
                    m = nc.tensor.matmul(o[:, h * SPAN:(h + 1) * SPAN], QS[p][0:ROWS, g, qt * P:(qt + 1) * P],
                                         KS[p][0:ROWS, g, qt * T:qt * T + SPAN],
                                         start=False, stop=True, skip_group_check=True)
                m.then_inc(max_mm, 1)

            def turn_max(u):
                pe.wait_ge(np_s, 5 * (u + 1))
                after(pe, mt_s, u)
                for c in range(2):
                    m = nc.tensor.transpose(m2h[0:3 * NH, c * P:(c + 1) * P],
                                            NPt[:, c, :, :].rearrange("p j h -> p (j h)"), identb[:, :])
                m.then_inc(mt_mm, 1)

            def score(u, b, p, n):
                hp, kt = n // 2, n % 2
                after(pe, exp_s, SUB * u + n - 1)
                o = bS[n % 2]
                nc.tensor.matmul(o[:, 0:2 * SPAN].rearrange("p (h k) -> p h k", h=2), identb[:, :],
                                 band[:, kt:kt + 1, :].to_broadcast([P, 2, SPAN]),
                                 start=True, stop=False, skip_group_check=True)
                for h in range(2):
                    g = b * NH + 2 * hp + h
                    m = nc.tensor.matmul(o[:, h * SPAN:(h + 1) * SPAN], KS[p][:, g, kt * P:(kt + 1) * P],
                                         QS[p][:, g, kt * T:kt * T + SPAN],
                                         start=False, stop=True, skip_group_check=True)
                m.then_inc(s_mm, 1)

            def weigh(u, b, p, n):
                hp, kt = n // 2, n % 2
                pe.wait_ge(exp_s, SUB * u + n + 1)
                if n == 0:
                    after(pe, o_s, u)
                for h in range(2):
                    g = 2 * hp + h
                    r, c = 32 * (g % 4), (g // 4) * KEYS + kt * T
                    m = nc.tensor.matmul(bO[r:r + 32, c:c + SPAN], VA[p][:, kt, b * NH + g, :],
                                         PT[n % 4][:, h, :], start=(kt == 0), stop=(kt == 1),
                                         skip_group_check=True, tile_position=(0, r))
                m.then_inc(pv_mm, 1)

            def sums(u):
                pe.wait_ge(o_s, u + 1)
                nc.tensor.matmul(m0[:, :], seld[:, :], Os[:, :], start=True, stop=True).then_inc(den_mm, 1)

            def out_project(u, b):
                pe.wait_ge(on_s, u + 1)
                for g in range(2):
                    m = nc.tensor.matmul(m1[b * T:(b + 1) * T, 0:KEYS], wout[:, g, :], On[:, g * KEYS:(g + 1) * KEYS],
                                         start=(g == 0), stop=(g == 1))
                m.then_inc(out_mm, 1)

            def combine(i):
                pe.wait_ge(y_s, i + 1)
                nc.tensor.matmul(m2[:, 0:KEYS], wct[:, :], yy[:, :], start=True, stop=True).then_inc(ct_mm, 1)

            def slot(t, k):
                u, i, b, p = 4 * t + k, 2 * t + k // 2, k % 2, k // 2
                first = is_first(t, k)
                for n in range(SUB + 2):
                    if n == 1 and b == 1 and (not isinstance(t, int) or i >= 1):
                        pe.wait_ge(mt_s, u + 1)
                        combine(i - 1)
                    if n == 2 and not first:
                        if b == 0:
                            pe.wait_ge(r0_s, 2 * (i + 2) if has_tile(t, k, 1) else 2 * TILES)
                        else:
                            after(pe, ln_s, 2 * (u - 1))
                        sums(u - 1)
                    if n == 6 and has_next_unit(t, k):
                        if b == 1 and (not isinstance(t, int) or i >= 1):
                            pe.wait_ge(x_s, i)
                        turn_max(u + 1)
                    if n == 5 and b == 1 and has_tile(t, k, 2):
                        project_qk(i + 2)
                    if n == 7 and not first:
                        if b == 0:
                            pe.wait_ge(v_s, i + 2 if has_tile(t, k, 1) else TILES)
                        else:
                            after(pe, relu_s, u - 1)
                        out_project(u - 1, 1 - b)
                    if n <= 3 and has_next_unit(t, k):
                        if n == 0 and b == 1:
                            pe.wait_ge(got[1 - p], 16 * 4 * (t + p + 1))
                        for m in range(2 * n, 2 * n + 2):
                            maximum(u + 1, 1 - b, p if b == 0 else 1 - p, m)
                    if n < SUB:
                        if n == 0:
                            pe.wait_ge(mrow[b], 16 * 3 * (i + 1))
                            pe.wait_ge(v_s, i + 1)
                        score(u, b, p, n)
                    if n == 9 and b == 1 and has_tile(t, k, 2):
                        project_v(i + 2)
                    if n >= 2:
                        weigh(u, b, p, n - 2)

            project_qk(0)
            project_v(0)
            pe.wait_ge(got[0], 16 * 4)
            for m in range(SUB):
                maximum(0, 0, 0, m)
            turn_max(0)
            project_qk(1)
            project_v(1)
            slot.engine = pe
            run_slots(slot)
            last = UNITS - 1
            pe.wait_ge(ln_s, 2 * last)
            sums(last)
            pe.wait_ge(relu_s, last)
            out_project(last, 1)
            combine(TILES - 1)

        @block.scalar
        def _(act):
            nc.scalar.preload_act_table_set("natural_log_exp_and_others")
            act.wait_ge(loaded, 16 * 13)
            act.wait_ge(zeroed, ZEROED)

            def norm(i):
                act.wait_ge(stats, 2 * (i + 1))
                nc.scalar.activation(lv[:, :], mv[:, 1:2], ACT.Ln, bias=eps[:, :]).then_inc(rstd_s, 1)
                act.wait_ge(rstd_s, 2 * i + 1)
                nc.scalar.activation(rstd[:, :], lv[:, :], ACT.Exp, scale=-0.5).then_inc(rstd_s, 1)

            def part(i, j):
                src, ready = ((r0, r0_s), (r1, r1_s), (r2, r2_s))[j]
                act.wait_ge(ready, (2 if j == 0 else 1) * (i + 1))
                nc.scalar.copy(parts[:, :, j, :], src[:, :].rearrange("p (w t) -> p w t", w=2)).then_inc(part_s[j], 1)

            def exps(u, n):
                act.wait_ge(s_mm, SUB * u + n + 1)
                after(act, pv_mm, SUB * u + n - 3)
                nc.scalar.activation(PT[n % 4][:, :, :].rearrange("p h t -> p (h t)"), bS[n % 2][:, 0:2 * SPAN],
                                     ACT.Exp).then_inc(exp_s, 1)

            def inverse_sums(u):
                act.wait_ge(den_mm, u + 1)
                after(act, on_s, u)
                nc.scalar.activation(lD[:, :], m0[:, :], ACT.Ln).then_inc(ln_s, 1)
                act.wait_ge(ln_s, 2 * u + 1)
                nc.scalar.activation(rDn[:, :], lD[:, :], ACT.Exp, scale=-1.0).then_inc(ln_s, 1)

            def relu(u, b, i):
                act.wait_ge(out_mm, u + 1)
                after(act, y_s, i)
                nc.scalar.activation(yr[b * T:(b + 1) * T, :], m1[b * T:(b + 1) * T, 0:KEYS], ACT.Relu,
                                     bias=bo[b * T:(b + 1) * T, :]).then_inc(relu_s, 1)

            def turned(u):
                act.wait_ge(mt_mm, u + 1)
                nc.scalar.copy(MT[:, :], m2h[0:3 * NH, 0:KEYS]).then_inc(mt_s, 1)

            def slot(t, k):
                u, i, b, p = 4 * t + k, 2 * t + k // 2, k % 2, k // 2
                first = is_first(t, k)
                for n in range(SUB):
                    if n == 7 and not first:
                        relu(u - 1, 1 - b, i - 1 if b == 0 else i)
                    exps(u, n)
                    if n == 0 and b == 0 and has_tile(t, k, 1):
                        part(i + 1, 2)
                    if n == 2 and not first:
                        inverse_sums(u - 1)
                    if n == 5 and has_next_unit(t, k):
                        act.wait_ge(mrow[b], 16 * 3 * (i + 1))
                        turned(u + 1)
                    if n == 6 and b == 1 and has_tile(t, k, 2):
                        act.wait_ge(put[1 - p], 16 * (t + p + 1))
                        part(i + 2, 0)
                if b == 0 and has_tile(t, k, 2):
                    norm(i + 2)
                if b == 1 and has_tile(t, k, 2):
                    part(i + 2, 1)

            norm(0)
            for j in range(3):
                part(0, j)
            norm(1)
            turned(0)
            act.wait_ge(put[0], 16)
            part(1, 0)
            part(1, 1)
            slot.engine = act
            run_slots(slot)
            inverse_sums(UNITS - 1)
            relu(UNITS - 1, 1, TILES - 1)

        @block.vector
        def _(dve):
            for p in range(2):
                nc.vector.memset(QS[p][64:P, :, :], 0.0).then_inc(zeroed, 1)
                nc.vector.memset(VA[p][:, :, :, :], 0.0).then_inc(zeroed, 1)
                dve.wait_ge(zeroed, 3 * p + 2)
                nc.vector.memset(VA[p][:, :, :, D8:D8 + 1], 1.0).then_inc(zeroed, 1)
            nc.vector.memset(eps[:, :], LN_EPS).then_inc(zeroed, 1)
            dve.wait_ge(loaded, 16 * 13)
            nc.vector.tensor_copy(identb[:, :], ident32[:, :]).then_inc(zeroed, 1)
            nc.vector.tensor_copy(band[:, :, :], band32[:, :, :]).then_inc(zeroed, 1)
            dve.wait_ge(zeroed, ZEROED)

            def tile_of(i):
                return X[:, i, :] if isinstance(i, int) else X[:, bass.ds(i, 1), :].rearrange("p n d -> p (n d)")

            def norm(i):
                nc.vector.bn_stats(st[:, :], tile_of(i)).then_inc(stats, 1)
                dve.wait_ge(stats, 2 * i + 1)
                dve.sem_inc(held, 1)
                nc.vector.bn_aggr(mv[:, :], st[:, :]).then_inc(stats, 1)

            def normalise(i):
                dve.wait_ge(rstd_s, 2 * (i + 1))
                after(dve, v_mm, i)
                nc.vector.tensor_scalar(xn[:, :], tile_of(i), mv[:, 0:1], rstd[:, 0:1], ALU.subtract, ALU.mult
                                        ).then_inc(xn_s, 1)

            def take_qk(i):
                dve.wait_ge(qk_mm, i + 1)
                after(dve, r1_s, i)
                after(dve, part_s[0], i)
                nc.vector.tensor_scalar(r0[:, 0:KEYS], m0[:, 0:KEYS], bq[:, 0:1], float(D8) ** -0.5,
                                        ALU.add, ALU.mult).then_inc(r0_s, 1)
                nc.vector.tensor_scalar(r0[:, KEYS:2 * KEYS], m0[:, KEYS:2 * KEYS], bk[:, 0:1], None,
                                        ALU.add).then_inc(r0_s, 1)

            def take_v(i, p):
                dve.wait_ge(v_mm, i + 1)
                after(dve, pv_mm, 2 * SUB * (i - 1))
                nc.vector.tensor_tensor(VA[p][:, :, :, 0:D8].rearrange("p c g d -> p (c g) d"),
                                        m1[:, 0:2 * P].rearrange("p (c d) -> p c d", d=D8),
                                        bv[:, :].rearrange("p (c d) -> p c d", d=D8), ALU.add).then_inc(v_s, 1)

            def maximum(u, n):
                dve.wait_ge(max_mm, SUB * u + n + 1)
                if n == 0:
                    after(dve, np_s, 5 * u)
                hp, qt = n // 2, n % 2
                nc.vector.tensor_reduce(nm[:, qt, 2 * hp:2 * hp + 2],
                                        bM[n % 2][:, 0:2 * SPAN].rearrange("p (h k) -> p h k", h=2),
                                        AX.X, ALU.max, negate=True).then_inc(max_s, 1)

            def take_o(u):
                dve.wait_ge(pv_mm, SUB * (u + 1))
                after(dve, den_mm, u)
                after(dve, on_s, u)
                nc.vector.tensor_copy(Os[:, :], bO[:, :]).then_inc(o_s, 1)

            def divide(u):
                dve.wait_ge(ln_s, 2 * (u + 1))
                after(dve, out_mm, u)
                nc.vector.tensor_tensor(On[:, :], Os[:, :], rDn[:, :], ALU.mult).then_inc(on_s, 1)

            def add(i):
                dve.wait_ge(ct_mm, i + 1)
                nc.vector.scalar_tensor_tensor(out=tile_of(i), in0=m2[:, 0:KEYS], scalar=bct[:, 0:1], in1=tile_of(i),
                                               op0=ALU.add, op1=ALU.add).then_inc(x_s, 1)

            def slot(t, k):
                u, i, b, p = 4 * t + k, 2 * t + k // 2, k % 2, k // 2
                first = is_first(t, k)
                if b == 0 and has_tile(t, k, 1):
                    take_v(i + 1, 1 - p)
                if has_next_unit(t, k):
                    for n in range(6):
                        maximum(u + 1, n)
                if b == 1 and (not isinstance(t, int) or i >= 1):
                    add(i - 1)
                if has_next_unit(t, k):
                    for n in range(6, SUB):
                        maximum(u + 1, n)
                if not first:
                    divide(u - 1)
                if b == 0 and has_tile(t, k, 2):
                    norm(i + 2)
                if b == 1 and has_tile(t, k, 2):
                    take_qk(i + 2)
                take_o(u)
                if b == 0 and has_tile(t, k, 2):
                    normalise(i + 2)

            norm(0)
            normalise(0)
            take_qk(0)
            take_v(0, 0)
            norm(1)
            normalise(1)
            for n in range(SUB):
                maximum(0, n)
            take_qk(1)
            slot.engine = dve
            run_slots(slot)
            divide(UNITS - 1)
            add(TILES - 1)

        @block.gpsimd
        def _(pool):
            for p in range(2):
                nc.gpsimd.memset(KS[p][64:P, :, :], 1.0).then_inc(zeroed_k, 1)
            pool.wait_ge(zeroed, ZEROED)

            def rest(i, j):
                src, dst, done = ((r0, r1, r1_s), (r1, r2, r2_s))[j]
                pool.wait_ge(part_s[j], i + 1)
                after(pool, part_s[j + 1], i)
                nc.gpsimd.tensor_tensor(dst[:, :].rearrange("p (w t) -> p w t", w=2),
                                        src[:, :].rearrange("p (w t) -> p w t", w=2), parts[:, :, j, :],
                                        ALU.subtract).then_inc(done, 1)

            def split_max(u):
                pool.wait_ge(max_s, SUB * (u + 1))
                after(pool, mt_mm, u)
                pool.sem_inc(held, 1)
                s = 5 * u
                nc.gpsimd.tensor_copy(NPt[:, :, 0, :], nm[:, :, :]).then_inc(np_s, 1)
                pool.wait_ge(np_s, s + 1)
                nc.gpsimd.tensor_tensor(n1[:, :, :], nm[:, :, :], NPt[:, :, 0, :], ALU.subtract).then_inc(np_s, 1)
                pool.wait_ge(np_s, s + 2)
                pool.sem_inc(held, 1)
                nc.gpsimd.tensor_copy(NPt[:, :, 1, :], n1[:, :, :]).then_inc(np_s, 1)
                pool.wait_ge(np_s, s + 3)
                nc.gpsimd.tensor_tensor(n2[:, :, :], n1[:, :, :], NPt[:, :, 1, :], ALU.subtract).then_inc(np_s, 1)
                pool.wait_ge(np_s, s + 4)
                pool.sem_inc(held, 1)
                nc.gpsimd.tensor_copy(NPt[:, :, 2, :], n2[:, :, :]).then_inc(np_s, 1)

            def times_ctx(i, p, half):
                pool.wait_ge(relu_s, 2 * (i + 1))
                pool.wait_ge(ctx_ld[p], 16 * (half + 1))
                after(pool, ct_mm, i)
                nc.gpsimd.tensor_tensor(yy[:, :], yr[:, :], ctxs[p][:, :], ALU.mult).then_inc(y_s, 1)

            def slot(t, k):
                u, i, b, p = 4 * t + k, 2 * t + k // 2, k % 2, k // 2
                if has_next_unit(t, k):
                    split_max(u + 1)
                if b == 1 and has_tile(t, k, 2):
                    rest(i + 2, 0)
                    rest(i + 2, 1)
                if b == 0 and (not isinstance(t, int) or i >= 1):
                    times_ctx(i - 1, 1 - p, t - 1 + p)

            rest(0, 0)
            rest(0, 1)
            split_max(0)
            rest(1, 0)
            rest(1, 1)
            slot.engine = pool
            run_slots(slot)
            times_ctx(TILES - 1, 1, TILES // 2 - 1)


def attention_constants():
    r = np.arange(P)[:, None]
    c = np.arange(192)[None, :]
    masks = []
    for half in range(2):
        query, key = half * P + r, half * 64 + c
        masks.append(np.where(np.abs(query - key) <= 64, 0.0, -1e30))
    band = np.ascontiguousarray(np.stack(masks, 1)).astype(np.float32)
    rr, cc = np.arange(P)[:, None], np.arange(P)[None, :]
    return {
        "c_band": band,
        "c_seld": ((rr // 32 == cc // 32) & (rr % 32 == 8)).astype(np.float32),
    }


def experts(nc, X, dram, sems, out):
    with ExitStack() as ctx:
        def sb(name, shape, dt=F32):
            return ctx.enter_context(nc.sbuf_tensor(name, shape, dt))

        def bank(name, dt=F32):
            return ctx.enter_context(nc.psum_tensor(name, [P, 512], dt))

        def sem(name):
            sems.append(nc.alloc_semaphore(name))
            return sems[-1]

        OLD, NEW, TOPK, CAP, INTER = 128, 48, 8, 96, 96
        ROW = HID + NEW
        HALF = TOKENS // 2
        HT = TILES // 2
        ROUNDS = CAP // TOPK
        RING = 4
        BUFS = 4

        ident = sb("e_ident", [P, P])
        identb = sb("e_identb", [P, P], BF16)
        names = sb("e_names", [P, NEW])
        ramp = sb("e_ramp", [P, HALF])
        slotno = sb("e_slotno", [NEW, CAP])
        o2n = sb("e_o2n", [P, 1], I32)
        o2nf = sb("e_o2nf", [P, 1])
        perm = sb("e_perm", [P, NEW])
        gate = sb("e_gate", [P, HID])
        gT = sb("e_gT", [P, 2, NEW])
        eps = sb("e_eps", [P, 1])
        zrow = sb("e_zrow", [CAP, ROW])

        st = [sb(f"e_st{p}", [P, 6]) for p in range(BUFS)]
        mv = [sb(f"e_mv{p}", [P, 2]) for p in range(BUFS)]
        lv = [sb(f"e_lv{p}", [P, 1]) for p in range(BUFS)]
        rstd = [sb(f"e_rstd{p}", [P, 1]) for p in range(BUFS)]
        hw = [sb(f"e_hw{p}", [P, ROW]) for p in range(BUFS)]
        hT = [sb(f"e_hT{p}", [P, 2, P]) for p in range(2)]
        lg = [sb(f"e_lg{p}", [P, NEW]) for p in range(BUFS)]
        top = [sb(f"e_top{p}", [P, TOPK]) for p in range(BUFS)]
        rest = [sb(f"e_rest{p}", [P, NEW]) for p in range(BUFS)]
        chosen = [sb(f"e_chosen{p}", [P, NEW], BF16) for p in range(BUFS)]
        ntop = [sb(f"e_ntop{p}", [P, 1]) for p in range(BUFS)]
        ex = [sb(f"e_ex{p}", [P, NEW]) for p in range(BUFS)]
        em = [sb(f"e_em{p}", [P, NEW]) for p in range(BUFS)]
        es = [sb(f"e_es{p}", [P, 1]) for p in range(BUFS)]
        ei = [sb(f"e_ei{p}", [P, 1]) for p in range(BUFS)]
        queue = sb("e_queue", [P, HALF])
        first1 = sb("e_first1", [P, CAP])
        both2 = sb("e_both2", [NEW, 2 * CAP])
        first2 = sb("e_first2", [NEW, CAP])
        none = sb("e_none", [NEW, CAP])
        idf = sb("e_idf", [NEW, CAP])
        index = sb("e_index", [CAP, NEW], I32)
        gi = [sb(f"e_gi{k}", [CAP, 1], I32) for k in range(RING)]
        si = [sb(f"e_si{k}", [CAP, 1], I32) for k in range(2)]
        G = [sb(f"e_G{k}", [CAP, ROW]) for k in range(RING)]
        wgu = [sb(f"e_wgu{k}", [P, 2, 2 * INTER]) for k in range(RING)]
        wdn = [sb(f"e_wdn{k}", [INTER, HID]) for k in range(RING)]
        GT = [sb(f"e_GT{p}", [P, 2, CAP]) for p in range(2)]
        sg = [sb(f"e_sg{p}", [INTER, CAP]) for p in range(2)]
        act_ = [sb(f"e_act{p}", [INTER, CAP]) for p in range(2)]
        Y = [sb(f"e_Y{p}", [CAP, HID]) for p in range(2)]

        bT = [bank(f"e_bT{p}") for p in range(2)]
        bL = [bank(f"e_bL{p}") for p in range(2)]
        bC = [bank(f"e_bC{p}") for p in range(2)]
        bD = [bank(f"e_bD{p}") for p in range(2)]

        rows = nc.dram_tensor("e_rows", [TOKENS + CAP, ROW], F32, kind="Internal").ap()
        acc = nc.dram_tensor("e_acc", [TOKENS + CAP, HID], F32, kind="Internal").ap()

        loaded = sem("e_loaded")
        consts = sem("e_consts")
        held = sem("e_held")
        gT_mm = sem("e_gT_mm")
        gT_s = sem("e_gT")
        stats = sem("e_stats")
        rstd_s = sem("e_rstd")
        h_s = sem("e_h")
        hT_mm = sem("e_hT_mm")
        hT_s = sem("e_hT")
        l_mm = sem("e_l_mm")
        lg_s = sem("e_lg")
        top_s = sem("e_top")
        rest_s = sem("e_rest")
        chosen_s = sem("e_chosen")
        ntop_s = sem("e_ntop")
        ex_s = sem("e_ex")
        em_s = sem("e_em")
        ei_s = sem("e_ei")
        w_s = sem("e_w")
        c_mm = sem("e_c_mm")
        queue_s = sem("e_queue")
        rows_out = [sem(f"e_rows_out{p}") for p in range(BUFS)]
        acc_out = sem("e_acc_out")
        pad_out = sem("e_pad_out")
        pick = sem("e_pick")
        pick2 = sem("e_pick2")
        idf_s = sem("e_idf")
        id_mm = sem("e_id_mm")
        id_s = sem("e_id")
        gi_s = sem("e_gi")
        si_s = sem("e_si")
        fetched = [sem(f"e_fetched{k}") for k in range(RING)]
        w_ld = [sem(f"e_w_ld{k}") for k in range(RING)]
        gt_mm = sem("e_gt_mm")
        gt_s = sem("e_gt")
        gu_mm = sem("e_gu_mm")
        sg_s = sem("e_sg")
        act_s = sem("e_act")
        dn_mm = sem("e_dn_mm")
        y_s = sem("e_y")
        added = sem("e_added")
        final = sem("e_final")

        block = ctx.enter_context(nc.Block())

        def tile_of(i):
            return X[:, i, :] if isinstance(i, int) else X[:, bass.ds(i, 1), :].rearrange("p n d -> p (n d)")

        @block.sync
        def _(sp):
            for dst, src in ((ident, "c_ident"), (names, "c_names"), (ramp, "c_ramp"), (slotno, "c_slotno"),
                             (gate, "w_gate"), (o2n, "old_to_new")):
                sp.dma_start(dst[:, :], dram[src]).then_inc(loaded, 16)
            for part in range(2):
                n = TILES // 2
                sp.dma_start(acc[part * n * P:(part + 1) * n * P, :].rearrange("(n p) d -> p n d", p=P),
                             X[:, part * n:(part + 1) * n, :]).then_inc(acc_out, 16)
            sp.wait_ge(consts, 3)
            sp.dma_start(rows[TOKENS:TOKENS + CAP, :], zrow[:, :]).then_inc(pad_out, 16)
            sp.dma_start(acc[TOKENS:TOKENS + CAP, :], zrow[:, 0:HID]).then_inc(pad_out, 16)

            def load_weights(e, k):
                src_gu = dram["w_gu"][e] if isinstance(e, int) else \
                    dram["w_gu"][bass.ds(e, 1)].rearrange("n p c m -> (n p) c m")
                src_dn = dram["w_dn"][e] if isinstance(e, int) else \
                    dram["w_dn"][bass.ds(e, 1)].rearrange("n p m -> (n p) m")
                after(sp, dn_mm, e - RING + 1)
                sp.sem_inc(held, 1)
                sp.dma_start(wgu[k][:, :, :], src_gu).then_inc(w_ld[k], 16)
                sp.dma_start(wdn[k][:, :], src_dn).then_inc(w_ld[k], 16)

            for e in range(RING):
                load_weights(e, e)
            rows_t = rows[0:TOKENS, :].rearrange("(n p) d -> n p d", p=P)
            with sp.Fori(0, TILES // BUFS) as t:
                for p in range(BUFS):
                    sp.wait_ge(w_s, BUFS * t + p + 1)
                    sp.sem_inc(held, 1)
                    sp.dma_start(rows_t[bass.ds(BUFS * t + p, 1)].rearrange("n p d -> (n p) d"), hw[p][:, :]
                                 ).then_inc(rows_out[p], 16)
            with sp.Fori(1, NEW // RING) as t:
                for k in range(RING):
                    load_weights(RING * t + k, k)
            sp.wait_ge(added, 16 * NEW)
            sp.dma_start(out, acc[0:TOKENS, :]).then_inc(final, 16)
            sp.wait_ge(final, 16)
            sp.wait_ge(pad_out, 32)
            sp.wait_ge(acc_out, 32)
            for p in range(BUFS):
                sp.wait_ge(rows_out[p], 16 * (TILES // BUFS))

        def run_tiles(eng, step):
            quads = HT // BUFS
            for p in range(BUFS):
                step(0, p, 0, TILES)
            for half in range(2):
                with eng.Fori(1 - half, quads - half) as t:
                    for p in range(BUFS):
                        step(t, p, half, TILES)
            for p in range(BUFS):
                step(quads - 1, p, 1, BUFS - 1 - p)

        @block.tensor
        def _(pe):
            pe.wait_ge(loaded, 16 * 6)
            pe.wait_ge(consts, 5)
            for c in range(2):
                m = nc.tensor.matmul(bT[0][:, c * NEW:(c + 1) * NEW], gate[:, c * P:(c + 1) * P], perm[:, :],
                                     start=True, stop=True)
            m.then_inc(gT_mm, 1)
            pe.wait_ge(gT_s, 1)

            def turn(i, b):
                pe.wait_ge(h_s, i + 1)
                after(pe, hT_s, i - 1)
                for c in range(2):
                    m = nc.tensor.transpose(bT[b % 2][:, c * P:(c + 1) * P], hw[b][:, c * P:(c + 1) * P], ident[:, :])
                m.then_inc(hT_mm, 1)

            def route(i, b):
                pe.wait_ge(hT_s, i + 1)
                after(pe, lg_s, i - 1)
                for c in range(2):
                    m = nc.tensor.matmul(bL[b % 2][:, 0:NEW], hT[b % 2][:, c, :], gT[:, c, :],
                                         start=(c == 0), stop=(c == 1))
                m.then_inc(l_mm, 1)

            def turn_chosen(i, b, half):
                pe.wait_ge(chosen_s, i + 1)
                after(pe, queue_s, i - 1)
                nc.tensor.matmul(bC[b % 2][64 * half:64 * half + NEW, 0:P], chosen[b][:, :], identb[:, :],
                                 start=True, stop=True).then_inc(c_mm, 1)

            def step(t, p, half, left):
                i = BUFS * t + p + half * HT
                turn_chosen(i, p, half)
                if left > 1:
                    turn(i + 2, (p + 2) % BUFS)
                    route(i + 2, (p + 2) % BUFS)

            for i in range(2):
                turn(i, i)
                route(i, i)
            run_tiles(pe, step)
            pe.wait_ge(idf_s, 3)
            nc.tensor.transpose(bT[0][0:CAP, 0:NEW], idf[:, :], ident[0:NEW, 0:NEW]).then_inc(id_mm, 1)
            pe.wait_ge(id_s, 1)

            def expert(e, k, t):
                p = k % 2
                pe.wait_ge(fetched[k], 16 * (t + 1))
                after(pe, gt_s, e - 1)
                for c in range(2):
                    m = nc.tensor.transpose(bT[p][:, c * CAP:(c + 1) * CAP], G[k][:, c * P:(c + 1) * P],
                                            ident[0:CAP, 0:CAP])
                m.then_inc(gt_mm, 1)

            def expert_up(e, k, t):
                p = k % 2
                pe.wait_ge(w_ld[k], 32 * (t + 1))
                pe.wait_ge(gt_s, e + 1)
                after(pe, act_s, e - 1)
                for s in range(2):
                    for c in range(2):
                        m = nc.tensor.matmul(bL[p][0:INTER, s * CAP:(s + 1) * CAP],
                                             wgu[k][:, c, s * INTER:(s + 1) * INTER], GT[p][:, c, :],
                                             start=(c == 0), stop=(c == 1))
                m.then_inc(gu_mm, 1)

            def expert_down(e, k):
                p = k % 2
                pe.wait_ge(act_s, e + 1)
                after(pe, y_s, e - 1)
                nc.tensor.matmul(bD[p][0:CAP, 0:HID], act_[p][:, :], wdn[k][:, :], start=True, stop=True
                                 ).then_inc(dn_mm, 1)
            def experts_of(t):
                for k in range(RING):
                    e = RING * t + k
                    expert(e, k, t)
                    expert_up(e, k, t)
                    expert_down(e, k)
            experts_of(0)
            with pe.Fori(1, NEW // RING) as t:
                experts_of(t)

        @block.scalar
        def _(act):
            nc.scalar.preload_act_table_set("natural_log_exp_and_others")
            act.wait_ge(loaded, 16 * 6)
            act.wait_ge(consts, 5)
            act.wait_ge(gT_mm, 1)
            nc.scalar.copy(gT[:, :, :].rearrange("p c n -> p (c n)"), bT[0][:, 0:2 * NEW]).then_inc(gT_s, 1)

            def norm(i, b):
                act.wait_ge(stats, 2 * (i + 1))
                nc.scalar.activation(lv[b][:, :], mv[b][:, 1:2], ACT.Ln, bias=eps[:, :]).then_inc(rstd_s, 1)
                act.wait_ge(rstd_s, 2 * i + 1)
                nc.scalar.activation(rstd[b][:, :], lv[b][:, :], ACT.Exp, scale=-0.5).then_inc(rstd_s, 1)

            def take_turned(i, b):
                act.wait_ge(hT_mm, i + 1)
                after(act, l_mm, i - 1)
                nc.scalar.copy(hT[b % 2][:, :, :].rearrange("p c t -> p (c t)"), bT[b % 2][:, 0:2 * P]
                               ).then_inc(hT_s, 1)

            def exps(i, b):
                act.wait_ge(ntop_s, i + 1)
                after(act, em_s, i - BUFS + 1)
                nc.scalar.activation(ex[b][:, :], lg[b][:, :], ACT.Exp, bias=ntop[b][:, :]).then_inc(ex_s, 1)

            def step(t, p, half, left):
                i = BUFS * t + p + half * HT
                if left > 2:
                    norm(i + 3, (p + 3) % BUFS)
                if left > 1:
                    take_turned(i + 2, (p + 2) % BUFS)
                if left > 0:
                    exps(i + 1, (p + 1) % BUFS)

            for i in range(2):
                norm(i, i)
                take_turned(i, i)
            norm(2, 2)
            exps(0, 0)
            run_tiles(act, step)

            def gather_turned(e, k):
                p = k % 2
                act.wait_ge(gt_mm, e + 1)
                after(act, gu_mm, e - 1)
                nc.scalar.copy(GT[p][:, :, :].rearrange("p c t -> p (c t)"), bT[p][:, 0:2 * CAP]).then_inc(gt_s, 1)

            def silu(e, k):
                p = k % 2
                act.wait_ge(gu_mm, e + 1)
                after(act, act_s, e - 1)
                nc.scalar.activation(sg[p][:, :], bL[p][0:INTER, 0:CAP], ACT.Silu).then_inc(sg_s, 1)
            def experts_of(t):
                for k in range(RING):
                    gather_turned(RING * t + k, k)
                    silu(RING * t + k, k)
            experts_of(0)
            with act.Fori(1, NEW // RING) as t:
                experts_of(t)

        @block.vector
        def _(dve):
            nc.vector.memset(eps[:, :], LN_EPS).then_inc(consts, 1)
            nc.vector.memset(queue[:, :], 0.0).then_inc(consts, 1)
            nc.vector.memset(zrow[:, :], 0.0).then_inc(consts, 1)
            dve.wait_ge(loaded, 16 * 6)
            nc.vector.tensor_copy(identb[:, :], ident[:, :]).then_inc(consts, 1)
            nc.vector.tensor_copy(o2nf[:, :], o2n[:, :]).then_inc(pick, 1)
            dve.wait_ge(pick, 1)
            nc.vector.tensor_scalar(perm[:, :], names[:, :], o2nf[:, 0:1], None, ALU.is_equal).then_inc(consts, 1)
            dve.wait_ge(consts, 5)

            def norm(i, b):
                after(dve, rstd_s, 2 * (i - BUFS + 1))
                nc.vector.bn_stats(st[b][:, :], tile_of(i)).then_inc(stats, 1)
                dve.wait_ge(stats, 2 * i + 1)
                dve.sem_inc(held, 1)
                nc.vector.bn_aggr(mv[b][:, :], st[b][:, :]).then_inc(stats, 1)

            def normalise(i, b, before):
                dve.wait_ge(rstd_s, 2 * (i + 1))
                after(dve, hT_mm, i - BUFS + 1)
                after(dve, rows_out[b], 16 * before)
                nc.vector.tensor_scalar(hw[b][:, 0:HID], tile_of(i), mv[b][:, 0:1], rstd[b][:, 0:1],
                                        ALU.subtract, ALU.mult).then_inc(h_s, 1)

            def logits(i, b):
                dve.wait_ge(l_mm, i + 1)
                after(dve, ex_s, i - BUFS + 1)
                nc.vector.tensor_copy(lg[b][:, :], bL[b % 2][:, 0:NEW]).then_inc(lg_s, 1)

            def choose(i, b):
                dve.wait_ge(lg_s, i + 1)
                dve.sem_inc(held, 1)
                nc.vector.max(top[b][:, :], lg[b][:, :]).then_inc(top_s, 1)
                dve.wait_ge(top_s, i + 1)
                nc.vector.tensor_scalar(ntop[b][:, :], top[b][:, 0:1], -1.0, None, ALU.mult).then_inc(ntop_s, 1)
                nc.vector.match_replace(out=rest[b][:, :], in_to_replace=top[b][:, :], in_values=lg[b][:, :],
                                        imm_value=-3e38).then_inc(rest_s, 1)

            def mark(i, b):
                dve.wait_ge(rest_s, i + 1)
                after(dve, c_mm, i - BUFS + 1)
                nc.vector.tensor_tensor(chosen[b][:, :], rest[b][:, :], lg[b][:, :], ALU.not_equal
                                        ).then_inc(chosen_s, 1)

            def mask(i, b):
                dve.wait_ge(ex_s, i + 1)
                dve.wait_ge(chosen_s, i + 1)
                nc.vector.scalar_tensor_tensor(out=em[b][:, :], in0=ex[b][:, :], scalar=1.0, in1=chosen[b][:, :],
                                               op0=ALU.mult, op1=ALU.mult, accum_out=es[b][:, :]).then_inc(em_s, 1)

            def invert(i, b):
                dve.wait_ge(em_s, i + 1)
                nc.vector.reciprocal(ei[b][:, :], es[b][:, :]).then_inc(ei_s, 1)

            def weigh(i, b):
                dve.wait_ge(ei_s, i + 1)
                nc.vector.tensor_scalar(hw[b][:, HID:ROW], em[b][:, :], ei[b][:, 0:1], None, ALU.mult
                                        ).then_inc(w_s, 1)

            def enqueue(i, b, half, col):
                dve.wait_ge(c_mm, i + 1)
                r = 64 * half
                where = bass.ds(col, P)
                nc.vector.tensor_tensor(queue[r:r + NEW, where], bC[b % 2][r:r + NEW, 0:P], ramp[r:r + NEW, where],
                                        ALU.mult).then_inc(queue_s, 1)

            def step(t, p, half, left):
                i = BUFS * t + p + half * HT
                b1, b2, b3 = (p + 1) % BUFS, (p + 2) % BUFS, (p + 3) % BUFS
                if left > 1:
                    normalise(i + 2, b2, t + (p + 2) // BUFS + half * HT // BUFS)
                if left > 0:
                    logits(i + 1, b1)
                if left > 2:
                    norm(i + 3, b3)
                mask(i, p)
                if left > 0:
                    choose(i + 1, b1)
                invert(i, p)
                enqueue(i, p, half, (BUFS * t + p) * P)
                weigh(i, p)
                if left > 0:
                    mark(i + 1, b1)

            for i in range(2):
                norm(i, i)
                normalise(i, i, 0)
            norm(2, 2)
            logits(0, 0)
            choose(0, 0)
            mark(0, 0)
            run_tiles(dve, step)
            for r in range(ROUNDS):
                dve.wait_ge(pick, 1 + 2 * r)
                if r == 0:
                    dve.wait_ge(queue_s, TILES)
                nc.vector.max(first1[0:112, r * TOPK:(r + 1) * TOPK], queue[0:112, :]).then_inc(pick, 1)
                dve.wait_ge(pick, 2 + 2 * r)
                nc.vector.match_replace(out=queue[0:112, :], in_to_replace=first1[0:112, r * TOPK:(r + 1) * TOPK],
                                        in_values=queue[0:112, :], imm_value=-1.0).then_inc(pick, 1)
            dve.wait_ge(pick, 1 + 2 * ROUNDS)
            nc.vector.tensor_scalar(none[:, :], first1[0:NEW, :], 0.0, float(HALF), ALU.is_gt, ALU.mult
                                    ).then_inc(pick2, 1)
            nc.vector.tensor_copy(both2[:, CAP:2 * CAP], first1[64:64 + NEW, :]).then_inc(pick2, 1)
            dve.wait_ge(pick2, 2)
            nc.vector.tensor_tensor(both2[:, 0:CAP], first1[0:NEW, :], none[:, :], ALU.add).then_inc(pick2, 1)
            for r in range(ROUNDS):
                dve.wait_ge(pick2, 3 + 2 * r)
                nc.vector.max(first2[:, r * TOPK:(r + 1) * TOPK], both2[:, :]).then_inc(pick2, 1)
                dve.wait_ge(pick2, 4 + 2 * r)
                nc.vector.match_replace(out=both2[:, :], in_to_replace=first2[:, r * TOPK:(r + 1) * TOPK],
                                        in_values=both2[:, :], imm_value=-1.0).then_inc(pick2, 1)
            dve.wait_ge(pick2, 3 + 2 * ROUNDS)
            nc.vector.tensor_scalar(none[:, :], first2[:, :], 0.0, None, ALU.is_le).then_inc(idf_s, 1)
            dve.wait_ge(idf_s, 1)
            nc.vector.tensor_tensor(none[:, :], none[:, :], slotno[:, :], ALU.mult).then_inc(idf_s, 1)
            dve.wait_ge(idf_s, 2)
            nc.vector.scalar_tensor_tensor(out=idf[:, :], in0=none[:, :], scalar=float(TOKENS), in1=first2[:, :],
                                           op0=ALU.add, op1=ALU.subtract).then_inc(idf_s, 1)
            dve.wait_ge(id_mm, 1)
            nc.vector.tensor_copy(index[:, :], bT[0][0:CAP, 0:NEW]).then_inc(id_s, 1)

            def gated(e, k):
                p = k % 2
                dve.wait_ge(sg_s, e + 1)
                after(dve, dn_mm, e - 1)
                nc.vector.tensor_tensor(act_[p][:, :], sg[p][:, :], bL[p][0:INTER, CAP:2 * CAP], ALU.mult
                                        ).then_inc(act_s, 1)

            def weighted(e, k):
                p = k % 2
                dve.wait_ge(dn_mm, e + 1)
                after(dve, added, 16 * (e - 1))
                nc.vector.tensor_scalar(Y[p][:, :], bD[p][0:CAP, 0:HID], G[k][:, bass.ds(e + HID, 1)], None,
                                        ALU.mult).then_inc(y_s, 1)
            def experts_of(t):
                for k in range(RING):
                    gated(RING * t + k, k)
                    weighted(RING * t + k, k)
            experts_of(0)
            with dve.Fori(1, NEW // RING) as t:
                experts_of(t)

        @block.gpsimd
        def _(pool):
            pool.wait_ge(id_s, 1)
            for p in range(BUFS):
                pool.wait_ge(rows_out[p], 16 * (TILES // BUFS))
            pool.wait_ge(acc_out, 32)
            pool.wait_ge(pad_out, 32)

            def fetch(e, k):
                after(pool, y_s, e - RING + 1)
                pool.sem_inc(held, 1)
                nc.gpsimd.tensor_copy(gi[k][:, :], index[:, bass.ds(e, 1)]).then_inc(gi_s, 1)
                pool.wait_ge(gi_s, e + 1)
                pool.sem_inc(held, 1)
                nc.gpsimd.indirect_dma_start(G[k][:, :], None, rows, bass.IndirectOffsetOnAxis(ap=gi[k][:, :], axis=0)
                                             ).then_inc(fetched[k], 16)

            def scatter(e, p):
                after(pool, added, 16 * e)
                pool.sem_inc(held, 1)
                nc.gpsimd.tensor_copy(si[p][:, :], index[:, bass.ds(e, 1)]).then_inc(si_s, 1)
                pool.wait_ge(si_s, e + 1)
                pool.wait_ge(y_s, e + 1)
                pool.sem_inc(held, 1)
                nc.gpsimd.indirect_dma_start(acc, bass.IndirectOffsetOnAxis(ap=si[p][:, :], axis=0), Y[p][:, :], None,
                                             compute_op=ALU.add).then_inc(added, 16)
            for e in range(RING - 1):
                fetch(e, e)
            for e in range(RING):
                fetch(e + RING - 1, (e + RING - 1) % RING)
                scatter(e, e % 2)
            with pool.Fori(1, NEW // RING - 1) as t:
                for k in range(RING):
                    fetch(RING * t + k + RING - 1, (k + RING - 1) % RING)
                    scatter(RING * t + k, k % 2)
            for k in range(RING):
                e = NEW - RING + k
                if e + RING - 1 < NEW:
                    fetch(e + RING - 1, (k + RING - 1) % RING)
                scatter(e, k % 2)


def expert_constants():
    return {
        "c_names": np.ascontiguousarray(np.broadcast_to(np.arange(48), (P, 48))).astype(np.float32),
        "c_ramp": np.ascontiguousarray(np.broadcast_to(TOKENS // 2 - np.arange(TOKENS // 2),
                                                       (P, TOKENS // 2))).astype(np.float32),
        "c_slotno": np.ascontiguousarray(np.broadcast_to(np.arange(96), (48, 96))).astype(np.float32),
    }


def build(nc, dram, out):
    with nc.sbuf_tensor("x_residual", [P, TILES, HID], F32) as X:
        for stage, args in ((delta_rule, ()), (banded_attention, ()), (experts, (out,))):
            sems = []
            stage(nc, X, dram, sems, *args)
            nc.clear_and_free_semaphores(sems)
            nc.all_engine_barrier()


def laid_out(v):
    f = np.float32

    def chunks(q, k, v_):
        o = np.zeros((NCH, P) + q.shape[1:], f)
        h = 3 * DK
        o[0, :h], o[1, :h], o[2, :h], o[3, :h] = q[:h], q[h:], k[:h], k[h:]
        o[QKC:] = v_.reshape((3, P) + v_.shape[1:])
        return o

    def rows(a, n=P):
        return np.ascontiguousarray(np.broadcast_to(a, (n, a.shape[-1])))

    def diagonal(w):
        o = np.zeros((P, P), f)
        o[:T, :T] = w
        o[T:, T:] = w
        return o

    def column(b):
        return np.ascontiguousarray(np.concatenate([b, b])[:, None])

    def by_channel(a):
        return np.ascontiguousarray(a.reshape((16, 8) + a.shape[1:]).swapaxes(0, 1).reshape(a.shape))

    w_in, b_in = v["L0_xattn_w_in"], v["L0_xattn_b_in"]
    w_out = np.zeros((4, 32, 2, T), f)
    w_out[:, :8] = v["L0_xattn_w_out"].T.reshape(2, 4, 8, T).transpose(1, 2, 0, 3)
    gu, dn = v["L0_ffn_gate_up_proj"], v["L0_ffn_down_proj"]
    return {
        "x": np.ascontiguousarray(v["x"].reshape(TOKENS, HID)),
        "w_qkv": np.ascontiguousarray(chunks(v["L0_attn_Wq"], v["L0_attn_Wk"], v["L0_attn_Wv"])
                                      .reshape(NCH * P, HID).T),
        "w_conv": chunks(v["L0_attn_conv_wq"], v["L0_attn_conv_wk"], v["L0_attn_conv_wv"]),
        "w_gab": np.ascontiguousarray(np.concatenate([v["L0_attn_Wg"], v["L0_attn_Wb"], v["L0_attn_Wa"]]).T),
        "w_o": np.ascontiguousarray(v["L0_attn_Wo"].T),
        "norm_w": rows(np.tile(v["L0_attn_norm_w"], HEADS)),
        "A_log": rows(v["L0_attn_A_log"]),
        "dt_bias": rows(v["L0_attn_dt_bias"]),
        "ctx": np.ascontiguousarray(v["ctx_2048"].reshape(TILES, P, HID)),
        "w_in": np.stack([by_channel(diagonal(w_in[T * n:T * n + T])).T for n in range(2)]
                         + [diagonal(w_in[2 * T:].T)]),
        "w_out": np.ascontiguousarray(w_out.reshape(P, 2, T)),
        "w_ct": diagonal(v["L0_xattn_w_ct"]),
        "b_q": by_channel(column(b_in[:T])),
        "b_k": by_channel(column(b_in[T:2 * T])),
        "b_v": rows(np.tile(b_in[2 * T:], 4)),
        "b_out": column(v["L0_xattn_b_out"]),
        "b_ct": column(v["L0_xattn_b_ct"]),
        "w_gate": np.ascontiguousarray(v["L0_ffn_gate_weight"]),
        "old_to_new": np.ascontiguousarray(v["L0_ffn_old_to_new"][:, None]),
        "w_gu": np.ascontiguousarray(gu.transpose(0, 2, 1).reshape(48, 2, P, 192).transpose(0, 2, 1, 3)),
        "w_dn": np.ascontiguousarray(dn.transpose(0, 2, 1)),
    }


def kernel(**inputs):
    import concourse.bacc as bacc
    from concourse.bass_utils import run_bass_kernel_spmd

    arrays = laid_out({k: np.asarray(a) for k, a in inputs.items()})
    arrays.update(constants())
    arrays.update(attention_constants())
    arrays.update(expert_constants())
    nc = bacc.Bacc("TRN2", target_bir_lowering=False, num_devices=1)
    dram = {k: nc.dram_tensor("in_" + k, a.shape, mybir.dt.from_np(a.dtype), kind="ExternalInput").ap()
            for k, a in arrays.items()}
    out = nc.dram_tensor("out_dram", (TOKENS, HID), F32, kind="ExternalOutput").ap()
    build(nc, dram, out)
    r = run_bass_kernel_spmd(nc, [{"in_" + k: a for k, a in arrays.items()}], core_ids=[0])
    return np.asarray(r.results[0]["out_dram"]).reshape(64, 64, 256)
```
